# Optimizing a Trainium2 kernel written in Bass

```python
import numpy as np
import jax
import jax.numpy as jnp

def _softmax(x, axis=-1):
    return jax.nn.softmax(x, axis=axis)

def _gelu(x):
    return jax.nn.gelu(x, approximate=True)

def _silu(x):
    return jax.nn.silu(x)

def _sigmoid(x):
    return jax.nn.sigmoid(x)

def _layernorm(x, axis=-1, eps=1e-05):
    m = jnp.mean(x, axis=axis, keepdims=True)
    v = jnp.var(x, axis=axis, keepdims=True)
    return (x - m) / jnp.sqrt(v + eps)

def _scatter_add(tgt, idx, src, axis=0):
    return tgt.at[idx].add(src)

def _segment_sum(src, seg, n):
    return jax.ops.segment_sum(src, seg, n)
kernel_name = 'mk_seq_postln_d2_jaxref_r8_896d1f'

def setup_inputs(seed: int=0):
    np.random.seed(seed)
    _w = jnp.asarray

    def _L0_attn_setup():
        import jax, jax.numpy as jnp
        import numpy as np
        B, N, C = (2, 256, 128)
        H = 16
        HD = C // H
        R = 16
        LORA_SCALE = 32.0 / R
        ATTN_SCALE = HD ** (-0.5)
        key = jax.random.key(seed)
        ks = jax.random.split(key, 10)
        s = lambda fan_in: 1.0 / np.sqrt(fan_in)
        return {'x': jax.random.normal(ks[0], (B, N, C), dtype=jnp.float32), 'w_qkv': jax.random.normal(ks[1], (C, 3 * C), dtype=jnp.float32) * s(C), 'b_qkv': jax.random.normal(ks[2], (3 * C,), dtype=jnp.float32) * 0.02, 'a_q': jax.random.normal(ks[3], (HD, R), dtype=jnp.float32) * s(HD), 'b_q': jax.random.normal(ks[4], (R, HD), dtype=jnp.float32) * 0.02, 'a_v': jax.random.normal(ks[5], (HD, R), dtype=jnp.float32) * s(HD), 'b_v': jax.random.normal(ks[6], (R, HD), dtype=jnp.float32) * 0.02, 'w_proj': jax.random.normal(ks[7], (C, C), dtype=jnp.float32) * s(C), 'b_proj': jax.random.normal(ks[8], (C,), dtype=jnp.float32) * 0.02}
    _L0_attn_in = _L0_attn_setup()

    def _L0_ffn_setup():
        import jax, jax.numpy as jnp
        import numpy as np
        CAPACITY_FACTOR = 1.25
        key = jax.random.key(seed)
        ks = jax.random.split(key, 6)
        B, S, H, E = (4, 512, 128, 8)
        scale = 1.0 / np.sqrt(H)
        return {'tokens': jax.random.normal(ks[0], (B, S, H), dtype=jnp.float32), 'gate_w': jax.random.normal(ks[1], (E, H), dtype=jnp.float32) * scale, 'w1': jax.random.normal(ks[2], (E, H, H), dtype=jnp.float32) * scale, 'b1': jax.random.normal(ks[3], (E, H), dtype=jnp.float32) * 0.01, 'w2': jax.random.normal(ks[4], (E, H, H), dtype=jnp.float32) * scale, 'b2': jax.random.normal(ks[5], (E, H), dtype=jnp.float32) * 0.01}
    _L0_ffn_in = _L0_ffn_setup()

    def _L1_attn_setup():
        import jax, jax.numpy as jnp
        import numpy as np
        N_HEAD = 16
        ROPE_BASE = 10000.0

        def _rotate_half(t):
            d = t.shape[-1] // 2
            return jnp.concatenate([-t[..., d:], t[..., :d]], axis=-1)

        def _rope_cos_sin(T, D, dtype):
            half = D // 2
            theta = 1.0 / ROPE_BASE ** (jnp.arange(half, dtype=dtype) / half)
            pos = jnp.arange(T, dtype=dtype)
            freqs = pos[:, None] * theta[None, :]
            cos = jnp.repeat(jnp.cos(freqs), 2, axis=-1)
            sin = jnp.repeat(jnp.sin(freqs), 2, axis=-1)
            return (cos, sin)
        key = jax.random.key(seed)
        k1, k2, k3 = jax.random.split(key, 3)
        B, T, C = (2, 256, 128)
        x = jax.random.normal(k1, (B, T, C), dtype=jnp.float32)
        w_qkv = jax.random.normal(k2, (C, 3 * C), dtype=jnp.float32) * C ** (-0.5)
        w_proj = jax.random.normal(k3, (C, C), dtype=jnp.float32) * C ** (-0.5)
        return {'x': x, 'w_qkv': w_qkv, 'w_proj': w_proj}
    _L1_attn_in = _L1_attn_setup()

    def _L1_ffn_setup():
        import jax, jax.numpy as jnp
        import numpy as np
        D_MODEL = 128
        NUM_TILES = 64
        TPC = 8
        NUM_CLUSTERS = NUM_TILES // TPC
        GRID = 16
        COMP_H = 32
        NUM_KNOTS = 8
        EPS_LN = 1e-05

        def _calibrate(scores, knots, temperature):
            K = knots.shape[0]
            normalized = jax.nn.sigmoid(scores / (temperature[0] + 1e-06))
            idx_float = normalized * (K - 1)
            idx_low = jnp.clip(idx_float.astype(jnp.int32), 0, K - 2)
            idx_high = idx_low + 1
            t = idx_float - idx_low.astype(scores.dtype)
            val_low = knots[idx_low]
            val_high = knots[idx_high]
            return val_low + t * (val_high - val_low)

        def _forward(x, signatures_raw, knot_values, temperature, compress_w1, compress_b1, compress_w2, compress_b2, spline_w1, spline_b1, spline_w2, spline_b2, directions, norm_gamma, norm_beta, output_scale):
            B, T, D = x.shape
            xf = x.reshape(-1, D)
            q = jnp.where(signatures_raw > 0.3, 1.0, jnp.where(signatures_raw < -0.3, -1.0, 0.0)).astype(signatures_raw.dtype)
            sigs = signatures_raw + jax.lax.stop_gradient(q - signatures_raw)
            cluster_sigs = jnp.sign(sigs.reshape(NUM_CLUSTERS, TPC, D).mean(axis=1))
            cluster_scores = xf @ cluster_sigs.T
            cluster_gates = _calibrate(cluster_scores, knot_values, temperature)
            cluster_idx = jnp.argmax(cluster_gates, axis=-1)
            tile_scores = xf @ sigs.T
            tile_gates = _calibrate(tile_scores, knot_values, temperature)
            gates_by_cluster = tile_gates.reshape(-1, NUM_CLUSTERS, TPC)
            sel_gates = jnp.take_along_axis(gates_by_cluster, cluster_idx[:, None, None], axis=1)[:, 0, :]
            local_idx = jnp.argmax(sel_gates, axis=-1)
            tile_idx = cluster_idx * TPC + local_idx
            h = jax.nn.gelu(xf @ compress_w1 + compress_b1, approximate=False)
            comp = jnp.tanh(h @ compress_w2 + compress_b2)
            w1 = spline_w1[tile_idx]
            b1 = spline_b1[tile_idx]
            hh = jax.nn.relu(jnp.einsum('ni,nig->ng', comp, w1) + b1)
            w2 = spline_w2[tile_idx]
            b2 = spline_b2[tile_idx]
            mag = jnp.einsum('ng,ngo->no', hh, w2) + b2
            ffn_out = mag * directions[tile_idx] * output_scale[0]
            y = xf + ffn_out
            mu = y.mean(axis=-1, keepdims=True)
            var = ((y - mu) ** 2).mean(axis=-1, keepdims=True)
            y = (y - mu) / jnp.sqrt(var + EPS_LN) * norm_gamma + norm_beta
            return y.reshape(B, T, D)
        key = jax.random.key(seed)
        ks = jax.random.split(key, 12)
        B, T = (4, 512)
        x = jax.random.normal(ks[0], (B, T, D_MODEL), dtype=jnp.float32)
        signatures_raw = jax.random.normal(ks[1], (NUM_TILES, D_MODEL), dtype=jnp.float32) * 0.5
        knot_values = jax.nn.sigmoid(jnp.linspace(-3.0, 3.0, NUM_KNOTS).astype(jnp.float32))
        temperature = jnp.ones((1,), dtype=jnp.float32)
        compress_w1 = jax.random.normal(ks[2], (D_MODEL, COMP_H), dtype=jnp.float32) * (1.0 / np.sqrt(D_MODEL))
        compress_b1 = jnp.zeros((COMP_H,), dtype=jnp.float32)
        compress_w2 = jax.random.normal(ks[3], (COMP_H, 2), dtype=jnp.float32) * (1.0 / np.sqrt(COMP_H))
        compress_b2 = jnp.zeros((2,), dtype=jnp.float32)
        spline_w1 = jax.random.normal(ks[4], (NUM_TILES, 2, GRID), dtype=jnp.float32) * (1.0 / np.sqrt(2.0))
        spline_b1 = jnp.zeros((NUM_TILES, GRID), dtype=jnp.float32)
        spline_w2 = jax.random.normal(ks[5], (NUM_TILES, GRID, 1), dtype=jnp.float32) * (1.0 / np.sqrt(GRID))
        spline_b2 = jnp.zeros((NUM_TILES, 1), dtype=jnp.float32)
        directions = jax.random.normal(ks[6], (NUM_TILES, D_MODEL), dtype=jnp.float32) * 0.02
        norm_gamma = jnp.ones((D_MODEL,), dtype=jnp.float32)
        norm_beta = jnp.zeros((D_MODEL,), dtype=jnp.float32)
        output_scale = jnp.ones((1,), dtype=jnp.float32) * 0.1
        return dict(x=x, signatures_raw=signatures_raw, knot_values=knot_values, temperature=temperature, compress_w1=compress_w1, compress_b1=compress_b1, compress_w2=compress_w2, compress_b2=compress_b2, spline_w1=spline_w1, spline_b1=spline_b1, spline_w2=spline_w2, spline_b2=spline_b2, directions=directions, norm_gamma=norm_gamma, norm_beta=norm_beta, output_scale=output_scale)
    _L1_ffn_in = _L1_ffn_setup()
    _d = {'L0_attn_x': _L0_attn_in['x'], 'L0_attn_w_qkv': _L0_attn_in['w_qkv'], 'L0_attn_b_qkv': _L0_attn_in['b_qkv'], 'L0_attn_a_q': _L0_attn_in['a_q'], 'L0_attn_b_q': _L0_attn_in['b_q'], 'L0_attn_a_v': _L0_attn_in['a_v'], 'L0_attn_b_v': _L0_attn_in['b_v'], 'L0_attn_w_proj': _L0_attn_in['w_proj'], 'L0_attn_b_proj': _L0_attn_in['b_proj'], 'L0_ffn_gate_w': _L0_ffn_in['gate_w'], 'L0_ffn_w1': _L0_ffn_in['w1'], 'L0_ffn_b1': _L0_ffn_in['b1'], 'L0_ffn_w2': _L0_ffn_in['w2'], 'L0_ffn_b2': _L0_ffn_in['b2'], 'L1_attn_w_qkv': _L1_attn_in['w_qkv'], 'L1_attn_w_proj': _L1_attn_in['w_proj'], 'L1_ffn_signatures_raw': _L1_ffn_in['signatures_raw'], 'L1_ffn_knot_values': _L1_ffn_in['knot_values'], 'L1_ffn_temperature': _L1_ffn_in['temperature'], 'L1_ffn_compress_w1': _L1_ffn_in['compress_w1'], 'L1_ffn_compress_b1': _L1_ffn_in['compress_b1'], 'L1_ffn_compress_w2': _L1_ffn_in['compress_w2'], 'L1_ffn_compress_b2': _L1_ffn_in['compress_b2'], 'L1_ffn_spline_w1': _L1_ffn_in['spline_w1'], 'L1_ffn_spline_b1': _L1_ffn_in['spline_b1'], 'L1_ffn_spline_w2': _L1_ffn_in['spline_w2'], 'L1_ffn_spline_b2': _L1_ffn_in['spline_b2'], 'L1_ffn_directions': _L1_ffn_in['directions'], 'L1_ffn_norm_gamma': _L1_ffn_in['norm_gamma'], 'L1_ffn_norm_beta': _L1_ffn_in['norm_beta'], 'L1_ffn_output_scale': _L1_ffn_in['output_scale']}
    _x0 = _d['L0_attn_x']
    _d['L0_attn_x'] = jax.random.normal(jax.random.fold_in(jax.random.key(seed), 1), (32, 256, 128), dtype=_x0.dtype)
    del _x0
    return _d

def reference(L0_attn_x, L0_attn_w_qkv, L0_attn_b_qkv, L0_attn_a_q, L0_attn_b_q, L0_attn_a_v, L0_attn_b_v, L0_attn_w_proj, L0_attn_b_proj, L0_ffn_gate_w, L0_ffn_w1, L0_ffn_b1, L0_ffn_w2, L0_ffn_b2, L1_attn_w_qkv, L1_attn_w_proj, L1_ffn_signatures_raw, L1_ffn_knot_values, L1_ffn_temperature, L1_ffn_compress_w1, L1_ffn_compress_b1, L1_ffn_compress_w2, L1_ffn_compress_b2, L1_ffn_spline_w1, L1_ffn_spline_b1, L1_ffn_spline_w2, L1_ffn_spline_b2, L1_ffn_directions, L1_ffn_norm_gamma, L1_ffn_norm_beta, L1_ffn_output_scale):

    def _L0_attn_ref(x, w_qkv, b_qkv, a_q, b_q, a_v, b_v, w_proj, b_proj):
        import jax, jax.numpy as jnp
        import numpy as np
        B, N, C = (2, 256, 128)
        H = 16
        HD = C // H
        R = 16
        LORA_SCALE = 32.0 / R
        ATTN_SCALE = HD ** (-0.5)
        Bb, Nn, Cc = x.shape
        qkv = (x @ w_qkv + b_qkv).reshape(Bb, Nn, 3, H, HD).transpose(2, 0, 3, 1, 4)
        q, k, v = (qkv[0], qkv[1], qkv[2])
        q = q + jnp.einsum('bhnr,rd->bhnd', jnp.einsum('bhnd,dr->bhnr', q, a_q), b_q) * LORA_SCALE
        v = v + jnp.einsum('bhnr,rd->bhnd', jnp.einsum('bhnd,dr->bhnr', v, a_v), b_v) * LORA_SCALE
        attn = jax.nn.softmax(jnp.einsum('bhnd,bhmd->bhnm', q, k) * ATTN_SCALE, axis=-1)
        out = jnp.einsum('bhnm,bhmd->bhnd', attn, v)
        out = out.transpose(0, 2, 1, 3).reshape(Bb, Nn, Cc)
        return out @ w_proj + b_proj

    def _L0_ffn_ref(tokens, gate_w, w1, b1, w2, b2):
        import jax, jax.numpy as jnp
        import numpy as np
        CAPACITY_FACTOR = 1.25
        B, S, H = tokens.shape
        E = gate_w.shape[0]
        N = B * S
        cap = int(CAPACITY_FACTOR * N / E)
        x = tokens.reshape(N, H)
        probs = jax.nn.softmax(x @ gate_w.T, axis=-1)
        top2_w, top2_idx = jax.lax.top_k(probs, 2)
        a_e = top2_idx.reshape(-1)
        a_w = top2_w.reshape(-1)
        tok_id = jnp.arange(2 * N) // 2
        counts = jnp.bincount(a_e, length=E)
        keep = counts <= cap
        valid = keep[a_e]
        onehot = jax.nn.one_hot(a_e, E, dtype=jnp.int32)
        pos = jnp.take_along_axis(jnp.cumsum(onehot, axis=0) - 1, a_e[:, None], axis=1)[:, 0]
        p = jnp.where(valid, jnp.minimum(pos, cap - 1), cap)
        x_a = x[tok_id]
        buf = jnp.zeros((E, cap + 1, H), dtype=x.dtype).at[a_e, p].set(x_a)
        h = jax.nn.silu(jnp.einsum('ech,efh->ecf', buf, w1) + b1[:, None, :])
        y = jnp.einsum('ecf,egf->ecg', h, w2) + b2[:, None, :]
        contrib = y[a_e, p] * (a_w * valid.astype(x.dtype))[:, None]
        out = contrib.reshape(N, 2, H).sum(axis=1)
        return out.reshape(B, S, H)

    def _L1_attn_ref(x, w_qkv, w_proj):
        import jax, jax.numpy as jnp
        import numpy as np
        N_HEAD = 16
        ROPE_BASE = 10000.0

        def _rotate_half(t):
            d = t.shape[-1] // 2
            return jnp.concatenate([-t[..., d:], t[..., :d]], axis=-1)

        def _rope_cos_sin(T, D, dtype):
            half = D // 2
            theta = 1.0 / ROPE_BASE ** (jnp.arange(half, dtype=dtype) / half)
            pos = jnp.arange(T, dtype=dtype)
            freqs = pos[:, None] * theta[None, :]
            cos = jnp.repeat(jnp.cos(freqs), 2, axis=-1)
            sin = jnp.repeat(jnp.sin(freqs), 2, axis=-1)
            return (cos, sin)
        B, T, C = x.shape
        H = N_HEAD
        D = C // H
        scale = D ** (-0.5)
        qkv = x @ w_qkv
        q, k, v = jnp.split(qkv, 3, axis=-1)
        to_heads = lambda t: t.reshape(B, T, H, D).transpose(0, 2, 1, 3)
        q, k, v = (to_heads(q), to_heads(k), to_heads(v))
        cos, sin = _rope_cos_sin(T, D, x.dtype)
        q = q * cos + _rotate_half(q) * sin
        k = k * cos + _rotate_half(k) * sin
        att = jnp.einsum('bhtd,bhsd->bhts', q, k) * scale
        causal = jnp.tril(jnp.ones((T, T), dtype=bool))
        att = jnp.where(causal, att, jnp.finfo(att.dtype).min)
        att = jax.nn.softmax(att, axis=-1)
        y = jnp.einsum('bhts,bhsd->bhtd', att, v)
        y = y.transpose(0, 2, 1, 3).reshape(B, T, C)
        return y @ w_proj

    def _L1_ffn_ref(x, signatures_raw, knot_values, temperature, compress_w1, compress_b1, compress_w2, compress_b2, spline_w1, spline_b1, spline_w2, spline_b2, directions, norm_gamma, norm_beta, output_scale):
        import jax, jax.numpy as jnp
        import numpy as np
        D_MODEL = 128
        NUM_TILES = 64
        TPC = 8
        NUM_CLUSTERS = NUM_TILES // TPC
        GRID = 16
        COMP_H = 32
        NUM_KNOTS = 8
        EPS_LN = 1e-05

        def _calibrate(scores, knots, temperature):
            K = knots.shape[0]
            normalized = jax.nn.sigmoid(scores / (temperature[0] + 1e-06))
            idx_float = normalized * (K - 1)
            idx_low = jnp.clip(idx_float.astype(jnp.int32), 0, K - 2)
            idx_high = idx_low + 1
            t = idx_float - idx_low.astype(scores.dtype)
            val_low = knots[idx_low]
            val_high = knots[idx_high]
            return val_low + t * (val_high - val_low)

        def _forward(x, signatures_raw, knot_values, temperature, compress_w1, compress_b1, compress_w2, compress_b2, spline_w1, spline_b1, spline_w2, spline_b2, directions, norm_gamma, norm_beta, output_scale):
            B, T, D = x.shape
            xf = x.reshape(-1, D)
            q = jnp.where(signatures_raw > 0.3, 1.0, jnp.where(signatures_raw < -0.3, -1.0, 0.0)).astype(signatures_raw.dtype)
            sigs = signatures_raw + jax.lax.stop_gradient(q - signatures_raw)
            cluster_sigs = jnp.sign(sigs.reshape(NUM_CLUSTERS, TPC, D).mean(axis=1))
            cluster_scores = xf @ cluster_sigs.T
            cluster_gates = _calibrate(cluster_scores, knot_values, temperature)
            cluster_idx = jnp.argmax(cluster_gates, axis=-1)
            tile_scores = xf @ sigs.T
            tile_gates = _calibrate(tile_scores, knot_values, temperature)
            gates_by_cluster = tile_gates.reshape(-1, NUM_CLUSTERS, TPC)
            sel_gates = jnp.take_along_axis(gates_by_cluster, cluster_idx[:, None, None], axis=1)[:, 0, :]
            local_idx = jnp.argmax(sel_gates, axis=-1)
            tile_idx = cluster_idx * TPC + local_idx
            h = jax.nn.gelu(xf @ compress_w1 + compress_b1, approximate=False)
            comp = jnp.tanh(h @ compress_w2 + compress_b2)
            w1 = spline_w1[tile_idx]
            b1 = spline_b1[tile_idx]
            hh = jax.nn.relu(jnp.einsum('ni,nig->ng', comp, w1) + b1)
            w2 = spline_w2[tile_idx]
            b2 = spline_b2[tile_idx]
            mag = jnp.einsum('ng,ngo->no', hh, w2) + b2
            ffn_out = mag * directions[tile_idx] * output_scale[0]
            y = xf + ffn_out
            mu = y.mean(axis=-1, keepdims=True)
            var = ((y - mu) ** 2).mean(axis=-1, keepdims=True)
            y = (y - mu) / jnp.sqrt(var + EPS_LN) * norm_gamma + norm_beta
            return y.reshape(B, T, D)
        return _forward(x, signatures_raw, knot_values, temperature, compress_w1, compress_b1, compress_w2, compress_b2, spline_w1, spline_b1, spline_w2, spline_b2, directions, norm_gamma, norm_beta, output_scale)
    x = L0_attn_x
    x = _layernorm(x + _L0_attn_ref(x, L0_attn_w_qkv, L0_attn_b_qkv, L0_attn_a_q, L0_attn_b_q, L0_attn_a_v, L0_attn_b_v, L0_attn_w_proj, L0_attn_b_proj), axis=-1)
    x = _layernorm(x + _L0_ffn_ref(x, L0_ffn_gate_w, L0_ffn_w1, L0_ffn_b1, L0_ffn_w2, L0_ffn_b2), axis=-1)
    x = _layernorm(x + _L1_attn_ref(x, L1_attn_w_qkv, L1_attn_w_proj), axis=-1)
    x = _layernorm(x + _L1_ffn_ref(x, L1_ffn_signatures_raw, L1_ffn_knot_values, L1_ffn_temperature, L1_ffn_compress_w1, L1_ffn_compress_b1, L1_ffn_compress_w2, L1_ffn_compress_b2, L1_ffn_spline_w1, L1_ffn_spline_b1, L1_ffn_spline_w2, L1_ffn_spline_b2, L1_ffn_directions, L1_ffn_norm_gamma, L1_ffn_norm_beta, L1_ffn_output_scale), axis=-1)
    return x

_drawn_inputs = setup_inputs


def setup_inputs(seed=0):
    import zlib

    import numpy as np

    out = dict(_drawn_inputs(seed))
    spreads = {'L1_ffn_compress_b1': (0.0, 0.8),
     'L1_ffn_compress_b2': (0.0, 2.0),
     'L1_ffn_spline_b1': (0.0, 2.0),
     'L1_ffn_spline_b2': (0.0, 2.0),
     'L1_ffn_norm_gamma': (1.0, 0.2),
     'L1_ffn_norm_beta': (0.0, 0.1)}
    factors = {'L1_ffn_signatures_raw': 8.0,
     'L1_ffn_knot_values': 8.0,
     'L1_ffn_compress_w1': 8.0,
     'L1_ffn_compress_w2': 8.0,
     'L1_ffn_spline_w1': 8.0,
     'L1_ffn_spline_w2': 8.0,
     'L1_ffn_directions': 8.0}
    for name, (base, spread) in spreads.items():
        noise = np.random.default_rng([zlib.crc32(name.encode()), seed]).standard_normal(out[name].shape)
        drawn = base * np.exp(spread * noise) if base else spread * noise
        out[name] = jnp.asarray(drawn.astype(out[name].dtype))
    for name, factor in factors.items():
        out[name] = (out[name] * factor).astype(out[name].dtype)
    return out
```

```python
from contextlib import ExitStack

import concourse.bass as bass
import numpy as np
from concourse import mybir

F32 = mybir.dt.float32
BF16 = mybir.dt.bfloat16
I32 = mybir.dt.int32
ALU = mybir.AluOpType
ACT = mybir.ActivationFunctionType
AX_X = mybir.AxisListType.X

P = 128
B, N, C = 32, 256, 128
H, D = 16, 8
R = 16
TILES = B * N // P
TB = N // P
LORA_SCALE = 32.0 / R
EPS = 1e-5
MASKED = -1e30

PARTS = 3
KROWS = PARTS * PARTS * D
MROWS = 2
NH = H // 2
SLOTS = 3
DEPTH = 5


def strided(ap, dims):
    return bass.AP(ap.tensor, ap.offset, [list(ap.ap[0])] + dims)


class Step:

    def __init__(self, i, off, slots, total):
        self.i, self.off, self.slots, self.total, self.loop = i, off, slots, total, not isinstance(i, int)

    def has(self, lag):
        return self.loop or 0 <= self.off - lag < self.total

    def seq(self, lag, k=1, c=0):
        return self.i * (self.slots * k) + (k * (self.off - lag) + c)

    def slot(self, lag):
        return (self.off - lag) % self.slots

    def turn(self, lag, k=16, c=0):
        return self.i * k + (k * ((self.off - lag) // self.slots + 1) + c)


def apart(eng, mem):
    eng.sem_inc(mem["apart"], 1)


def wait(eng, sem, value):
    if not isinstance(value, int) or value > 0:
        eng.wait_ge(sem, value)


def pipeline(eng, step, slots=SLOTS, depth=DEPTH, total=B, ahead=1):
    first = depth
    loops = (total - ahead - first) // slots
    for s in range(first):
        step(Step(0, s, slots, total))
    with eng.Fori(0, loops) as i:
        for r in range(slots):
            step(Step(i, first + r, slots, total))
    for s in range(first + slots * loops, total + depth - 1):
        step(Step(0, s, slots, total))


def attention(nc, name, mem, causal, x_dram, lora, rope):
    x_all, wqk, wv, wo, bqk, bv, bo = (mem[k] for k in ("x_all", "wqk", "wv", "wo", "bqk", "bv", "bo"))
    ident, ident_h, mask_qk, mask_kq = (mem[k] for k in ("ident", "ident_h", "mask_qk", "mask_kq"))
    scale = float(D) ** -0.5
    W = N // 2 + N if causal else 2 * N
    QKOPS = 4 if rope else 2
    MAXOPS = TB if causal else 1

    with ExitStack() as ctx:
        def sb(label, shape, dt=F32):
            return ctx.enter_context(nc.sbuf_tensor(f"{name}_{label}", shape, dt))

        def sem(label):
            return nc.alloc_semaphore(name=f"{name}_{label}")

        scratch = nc.dram_tensor(f"{name}_scratch", (SLOTS, 2, PARTS, P, N), BF16, kind="Internal").ap()
        x_in = sb("x_in", [P, SLOTS, TB, C])
        xT = sb("xT", [P, SLOTS, N])
        qk = sb("qk", [P, 2, N])
        q_half = sb("q_half", [P, 2, N]) if rope else None
        rest = sb("rest", [P, 2, N])
        parts = sb("parts", [P, 2, PARTS, N], BF16)
        q_st = sb("q_st", [P, SLOTS, H, N], BF16)
        k_st = sb("k_st", [P, SLOTS, H, N], BF16)
        negmax = sb("negmax", [P, TB, H])
        mparts = sb("mparts", [P, 2, TB, MROWS, NH], BF16)
        mT_sb = sb("mT_sb", [MROWS * NH, 2, N], BF16)
        v_sb = sb("v_sb", [P, SLOTS, TB, H * 32])
        probs = sb("probs", [P, 2, 4, 2 * N])
        oT_sb = sb("oT_sb", [P, 2 * N])
        rden = sb("rden", [P, TB, H])
        o_sb = sb("o_sb", [P, TB, C])
        onT_sb = sb("onT_sb", [P, N])
        x_res = sb("x_res", [P, TB, C])
        y_sb = sb("y_sb", [P, TB, C])
        stats = sb("stats", [P, TB, 6])
        mv = sb("mv", [P, TB, 2])
        var = sb("var", [P, TB])
        rstd = sb("rstd", [P, TB])

        row_ps = ctx.enter_context(nc.psum_tensor(f"{name}_row_ps", [P, 4, 512], F32))
        col_ps = ctx.enter_context(nc.psum_tensor(f"{name}_col_ps", [P, 2, 512], F32))
        out_ps = ctx.enter_context(nc.psum_tensor(f"{name}_out_ps", [P, 512], F32))
        misc_ps = ctx.enter_context(nc.psum_tensor(f"{name}_misc_ps", [P, 512], F32))

        x_loaded = [sem(f"x_loaded{j}") for j in range(SLOTS)]
        parts_stored = [sem(f"parts_stored{j}") for j in range(SLOTS)]
        q_stacked = [sem(f"q_stacked{j}") for j in range(SLOTS)]
        k_stacked = [sem(f"k_stacked{j}") for j in range(SLOTS)]
        m_placed = [[sem(f"m_placed{g}{j}") for j in range(SLOTS)] for g in range(2)]
        xT_ready, qk_ready, v_ready, rows_ready, mT_ready, cols_ready, pv_ready, o_ready, onT_ready, y_ready = (
            sem(x) for x in ("xT_ready", "qk_ready", "v_ready", "rows_ready", "mT_ready", "cols_ready", "pv_ready",
                             "o_ready", "onT_ready", "y_ready"))
        xT_kept, qk_kept, v_kept, max_kept, mhi_kept, mparts_kept, mT_kept, probs_kept, oT_kept = (
            sem(x) for x in ("xT_kept", "qk_kept", "v_kept", "max_kept", "mhi_kept", "mparts_kept", "mT_kept",
                             "probs_kept", "oT_kept"))
        rden_kept, o_kept, onT_kept, y_kept, stats_kept, mv_kept, x_res_kept, var_kept, rstd_kept, ln_kept = (
            sem(x) for x in ("rden_kept", "o_kept", "onT_kept", "y_kept", "stats_kept", "mv_kept", "x_res_kept",
                             "var_kept", "rstd_kept", "ln_kept"))
        cos_done, sin_done, turned = (sem(x) for x in ("cos_done", "sin_done", "turned"))
        hi_kept, rest_kept, mid_kept, lo_kept = (sem(x) for x in ("hi_kept", "rest_kept", "mid_kept", "lo_kept"))
        v_cleared, k_ones = sem("v_cleared"), sem("k_ones")
        block = ctx.enter_context(nc.Block())

        def head(n):
            u, j = n // 4, n % 4
            return NH * (u // 2) + 2 * j + u % 2

        @block.sync
        def _(sp):
            def load_x(st, lag):
                wait(sp, xT_ready, st.seq(lag, c=1 - SLOTS))
                src = x_all[:, bass.ds(st.seq(lag, TB), TB), :] if x_dram is None else \
                    x_dram[:, bass.ds(st.seq(lag, TB), TB), :]
                sp.dma_start(x_in[:, st.slot(lag), :, :], src).then_inc(x_loaded[st.slot(lag)], 16)

            def step(st):
                if st.has(-1):
                    load_x(st, -1)
                if st.has(3):
                    sp.wait_ge(mT_kept, st.seq(3, 2, 2))
                    sl = st.slot(3)
                    sp.dma_start(q_st[KROWS:KROWS + MROWS, sl, NH:H, :], mT_sb[:, 1, :]).then_inc(m_placed[1][sl], 16)
                if st.has(0):
                    sl = st.slot(0)
                    sp.wait_ge(lo_kept, st.seq(0, c=1))
                    apart(sp, mem)
                    wait(sp, q_stacked[sl], st.turn(SLOTS, 48))
                    apart(sp, mem)
                    wait(sp, k_stacked[sl], st.turn(SLOTS, 16))
                    sp.dma_start(scratch[sl].rearrange("s j p n -> p (s j) n"),
                                 parts[:, :, :, :].rearrange("p s j n -> p (s j) n")).then_inc(parts_stored[sl], 16)
                if st.has(2):
                    sp.wait_ge(mT_kept, st.seq(2, 2, 1))
                    sl = st.slot(2)
                    sp.dma_start(q_st[KROWS:KROWS + MROWS, sl, 0:NH, :], mT_sb[:, 0, :]).then_inc(m_placed[0][sl], 16)
                if st.has(0):
                    sl = st.slot(0)
                    sp.wait_ge(k_ones, 1)
                    sp.wait_ge(parts_stored[sl], st.turn(0))
                    apart(sp, mem)
                    wait(sp, cols_ready, st.seq(SLOTS, H, H))
                    q_src = scratch[sl, 0].rearrange("j (d h) n -> j d (h n)", d=D)
                    k_src = scratch[sl, 1].rearrange("j (d h) n -> (j d) (h n)", d=D)
                    for j in range(PARTS):
                        rows = slice(PARTS * D * j, PARTS * D * (j + 1))
                        src = q_src[j]
                        thrice = bass.AP(src.tensor, src.offset, [[0, PARTS]] + [list(x) for x in src.ap])
                        sp.dma_start(q_st[rows, sl, :, :].rearrange("p h n -> p (h n)"), thrice)\
                            .then_inc(q_stacked[sl], 16)
                    thrice = bass.AP(k_src.tensor, k_src.offset, [[0, PARTS]] + [list(x) for x in k_src.ap])
                    sp.dma_start(k_st[0:KROWS, sl, :, :].rearrange("p h n -> p (h n)"), thrice)\
                        .then_inc(k_stacked[sl], 16)

            load_x(Step(0, 0, SLOTS, B), 0)
            pipeline(sp, step)

        @block.gpsimd
        def _(pool):
            nc.gpsimd.memset(k_st[64:96, :, :, :], 1.0).then_inc(k_ones, 1)
            pool.wait_ge(k_ones, 1)
            nc.gpsimd.memset(v_sb[:, :, :, :], 0.0).then_inc(v_cleared, 1)
            pool.wait_ge(v_cleared, 1)
            for a in range(2):
                one = v_sb[:, :, :, :].rearrange("p s t (q c) -> p (s t q) c", c=64)[:, :, 41 * a + D:41 * a + D + 1]
                nc.gpsimd.memset(one, 1.0).then_inc(v_cleared, 1)
            if x_dram is not None:
                pool.wait_ge(mem["x_all_loaded"], 16 * 8)

            def step(st):
                if st.has(4) and x_dram is not None:
                    wait(pool, y_kept, st.seq(4))
                    nc.gpsimd.tensor_tensor(x_res[:, :, :], x_all[:, bass.ds(st.seq(4, TB), TB), :],
                                            bo[:, :].unsqueeze(1).broadcast_to([P, TB, C]), ALU.add)\
                        .then_inc(x_res_kept, 1)
                if st.has(0):
                    pool.wait_ge(qk_kept, st.seq(0, QKOPS, QKOPS))
                    if rope:
                        pool.wait_ge(qk_kept, st.seq(0, QKOPS, QKOPS))
                        cos, sin = (mem[k][:, :].unsqueeze(1).broadcast_to([P, 2, N]) for k in ("cos", "sin"))
                        nc.gpsimd.tensor_tensor(q_half[:, :, :], q_half[:, :, :], sin, ALU.mult).then_inc(sin_done, 1)
                        nc.gpsimd.tensor_tensor(qk[:, :, :], qk[:, :, :], cos, ALU.mult).then_inc(cos_done, 1)
                        pool.wait_ge(sin_done, st.seq(0, c=1))
                        pool.wait_ge(cos_done, st.seq(0, c=1))
                        nc.gpsimd.tensor_tensor(qk[:, :, :], qk[:, :, :], q_half[:, :, :], ALU.add)\
                            .then_inc(turned, 1)
                        pool.wait_ge(turned, st.seq(0, c=1))
                    if st.has(1):
                        pool.wait_ge(parts_stored[st.slot(1)], st.turn(1))
                    apart(pool, mem)
                    nc.gpsimd.tensor_scalar(parts[:, :, 0, :], qk[:, :, :], 1.0, 0.0, ALU.mult, ALU.add)\
                        .then_inc(hi_kept, 1)
                    pool.wait_ge(hi_kept, st.seq(0, c=1))
                    nc.gpsimd.tensor_tensor(rest[:, :, :], qk[:, :, :], parts[:, :, 0, :], ALU.subtract)\
                        .then_inc(rest_kept, 1)
                    pool.wait_ge(rest_kept, st.seq(0, c=1))
                    apart(pool, mem)
                    nc.gpsimd.tensor_scalar(parts[:, :, 1, :], rest[:, :, :], 1.0, 0.0, ALU.mult, ALU.add)\
                        .then_inc(mid_kept, 1)
                    pool.wait_ge(mid_kept, st.seq(0, c=1))
                    nc.gpsimd.tensor_tensor(parts[:, :, 2, :], rest[:, :, :], parts[:, :, 1, :], ALU.subtract)\
                        .then_inc(lo_kept, 1)
                if st.has(4):
                    pool.wait_ge(var_kept, st.seq(4, c=1))
                    nc.gpsimd.tensor_tensor(rstd[:, :], var[:, :], mem["minus_half"][:, 0:TB], ALU.pow)\
                        .then_inc(rstd_kept, 1)

            pipeline(pool, step)

        @block.scalar
        def _(act):
            def step(st):
                for n in range(H):
                    if st.has(3):
                        u, j = n // 4, n % 4
                        act.wait_ge(cols_ready, st.seq(3, H, n + 1))
                        if j == 0:
                            wait(act, pv_ready, st.seq(3, 4, u - 1))
                        nc.scalar.activation(probs[:, u % 2, j, 0:W], col_ps[:, n % 2, 0:W], ACT.Exp,
                                             scale=scale).then_inc(probs_kept, 1)
                    if n == 0 and st.has(0):
                        act.wait_ge(xT_ready, st.seq(0, c=1))
                        wait(act, v_ready, st.seq(SLOTS, c=1))
                        nc.scalar.copy(xT[:, st.slot(0), :], misc_ps[:, 0:N]).then_inc(xT_kept, 1)
                    if n == 1 and st.has(3):
                        act.wait_ge(mT_ready, st.seq(3, 2, 2))
                        if st.has(4):
                            act.wait_ge(m_placed[1][st.slot(4)], st.turn(4))
                        nc.scalar.copy(mT_sb[:, 1, :], misc_ps[0:MROWS * NH, 0:N // 2].bitcast(BF16))\
                            .then_inc(mT_kept, 1)
                    if n == 2 and st.has(0):
                        act.wait_ge(qk_ready, st.seq(0, c=1))
                        wait(act, rest_kept, st.seq(0))
                        if rope:
                            for to, of in ((0, P // 2), (P // 2, 0)):
                                nc.scalar.copy(q_half[to:to + P // 2, :, :].rearrange("p s n -> p (s n)"),
                                               misc_ps[of:of + P // 2, :]).then_inc(qk_kept, 1)
                        for s in range(2):
                            if lora:
                                nc.scalar.activation(qk[:, s, :], misc_ps[:, s * N:(s + 1) * N], ACT.Identity,
                                                     bias=bqk[:, s:s + 1]).then_inc(qk_kept, 1)
                            else:
                                nc.scalar.copy(qk[:, s, :], misc_ps[:, s * N:(s + 1) * N]).then_inc(qk_kept, 1)
                    if n == 3 and st.has(4):
                        act.wait_ge(pv_ready, st.seq(4, 4, 4))
                        wait(act, o_ready, st.seq(4))
                        nc.scalar.copy(oT_sb[:, :], out_ps[:, :]).then_inc(oT_kept, 1)
                    if n == 8 and st.has(4):
                        act.wait_ge(onT_ready, st.seq(4, c=1))
                        wait(act, y_ready, st.seq(4))
                        nc.scalar.copy(onT_sb[:, :], misc_ps[:, 0:N]).then_inc(onT_kept, 1)
                    if n == 10 and st.has(2):
                        act.wait_ge(mT_ready, st.seq(2, 2, 1))
                        if st.has(3):
                            act.wait_ge(m_placed[0][st.slot(3)], st.turn(3))
                        nc.scalar.copy(mT_sb[:, 0, :], misc_ps[0:MROWS * NH, 0:N // 2].bitcast(BF16))\
                            .then_inc(mT_kept, 1)

            pipeline(act, step)

        @block.vector
        def _(dve):
            def row_max(st, p):
                dve.wait_ge(rows_ready, st.seq(2, NH, p + 1))
                if p % 4 == 0:
                    wait(dve, mparts_kept, st.seq(2, 2, p // 4 - 1))
                bank = 2 * (p % 2)
                if causal:
                    for t in range(TB):
                        keys = (t + 1) * P
                        nc.vector.tensor_reduce(
                            negmax[:, t, 2 * p:2 * p + 2],
                            row_ps[:, bank + t, 0:2 * keys].rearrange("p (a k) -> p a k", a=2),
                            AX_X, ALU.max, negate=True).then_inc(max_kept, 1)
                else:
                    nc.vector.tensor_reduce(
                        negmax[:, :, 2 * p:2 * p + 2],
                        row_ps[:, bank:bank + 2, :].rearrange("p t (a k) -> p t a k", a=2),
                        AX_X, ALU.max, negate=True).then_inc(max_kept, 1)

            def split_max(st, g):
                dve.wait_ge(max_kept, st.seq(2, MAXOPS * NH, MAXOPS * NH // 2 * (g + 1)))
                wait(dve, mT_ready, st.seq(3, 2, g + 1))
                half = negmax[:, :, NH * g:NH * (g + 1)]
                nc.vector.tensor_copy(mparts[:, g, :, 0, :], half).then_inc(mhi_kept, 1)
                dve.wait_ge(mhi_kept, st.seq(2, 2, g + 1))
                nc.vector.tensor_tensor(mparts[:, g, :, 1, :], half, mparts[:, g, :, 0, :], ALU.subtract)\
                    .then_inc(mparts_kept, 1)

            def keep_v(st):
                dve.wait_ge(v_ready, st.seq(2, c=1))
                wait(dve, pv_ready, st.seq(2 + SLOTS, 4, 4))
                dve.wait_ge(v_cleared, 3)
                for t in range(TB):
                    to = strided(v_sb[:, st.slot(2), t, 0:1], [[64, H // 2], [41, 2], [1, D]])
                    of = misc_ps[:, t * C:(t + 1) * C].rearrange("p (q a d) -> p q a d", a=2, d=D)
                    if lora:
                        nc.vector.tensor_tensor(to, of, bv[:, :].rearrange("p (q a d) -> p q a d", a=2, d=D),
                                                ALU.add).then_inc(v_kept, 1)
                    else:
                        nc.vector.tensor_copy(to, of).then_inc(v_kept, 1)

            def normalise_o(st):
                dve.wait_ge(o_ready, st.seq(4, c=1))
                wait(dve, onT_ready, st.seq(4))
                nc.vector.reciprocal(rden[:, :, :].rearrange("p t (j a) -> p (t j) a", a=2),
                                     strided(misc_ps[:, D:D + 1], [[32, 2 * NH], [D + 1, 2]])).then_inc(rden_kept, 1)
                dve.wait_ge(rden_kept, st.seq(4, c=1))
                for t in range(TB):
                    nc.vector.tensor_tensor(
                        o_sb[:, t, :].rearrange("p (j a d) -> p j a d", a=2, d=D),
                        strided(misc_ps[:, 256 * t:256 * t + 1], [[32, NH], [D + 1, 2], [1, D]]),
                        rden[:, t, :].rearrange("p (j a) -> p j a", a=2).unsqueeze(3).broadcast_to([P, NH, 2, D]),
                        ALU.mult).then_inc(o_kept, 1)

            def add_residual(st):
                dve.wait_ge(y_ready, st.seq(4, c=1))
                if x_dram is not None:
                    dve.wait_ge(x_res_kept, st.seq(4, c=1))
                    x_old = x_res[:, :, :]
                else:
                    x_old = x_all[:, bass.ds(st.seq(4, TB), TB), :]
                nc.vector.tensor_tensor(y_sb[:, :, :], misc_ps[:, 0:N].rearrange("p (t c) -> p t c", t=TB), x_old,
                                        ALU.add).then_inc(y_kept, 1)
                dve.wait_ge(y_kept, st.seq(4, c=1))
                for t in range(TB):
                    nc.vector.bn_stats(stats[:, t, :], y_sb[:, t, :]).then_inc(stats_kept, 1)

            def variance(st):
                dve.wait_ge(stats_kept, st.seq(4, TB, TB))
                apart(dve, mem)
                for t in range(TB):
                    nc.vector.bn_aggr(mv[:, t, :], stats[:, t, :]).then_inc(mv_kept, 1)
                dve.wait_ge(mv_kept, st.seq(4, TB, TB))
                wait(dve, rstd_kept, st.seq(4))
                nc.vector.tensor_scalar(var[:, :], mv[:, :, 1], EPS, None, ALU.add).then_inc(var_kept, 1)

            def layer_norm(st):
                dve.wait_ge(rstd_kept, st.seq(4, c=1))
                for t in range(TB):
                    nc.vector.tensor_scalar(x_all[:, bass.ds(st.seq(4, TB, t), 1), :].rearrange("p t c -> p (t c)"),
                                            y_sb[:, t, :], mv[:, t, 0:1], rstd[:, t:t + 1],
                                            ALU.subtract, ALU.mult).then_inc(ln_kept, 1)

            def step(st):
                for n in range(H):
                    if n % 2 == 0 and st.has(2):
                        row_max(st, n // 2)
                    if n == 5 and st.has(4):
                        normalise_o(st)
                    if n == 6 and st.has(2):
                        split_max(st, 0)
                    if n == 7 and st.has(2):
                        keep_v(st)
                    if n == 13 and st.has(4):
                        add_residual(st)
                    if n == 14 and st.has(2):
                        split_max(st, 1)
                    if n == 14 and st.has(4):
                        variance(st)
                    if n == 15 and st.has(4):
                        layer_norm(st)

            pipeline(dve, step)

        @block.tensor
        def _(pe):
            def transpose_x(st):
                pe.wait_ge(x_loaded[st.slot(0)], st.turn(0))
                if st.has(5):
                    pe.wait_ge(y_kept, st.seq(5, c=1))
                elif st.has(3):
                    pe.wait_ge(mT_kept, st.seq(3, 2, 1))
                elif st.has(1):
                    pe.wait_ge(qk_kept, st.seq(1, QKOPS, QKOPS))
                for t in range(TB):
                    last = nc.tensor.transpose(misc_ps[:, t * P:(t + 1) * P], x_in[:, st.slot(0), t, :], ident[:, :])
                last.then_inc(xT_ready, 1)

            def transpose_max(st, lag, g):
                if g == 1:
                    if st.has(0):
                        pe.wait_ge(xT_kept, st.seq(0, c=1))
                    elif st.has(5):
                        pe.wait_ge(y_kept, st.seq(5, c=1))
                else:
                    pe.wait_ge(v_kept, st.seq(2, TB, TB))
                    if st.has(4):
                        pe.wait_ge(onT_kept, st.seq(4, c=1))
                pe.wait_ge(mparts_kept, st.seq(lag, 2, g + 1))
                for t in range(TB):
                    last = nc.tensor.transpose(
                        misc_ps[0:MROWS * NH, t * P // 2:(t + 1) * P // 2].bitcast(BF16),
                        mparts[:, g, t, :, :].rearrange("p m h -> p (m h)"), ident_h[:, :])
                last.then_inc(mT_ready, 1)

            def project_qk(st):
                pe.wait_ge(xT_kept, st.seq(0, c=1))
                if st.has(3):
                    pe.wait_ge(mT_kept, st.seq(3, 2, 2))
                for s in range(2):
                    last = nc.tensor.matmul(misc_ps[:, s * N:(s + 1) * N], wqk[:, s, :], xT[:, st.slot(0), :],
                                            start=True, stop=True)
                last.then_inc(qk_ready, 1)

            def transpose_o(st):
                if st.has(0):
                    pe.wait_ge(qk_kept, st.seq(0, QKOPS, QKOPS))
                elif st.has(3):
                    pe.wait_ge(mT_kept, st.seq(3, 2, 2))
                elif st.has(5):
                    pe.wait_ge(y_kept, st.seq(5, c=1))
                pe.wait_ge(oT_kept, st.seq(4, c=1))
                for t in range(TB):
                    for g in range(2):
                        last = nc.tensor.transpose(misc_ps[:, (2 * t + g) * P:(2 * t + g + 1) * P],
                                                   oT_sb[:, g * N + t * P:g * N + (t + 1) * P], ident[:, :])
                last.then_inc(o_ready, 1)

            def project_v(st):
                if st.has(4):
                    pe.wait_ge(o_kept, st.seq(4, TB, TB))
                elif st.has(3):
                    pe.wait_ge(mT_kept, st.seq(3, 2, 2))
                if st.has(0):
                    pe.wait_ge(qk_kept, st.seq(0, QKOPS, QKOPS))
                for t in range(TB):
                    last = nc.tensor.matmul(misc_ps[:, t * C:(t + 1) * C], xT[:, st.slot(2), t * P:(t + 1) * P],
                                            wv[:, :], start=True, stop=True)
                last.then_inc(v_ready, 1)

            def transpose_on(st):
                if st.has(2):
                    pe.wait_ge(v_kept, st.seq(2, TB, TB))
                pe.wait_ge(o_kept, st.seq(4, TB, TB))
                for t in range(TB):
                    last = nc.tensor.transpose(misc_ps[:, t * P:(t + 1) * P], o_sb[:, t, :], ident[:, :])
                last.then_inc(onT_ready, 1)

            def project_o(st):
                if st.has(2):
                    pe.wait_ge(mT_kept, st.seq(2, 2, 1))
                pe.wait_ge(onT_kept, st.seq(4, c=1))
                for t in range(TB):
                    last = nc.tensor.matmul(misc_ps[:, t * C:(t + 1) * C], onT_sb[:, t * P:(t + 1) * P], wo[:, :],
                                            start=True, stop=True)
                last.then_inc(y_ready, 1)

            def score_rows(st, p):
                sl = st.slot(2)
                if p == 0:
                    pe.wait_ge(q_stacked[sl], st.turn(2, 48))
                    pe.wait_ge(k_stacked[sl], st.turn(2, 16))
                wait(pe, max_kept, st.seq(2, MAXOPS * NH, MAXOPS * (p - 1)))
                for t in range(TB):
                    bank = row_ps[:, 2 * (p % 2) + t, :]
                    keys = (t + 1) * P if causal else N
                    if causal:
                        seen = bank[:, 0:2 * keys].rearrange("p (a k) -> p a k", a=2)
                        nc.tensor.matmul(seen[:, :, keys - P:keys], ident_h[:, :], mask_qk[:, :, :],
                                         start=True, stop=False, skip_group_check=True)
                    for a in range(2):
                        h = 2 * p + a
                        last = nc.tensor.matmul(bank[:, a * keys:(a + 1) * keys],
                                                q_st[0:KROWS, sl, h, t * P:(t + 1) * P], k_st[0:KROWS, sl, h, 0:keys],
                                                start=not causal, stop=True, skip_group_check=causal)
                last.then_inc(rows_ready, 1)

            def score_cols(st, n):
                sl, h = st.slot(3), head(n)
                if n == 0:
                    pe.wait_ge(m_placed[0][sl], st.turn(3))
                if n == H // 2:
                    pe.wait_ge(m_placed[1][sl], st.turn(3))
                wait(pe, probs_kept, st.seq(3, H, n - 1))
                bank = col_ps[:, n % 2, :]
                rows = KROWS + MROWS
                if causal:
                    seen = bank[:, 0:2 * N].rearrange("p (a q) -> p a q", a=2)
                    nc.tensor.matmul(seen[:, :, 0:P], ident_h[:, :], mask_kq[:, :, :],
                                     start=True, stop=False, skip_group_check=True)
                for t in range(TB):
                    first = t * P if causal else 0
                    last = nc.tensor.matmul(bank[:, t * N:(t + 1) * N - first],
                                            k_st[0:rows, sl, h, t * P:(t + 1) * P], q_st[0:rows, sl, h, first:N],
                                            start=not causal, stop=True, skip_group_check=causal)
                last.then_inc(cols_ready, 1)

            def sum_values(st, lag, u):
                g, a = u // 2, u % 2
                if u == 0:
                    wait(pe, oT_kept, st.seq(lag))
                    pe.wait_ge(v_kept, st.seq(lag, TB, TB))
                pe.wait_ge(probs_kept, st.seq(lag, H, 4 * u + 4))
                for t in range(TB):
                    first = t * P if causal else 0
                    for j in range(4):
                        h = head(4 * u + j)
                        last = nc.tensor.matmul(out_ps[32 * j:32 * j + 32, g * N + first:(g + 1) * N],
                                                v_sb[:, st.slot(lag), t, 32 * h:32 * h + 32],
                                                probs[:, u % 2, j, t * N:(t + 1) * N - first],
                                                start=a == 0 and t == 0, stop=a == 1 and t == TB - 1,
                                                skip_group_check=True)
                last.then_inc(pv_ready, 1)

            def step(st):
                for n in range(H):
                    if st.has(3):
                        score_cols(st, n)
                    if n % 2 == 0 and st.has(2):
                        score_rows(st, n // 2)
                    if n == 0 and st.has(0):
                        transpose_x(st)
                    if n == 1 and st.has(3):
                        transpose_max(st, 3, 1)
                    if n == 2 and st.has(4):
                        sum_values(st, 4, 3)
                    if n == 2 and st.has(0):
                        project_qk(st)
                    if n == 4 and st.has(4):
                        transpose_o(st)
                    if n in (6, 10, 14) and st.has(3):
                        sum_values(st, 3, (n - 6) // 4)
                    if n == 6 and st.has(2):
                        project_v(st)
                    if n == 8 and st.has(4):
                        transpose_on(st)
                    if n == 10 and st.has(2):
                        transpose_max(st, 2, 0)
                    if n == 12 and st.has(4):
                        project_o(st)

            pipeline(pe, step)



E = 8
CAP = int(1.25 * B * N / E)
GT = 8
GROUPS = TILES // GT
MT = 4


def groups(eng, step):
    pipeline(eng, step, 2, 3, GROUPS, 0)


def moe(nc, mem, w):
    x_all, ident = mem["x_all"], mem["ident"]
    with ExitStack() as ctx:
        def sb(label, shape, dt=F32):
            return ctx.enter_context(nc.sbuf_tensor(f"moe_{label}", shape, dt))

        def sem(label):
            return nc.alloc_semaphore(name=f"moe_{label}")

        gate_T = sb("gate_T", [P, E])
        rank = sb("rank", [P, E])
        ones = sb("ones", [P, P])
        xs = sb("xs", [P, 2, GT, C])
        xT = sb("xT", [P, 2, GT * P])
        logits = sb("logits", [P, TILES, E])
        probs = sb("probs", [P, TILES, E])
        left = sb("left", [P, TILES, E])
        equal = sb("equal", [P, TILES, E])
        score = sb("score", [P, TILES, E])
        chosen = [sb(f"chosen{k}", [P, TILES, E]) for k in range(2)]
        top = sb("top", [P, TILES])
        total = sb("total", [P, TILES])
        counts = sb("counts", [P, E])
        keep = sb("keep", [P, E])
        any_kept = sb("any_kept", [P, 1])
        flag = sb("flag", [P, 1], I32)
        weight = sb("weight", [P, TILES, E])
        stats = sb("stats", [P, 2, GT, 6])
        mv = sb("mv", [P, 2, GT, 2])
        var = sb("var", [P, 2, GT])
        rstd = sb("rstd", [P, 2, GT])
        e_w = sb("e_w", [P, 2, E, C])
        e_wT = sb("e_wT", [P, 2, E, C])
        e_b = sb("e_b", [P, 2, E, C])
        e_x = sb("e_x", [P, MT, C])
        e_xT = sb("e_xT", [P, MT * P])
        e_pre = sb("e_pre", [P, MT, C])
        e_h = sb("e_h", [P, MT, C])
        e_hT = sb("e_hT", [P, MT * P])
        e_y = sb("e_y", [P, MT, C])
        e_acc = sb("e_acc", [P, MT, C])

        t_ps = ctx.enter_context(nc.psum_tensor("moe_t_ps", [P, 2, 2, 512], F32))
        l_ps = ctx.enter_context(nc.psum_tensor("moe_l_ps", [P, 2, 512], F32))
        c_ps = ctx.enter_context(nc.psum_tensor("moe_c_ps", [P, 512], F32))

        loaded, consts, xs_loaded = sem("loaded"), sem("consts"), [sem(f"xs_loaded{j}") for j in range(2)]
        xT_ready, xT_kept, logits_ready, logits_kept = (
            sem(x) for x in ("xT_ready", "xT_kept", "logits_ready", "logits_kept"))
        shifted, exp_kept, routed, counts_ready, flag_kept = (
            sem(x) for x in ("shifted", "exp_kept", "routed", "counts_ready", "flag_kept"))
        stats_kept, mv_kept, var_kept, rstd_kept, ln_kept = (
            sem(x) for x in ("stats_kept", "mv_kept", "var_kept", "rstd_kept", "ln_kept"))
        e_loaded, e_x_loaded, ewT_ready, ewT_kept = (
            sem(x) for x in ("e_loaded", "e_x_loaded", "ewT_ready", "ewT_kept"))
        exT_ready, exT_kept, h_ready, pre_kept, h_kept, hT_ready, hT_kept, y_ready = (
            sem(x) for x in ("exT_ready", "exT_kept", "h_ready", "pre_kept", "h_kept", "hT_ready", "hT_kept",
                             "y_ready"))
        y_kept, acc_kept, cleared, experts_done = (sem(x) for x in ("y_kept", "acc_kept", "cleared", "experts_done"))

        COUNTED = 15

        with nc.Block() as block:

            @block.sync
            def _(sp):
                sp.dma_start(gate_T[:, :], w["L0_ffn_gate_w"].rearrange("e c -> c e"),
                             allow_slow_non_contiguous=True).then_inc(loaded, 16)

                def step(st):
                    if st.has(0):
                        j = st.slot(0)
                        wait(sp, xT_ready, st.seq(1))
                        sp.dma_start(xs[:, j, :, :], x_all[:, bass.ds(st.seq(0, GT), GT), :])\
                            .then_inc(xs_loaded[j], 16)

                groups(sp, step)

            @block.gpsimd
            def _(pool):
                for e in range(E):
                    nc.gpsimd.memset(rank[:, e:e + 1], float(E - e)).then_inc(consts, 1)
                nc.gpsimd.memset(ones[:, :], 1.0).then_inc(consts, 1)

            @block.tensor
            def _(pe):
                pe.wait_ge(loaded, 16)

                def step(st):
                    if st.has(0):
                        j = st.slot(0)
                        pe.wait_ge(xs_loaded[j], st.turn(0))
                        wait(pe, xT_kept, st.seq(1, 2))
                        for t in range(GT):
                            last = nc.tensor.transpose(t_ps[:, j, t // 4, t % 4 * P:(t % 4 + 1) * P], xs[:, j, t, :],
                                                       ident[:, :])
                        last.then_inc(xT_ready, 1)
                    if st.has(1):
                        j = st.slot(1)
                        pe.wait_ge(xT_kept, st.seq(1, 2, 2))
                        wait(pe, logits_kept, st.seq(2))
                        for t in range(GT):
                            last = nc.tensor.matmul(l_ps[:, j, t * E:(t + 1) * E], xT[:, j, t * P:(t + 1) * P],
                                                    gate_T[:, :], start=True, stop=True)
                        last.then_inc(logits_ready, 1)

                groups(pe, step)
                pe.wait_ge(routed, COUNTED)
                nc.tensor.matmul(c_ps[:, 0:E], ones[:, :], counts[:, :], start=True, stop=True)\
                    .then_inc(counts_ready, 1)

            @block.scalar
            def _(act):
                def step(st):
                    if st.has(0):
                        j = st.slot(0)
                        act.wait_ge(xT_ready, st.seq(0, c=1))
                        wait(act, logits_ready, st.seq(1))
                        for b in range(2):
                            nc.scalar.copy(xT[:, j, b * 512:(b + 1) * 512], t_ps[:, j, b, :]).then_inc(xT_kept, 1)

                groups(act, step)
                act.wait_ge(shifted, 1)
                nc.scalar.activation(probs[:, :, :], left[:, :, :], ACT.Exp).then_inc(exp_kept, 1)

            @block.vector
            def _(dve):
                done = [0]

                def then(ins):
                    ins.then_inc(routed, 1)
                    done[0] += 1
                    dve.wait_ge(routed, done[0])

                def over_experts(ap):
                    return ap.unsqueeze(2).broadcast_to([P, TILES, E])

                def step(st):
                    if st.has(0):
                        dve.wait_ge(logits_ready, st.seq(0, c=1))
                        nc.vector.tensor_copy(logits[:, bass.ds(st.seq(0, GT), GT), :],
                                              l_ps[:, st.slot(0), 0:GT * E].rearrange("p (t e) -> p t e", e=E))\
                            .then_inc(logits_kept, 1)

                groups(dve, step)
                dve.wait_ge(logits_kept, GROUPS)
                dve.wait_ge(consts, E + 1)
                then(nc.vector.tensor_reduce(top[:, :], logits[:, :, :], AX_X, ALU.max))
                nc.vector.tensor_tensor(left[:, :, :], logits[:, :, :], over_experts(top[:, :]), ALU.subtract)\
                    .then_inc(shifted, 1)
                dve.wait_ge(exp_kept, 1)
                then(nc.vector.tensor_reduce(total[:, :], probs[:, :, :], AX_X, ALU.add))
                then(nc.vector.reciprocal(top[:, :], total[:, :]))
                then(nc.vector.tensor_tensor(probs[:, :, :], probs[:, :, :], over_experts(top[:, :]), ALU.mult))
                of = probs
                for k in range(2):
                    then(nc.vector.tensor_reduce(top[:, :], of[:, :, :], AX_X, ALU.max))
                    then(nc.vector.tensor_tensor(equal[:, :, :], of[:, :, :], over_experts(top[:, :]), ALU.is_equal))
                    then(nc.vector.tensor_tensor(score[:, :, :], equal[:, :, :],
                                                 rank[:, :].unsqueeze(1).broadcast_to([P, TILES, E]), ALU.mult))
                    then(nc.vector.tensor_reduce(top[:, :], score[:, :, :], AX_X, ALU.max))
                    then(nc.vector.tensor_tensor(chosen[k][:, :, :], score[:, :, :], over_experts(top[:, :]),
                                                 ALU.is_equal))
                    if k == 0:
                        nc.vector.scalar_tensor_tensor(out=left[:, :, :], in0=chosen[0][:, :, :], scalar=-2.0,
                                                       in1=probs[:, :, :], op0=ALU.mult, op1=ALU.add)\
                            .then_inc(shifted, 1)
                        dve.wait_ge(shifted, 2)
                        of = left
                nc.vector.tensor_tensor(chosen[0][:, :, :], chosen[0][:, :, :], chosen[1][:, :, :], ALU.add)\
                    .then_inc(shifted, 1)
                dve.wait_ge(shifted, 3)
                then(nc.vector.tensor_reduce(counts[:, :], chosen[0][:, :, :].rearrange("p t e -> p e t"), AX_X,
                                             ALU.add))
                assert done[0] == COUNTED
                dve.wait_ge(counts_ready, 1)
                then(nc.vector.tensor_scalar(keep[:, :], c_ps[:, 0:E], float(CAP), None, ALU.is_le))
                then(nc.vector.tensor_reduce(any_kept[:, :], keep[:, :], AX_X, ALU.max))
                nc.vector.tensor_copy(flag[:, :], any_kept[:, :]).then_inc(flag_kept, 1)

        FREE = 1
        with nc.Block() as block:

            @block.sync
            def _(sp):
                with sp.If(sp.value_load(flag[0:1, 0:1], min_val=0, max_val=1) > 0):
                    for n, k in enumerate(("1", "2")):
                        sp.dma_start(e_w[:, n, :, :], w[f"L0_ffn_w{k}"].rearrange("e o i -> o e i"))\
                            .then_inc(e_loaded, 16)
                        b = w[f"L0_ffn_b{k}"]
                        sp.dma_start(e_b[:, n, :, :].rearrange("p e c -> p (e c)"),
                                     bass.AP(b.tensor, b.offset, [[0, P], [1, E * C]])).then_inc(e_loaded, 16)
                    with sp.Fori(0, TILES // MT) as g:
                        sp.wait_ge(experts_done, g + FREE)
                        sp.dma_start(e_x[:, :, :], x_all[:, bass.ds(g * MT, MT), :]).then_inc(e_x_loaded, 16)
                with sp.Else():
                    sp.nop()
                sp.nop()

            @block.tensor
            def _(pe):
                with pe.If(pe.value_load(flag[0:1, 0:1], min_val=0, max_val=1) > 0):
                    for s in (h_ready, hT_ready, y_ready):
                        pe.sem_inc(s, FREE)
                    pe.wait_ge(e_loaded, 64)
                    for n in range(2):
                        for half in range(2):
                            k = 2 * n + half
                            if k >= 2:
                                pe.wait_ge(ewT_kept, k - 1)
                            for q in range(E // 2):
                                last = nc.tensor.transpose(t_ps[:, 0, k % 2, q * P:(q + 1) * P],
                                                           e_w[:, n, half * E // 2 + q, :], ident[:, :])
                            last.then_inc(ewT_ready, 1)
                    pe.wait_ge(ewT_kept, 4)
                    with pe.Fori(0, TILES // MT) as g:
                        pe.wait_ge(e_x_loaded, g * 16 + 16)
                        pe.wait_ge(exT_kept, g + FREE)
                        for t in range(MT):
                            last = nc.tensor.transpose(t_ps[:, 0, 0, t * P:(t + 1) * P], e_x[:, t, :], ident[:, :])
                        last.then_inc(exT_ready, 1)
                        pe.wait_ge(exT_kept, g + (1 + FREE))
                        apart(pe, mem)
                        with pe.Fori(0, E) as e:
                            pe.wait_ge(pre_kept, g * E + e + FREE)
                            for t in range(MT):
                                last = nc.tensor.matmul(t_ps[:, 0, 1, t * P:(t + 1) * P], e_xT[:, t * P:(t + 1) * P],
                                                        e_wT[:, 0, bass.ds(e, 1), :].rearrange("p e c -> p (e c)"),
                                                        start=True, stop=True)
                            last.then_inc(h_ready, 1)
                            pe.wait_ge(h_kept, g * E + (e + (1 + FREE)))
                            pe.wait_ge(hT_kept, g * E + e + FREE)
                            for t in range(MT):
                                last = nc.tensor.transpose(t_ps[:, 1, 0, t * P:(t + 1) * P], e_h[:, t, :],
                                                           ident[:, :])
                            last.then_inc(hT_ready, 1)
                            pe.wait_ge(hT_kept, g * E + (e + (1 + FREE)))
                            pe.wait_ge(y_kept, g * E + e + FREE)
                            for t in range(MT):
                                last = nc.tensor.matmul(t_ps[:, 1, 1, t * P:(t + 1) * P], e_hT[:, t * P:(t + 1) * P],
                                                        e_wT[:, 1, bass.ds(e, 1), :].rearrange("p e c -> p (e c)"),
                                                        start=True, stop=True)
                            last.then_inc(y_ready, 1)
                with pe.Else():
                    pe.nop()
                pe.nop()

            @block.scalar
            def _(act):
                with act.If(act.value_load(flag[0:1, 0:1], min_val=0, max_val=1) > 0):
                    for s in (exT_kept, h_kept, hT_kept):
                        act.sem_inc(s, FREE)
                    for k in range(4):
                        act.wait_ge(ewT_ready, k + 1)
                        nc.scalar.copy(e_wT[:, k // 2, k % 2 * 4:k % 2 * 4 + 4, :].rearrange("p e c -> p (e c)"),
                                       t_ps[:, 0, k % 2, :]).then_inc(ewT_kept, 1)
                    with act.Fori(0, TILES // MT) as g:
                        act.wait_ge(exT_ready, g + 1)
                        act.wait_ge(h_ready, g * E + FREE)
                        nc.scalar.copy(e_xT[:, :], t_ps[:, 0, 0, :]).then_inc(exT_kept, 1)
                        with act.Fori(0, E) as e:
                            act.wait_ge(pre_kept, g * E + (e + (1 + FREE)))
                            act.wait_ge(hT_ready, g * E + e + FREE)
                            nc.scalar.activation(e_h[:, :, :], e_pre[:, :, :], ACT.Silu).then_inc(h_kept, 1)
                            act.wait_ge(hT_ready, g * E + (e + (1 + FREE)))
                            act.wait_ge(y_ready, g * E + e + FREE)
                            nc.scalar.copy(e_hT[:, :], t_ps[:, 1, 0, :]).then_inc(hT_kept, 1)
                with act.Else():
                    act.nop()
                act.nop()

            @block.vector
            def _(dve):
                with dve.If(dve.value_load(flag[0:1, 0:1], min_val=0, max_val=1) > 0):
                    for s in (pre_kept, y_kept, experts_done):
                        dve.sem_inc(s, FREE)
                    nc.vector.tensor_tensor(weight[:, :, :], chosen[0][:, :, :], probs[:, :, :], ALU.mult)\
                        .then_inc(shifted, 1)
                    dve.wait_ge(shifted, 4)
                    nc.vector.tensor_tensor(weight[:, :, :], weight[:, :, :],
                                            keep[:, :].unsqueeze(1).broadcast_to([P, TILES, E]), ALU.mult)\
                        .then_inc(shifted, 1)
                    dve.wait_ge(shifted, 5)
                    dve.wait_ge(e_loaded, 64)
                    with dve.Fori(0, TILES // MT) as g:
                        dve.wait_ge(experts_done, g + FREE)
                        nc.vector.memset(e_acc[:, :, :], 0.0).then_inc(cleared, 1)
                        dve.wait_ge(cleared, g + 1)
                        apart(dve, mem)
                        with dve.Fori(0, E) as e:
                            dve.wait_ge(h_ready, g * E + (e + (1 + FREE)))
                            dve.wait_ge(h_kept, g * E + e + FREE)
                            nc.vector.tensor_tensor(
                                e_pre[:, :, :], t_ps[:, 0, 1, :].rearrange("p (t c) -> p t c", c=C),
                                e_b[:, 0, bass.ds(e, 1), :].broadcast_to([P, MT, C]), ALU.add).then_inc(pre_kept, 1)
                            dve.wait_ge(y_ready, g * E + (e + (1 + FREE)))
                            nc.vector.tensor_tensor(
                                e_y[:, :, :], t_ps[:, 1, 1, :].rearrange("p (t c) -> p t c", c=C),
                                e_b[:, 1, bass.ds(e, 1), :].broadcast_to([P, MT, C]), ALU.add).then_inc(y_kept, 1)
                            dve.wait_ge(y_kept, g * E + (e + (1 + FREE)))
                            for t in range(MT):
                                nc.vector.scalar_tensor_tensor(
                                    out=e_acc[:, t, :], in0=e_y[:, t, :],
                                    scalar=weight[:, bass.ds(g * MT + t, 1), bass.ds(e, 1)].rearrange(
                                        "p t e -> p (t e)"),
                                    in1=e_acc[:, t, :], op0=ALU.mult, op1=ALU.add).then_inc(acc_kept, 1)
                            dve.wait_ge(acc_kept, g * (E * MT) + e * MT + MT)
                        dve.wait_ge(e_x_loaded, g * 16 + 16)
                        nc.vector.tensor_tensor(x_all[:, bass.ds(g * MT, MT), :], x_all[:, bass.ds(g * MT, MT), :],
                                                e_acc[:, :, :], ALU.add).then_inc(experts_done, 1)
                with dve.Else():
                    dve.nop()
                dve.nop()

        with nc.Block() as block:

            @block.gpsimd
            def _(pool):
                def step(st):
                    if st.has(0):
                        pool.wait_ge(var_kept, st.seq(0, c=1))
                        nc.gpsimd.tensor_tensor(rstd[:, st.slot(0), :], var[:, st.slot(0), :],
                                                mem["minus_half"][:, 0:GT], ALU.pow).then_inc(rstd_kept, 1)

                groups(pool, step)

            @block.vector
            def _(dve):
                def measure(st):
                    j = st.slot(0)
                    for t in range(GT):
                        nc.vector.bn_stats(stats[:, j, t, :], x_all[:, bass.ds(st.seq(0, GT, t), 1), :].rearrange(
                            "p t c -> p (t c)")).then_inc(stats_kept, 1)
                    dve.wait_ge(stats_kept, st.seq(0, GT, GT))
                    apart(dve, mem)
                    for t in range(GT):
                        nc.vector.bn_aggr(mv[:, j, t, :], stats[:, j, t, :]).then_inc(mv_kept, 1)
                    dve.wait_ge(mv_kept, st.seq(0, GT, GT))
                    nc.vector.tensor_scalar(var[:, j, :], mv[:, j, :, 1], EPS, None, ALU.add).then_inc(var_kept, 1)

                def normalise(st):
                    j = st.slot(1)
                    dve.wait_ge(rstd_kept, st.seq(1, c=1))
                    for t in range(GT):
                        x = x_all[:, bass.ds(st.seq(1, GT, t), 1), :].rearrange("p t c -> p (t c)")
                        nc.vector.tensor_scalar(x, x, mv[:, j, t, 0:1], rstd[:, j, t:t + 1],
                                                ALU.subtract, ALU.mult).then_inc(ln_kept, 1)

                def step(st):
                    if st.has(0):
                        measure(st)
                    if st.has(1):
                        normalise(st)

                groups(dve, step)



NT = 64
TPC = 8
NC = NT // TPC
COMP = 32
GRID = 16
KNOTS = 8
W1, B1, W2, B2, DIR = 0, 2 * GRID, 3 * GRID, 4 * GRID, 4 * GRID + 1
TABLE = DIR + C
NS = NC + NT
SG = 4
SPLINE_SLOTS = 4
SPLINE_DEPTH = 4


def spline_ffn(nc, mem, w, out_tiles):
    x_all, ident, ident_h = mem["x_all"], mem["ident"], mem["ident_h"]
    with ExitStack() as ctx:
        def sb(label, shape, dt=F32):
            return ctx.enter_context(nc.sbuf_tensor(f"ffn_{label}", shape, dt))

        def sem(label):
            return nc.alloc_semaphore(name=f"ffn_{label}")

        raw = sb("raw", [NT, C])
        rawT = sb("rawT", [P, NT])
        above = sb("above", [P, NT])
        below = sb("below", [P, NT])
        sums = sb("sums", [P, NC])
        sigs = sb("sigs", [P, NS])
        knots = sb("knots", [P, KNOTS])
        rises = sb("rises", [P, KNOTS - 1])
        temp = sb("temp", [P, 1])
        cw1 = sb("cw1", [P, COMP])
        cb1 = sb("cb1", [COMP, 1])
        cw2 = sb("cw2", [COMP, 2])
        cb2 = sb("cb2", [P, 2])
        table = sb("table", [P, TABLE])
        table_rest = sb("table_rest", [P, TABLE])
        table_hm = sb("table_hm", [P, TABLE], BF16)
        table_l = sb("table_l", [P, TABLE], BF16)
        gamma = sb("gamma", [P, C])
        beta = sb("beta", [P, C])
        out_scale = sb("out_scale", [P, 1])
        rank = sb("rank", [P, TPC])
        xs = sb("xs", [P, 2, GT, C])
        xT = sb("xT", [P, 2, GT * P])
        hT = sb("hT", [COMP, 2, GT * P])
        scores = sb("scores", [P, TILES, NS])
        comp = sb("comp", [P, TILES, 2])
        big = sb("big", [P, TILES, NT])
        onehot = sb("onehot", [P, TILES, 2, NT], BF16)
        value, pos, low, val, rise, equal, score, cluster, local = (
            sb(x, [P, TILES, TPC]) for x in ("value", "pos", "low", "val", "rise", "equal", "score", "cluster",
                                            "local"))
        top = sb("top", [P, TILES])
        ohT = sb("ohT", [P, SPLINE_SLOTS, SG * P], BF16)
        rows = sb("rows", [P, SPLINE_SLOTS, SG, TABLE])
        bent = sb("bent", [P, 2, SG, GRID])
        mag = sb("mag", [P, SG])
        y = sb("y", [P, SPLINE_SLOTS, SG, C])
        z = sb("z", [P, SPLINE_SLOTS, SG, C])
        x_beta = sb("x_beta", [P, SG, C])
        stats = sb("stats", [P, 2, SG, 6])
        mv = sb("mv", [P, 2, SPLINE_SLOTS, SG, 2])
        var = sb("var", [P, 2, SG])
        rstd = sb("rstd", [P, 2, SPLINE_SLOTS, SG])
        shift = sb("shift", [P, SPLINE_SLOTS, SG])

        loaded, consts, rawT_ready, chain, tables_kept = (
            sem(x) for x in ("loaded", "consts", "rawT_ready", "chain", "tables_kept"))
        xs_loaded = [sem(f"xs_loaded{j}") for j in range(2)]
        xT_ready, xT_kept, h_ready, h_kept, scores_ready, scores_kept = (
            sem(x) for x in ("xT_ready", "xT_kept", "h_ready", "h_kept", "scores_ready", "scores_kept"))
        pos_ready, exp_kept, comp_ready, comp_kept = (
            sem(x) for x in ("pos_ready", "exp_kept", "comp_ready", "comp_kept"))
        LOADS = 10 + 2 * 5

        with nc.psum_tensor("ffn_t_ps", [P, 2, 2, 512], F32) as t_ps, \
                nc.psum_tensor("ffn_s_ps", [P, 2, 512], F32) as s_ps, \
                nc.psum_tensor("ffn_h_ps", [P, 2, 512], F32) as h_ps, nc.Block() as block:

            COMP_AT = 4 * NS

            @block.sync
            def _(sp):
                def wide(ap, n):
                    return bass.AP(ap.tensor, ap.offset, [[0, P], [1, n]])

                def column(ap):
                    return ap.rearrange("(n one) -> n one", one=1)

                for to, of in ((raw[:, :], w["L1_ffn_signatures_raw"]), (knots[:, :], wide(w["L1_ffn_knot_values"], KNOTS)),
                               (temp[:, :], wide(w["L1_ffn_temperature"], 1)), (cw1[:, :], w["L1_ffn_compress_w1"]),
                               (cb1[:, :], column(w["L1_ffn_compress_b1"])), (cw2[:, :], w["L1_ffn_compress_w2"]),
                               (cb2[:, :], wide(w["L1_ffn_compress_b2"], 2)),
                               (gamma[:, :], wide(w["L1_ffn_norm_gamma"], C)), (beta[:, :], wide(w["L1_ffn_norm_beta"], C)),
                               (out_scale[:, :], wide(w["L1_ffn_output_scale"], 1))):
                    sp.dma_start(to, of).then_inc(loaded, 16)
                for half in range(2):
                    rows_ = slice(half * NT, (half + 1) * NT)
                    for at, of in ((W1, w["L1_ffn_spline_w1"].rearrange("t i g -> t (i g)")), (B1, w["L1_ffn_spline_b1"]),
                                   (W2, w["L1_ffn_spline_w2"].rearrange("t g one -> t (g one)")),
                                   (B2, w["L1_ffn_spline_b2"]), (DIR, w["L1_ffn_directions"])):
                        sp.dma_start(table[rows_, at:at + of.shape[1]], of).then_inc(loaded, 16)

                def step(st):
                    if st.has(0):
                        j = st.slot(0)
                        wait(sp, xT_ready, st.seq(1))
                        sp.dma_start(xs[:, j, :, :], x_all[:, bass.ds(st.seq(0, GT), GT), :])\
                            .then_inc(xs_loaded[j], 16)

                groups(sp, step)

            @block.gpsimd
            def _(pool):
                for e in range(TPC):
                    nc.gpsimd.memset(rank[:, e:e + 1], float(TPC - e)).then_inc(consts, 1)
                pool.wait_ge(consts, TPC)
                nc.gpsimd.memset(table_l[NT:P, :], 0.0).then_inc(consts, 1)

            @block.tensor
            def _(pe):
                pe.wait_ge(loaded, 16 * LOADS)
                nc.tensor.transpose(h_ps[:, 0, 0:NT], raw[:, :], ident[0:NT, 0:NT]).then_inc(rawT_ready, 1)

                def transposes(st):
                    j = st.slot(0)
                    pe.wait_ge(xs_loaded[j], st.turn(0))
                    wait(pe, xT_kept, st.seq(1, 2))
                    for t in range(GT):
                        last = nc.tensor.transpose(t_ps[:, j, t // 4, t % 4 * P:(t % 4 + 1) * P], xs[:, j, t, :],
                                                   ident[:, :])
                    last.then_inc(xT_ready, 1)

                def products(st):
                    j = st.slot(1)
                    pe.wait_ge(xT_kept, st.seq(1, 2, 2))
                    wait(pe, h_kept, st.seq(1))
                    for b in range(2):
                        last = nc.tensor.matmul(h_ps[0:COMP, b, :], cw1[:, :], xT[:, j, b * 512:(b + 1) * 512],
                                                start=True, stop=True)
                    last.then_inc(h_ready, 1)
                    wait(pe, scores_kept, st.seq(1, 2))
                    for t in range(GT):
                        nc.tensor.matmul(s_ps[:, t // 4, t % 4 * NS:(t % 4 + 1) * NS], xT[:, j, t * P:(t + 1) * P],
                                         sigs[:, :], start=True, stop=True)
                    pe.wait_ge(h_kept, st.seq(1, c=1))
                    for t in range(GT):
                        at = COMP_AT + 2 * (t % 4)
                        last = nc.tensor.matmul(s_ps[:, t // 4, at:at + 2], hT[:, j, t * P:(t + 1) * P], cw2[:, :],
                                                start=True, stop=True)
                    last.then_inc(scores_ready, 1)

                def step(st):
                    if st.has(0):
                        transposes(st)
                    if st.has(1):
                        products(st)

                pe.wait_ge(tables_kept, 1)
                groups(pe, step)

            @block.scalar
            def _(act):
                def step(st):
                    if st.has(0):
                        j = st.slot(0)
                        act.wait_ge(xT_ready, st.seq(0, c=1))
                        wait(act, scores_ready, st.seq(1))
                        for b in range(2):
                            nc.scalar.copy(xT[:, j, b * 512:(b + 1) * 512], t_ps[:, j, b, :]).then_inc(xT_kept, 1)
                    if st.has(1):
                        act.wait_ge(h_ready, st.seq(1, c=1))
                        nc.scalar.activation(hT[:, st.slot(1), :], h_ps[0:COMP, :, :].rearrange("p b n -> p (b n)"),
                                             ACT.Gelu, bias=cb1[:, :]).then_inc(h_kept, 1)

                groups(act, step)
                act.wait_ge(comp_ready, 1)
                nc.scalar.activation(comp[:, :, :], comp[:, :, :], ACT.Tanh).then_inc(comp_kept, 1)
                for k in range(2):
                    act.wait_ge(pos_ready, k + 1)
                    nc.scalar.activation(pos[:, :, :], value[:, :, :], ACT.Exp).then_inc(exp_kept, 1)

            @block.vector
            def _(dve):
                done = [0]

                def then(ins):
                    ins.then_inc(chain, 1)
                    done[0] += 1
                    dve.wait_ge(chain, done[0])

                dve.wait_ge(rawT_ready, 1)
                dve.wait_ge(consts, TPC + 1)
                then(nc.vector.tensor_copy(rawT[:, :], h_ps[:, 0, 0:NT]))
                then(nc.vector.tensor_scalar(above[:, :], rawT[:, :], 0.3, None, ALU.is_gt))
                then(nc.vector.tensor_scalar(below[:, :], rawT[:, :], -0.3, None, ALU.is_lt))
                then(nc.vector.tensor_tensor(above[:, :], above[:, :], below[:, :], ALU.subtract))
                then(nc.vector.tensor_tensor(above[:, :], above[:, :], rawT[:, :], ALU.subtract))
                then(nc.vector.tensor_tensor(sigs[:, NC:NS], rawT[:, :], above[:, :], ALU.add))
                by_tile = sigs[:, NC:NS].rearrange("p (c t) -> p t c", t=TPC)
                then(nc.vector.tensor_tensor(sums[:, :], by_tile[:, 0, :], by_tile[:, 1, :], ALU.add))
                for t in range(2, TPC):
                    then(nc.vector.tensor_tensor(sums[:, :], sums[:, :], by_tile[:, t, :], ALU.add))
                then(nc.vector.tensor_scalar(above[:, 0:NC], sums[:, :], 0.0, None, ALU.is_gt))
                then(nc.vector.tensor_scalar(below[:, 0:NC], sums[:, :], 0.0, None, ALU.is_lt))
                nc.vector.tensor_tensor(sigs[:, 0:NC], above[:, 0:NC], below[:, 0:NC], ALU.subtract)\
                    .then_inc(tables_kept, 1)
                then(nc.vector.tensor_tensor(rises[:, :], knots[:, 1:KNOTS], knots[:, 0:KNOTS - 1], ALU.subtract))
                then(nc.vector.tensor_scalar(temp[:, :], temp[:, :], 1e-6, None, ALU.add))
                then(nc.vector.reciprocal(temp[:, :], temp[:, :]))
                then(nc.vector.tensor_scalar(temp[:, :], temp[:, :], -1.0, None, ALU.mult))
                then(nc.vector.tensor_copy(table_hm[:, :], table[:, :]))
                then(nc.vector.tensor_tensor(table_rest[:, :], table[:, :], table_hm[:, :], ALU.subtract))
                then(nc.vector.tensor_copy(table_hm[NT:P, :], table_rest[NT:P, :]))
                then(nc.vector.tensor_copy(table_l[0:NT, :], table_rest[0:NT, :]))
                then(nc.vector.tensor_tensor(table_rest[0:NT, :], table_rest[0:NT, :], table_l[0:NT, :], ALU.subtract))
                then(nc.vector.tensor_copy(table_l[0:NT, :], table_rest[0:NT, :]))

                def step(st):
                    if st.has(0):
                        dve.wait_ge(scores_ready, st.seq(0, c=1))
                        first = st.seq(0, GT)
                        nc.vector.tensor_copy(scores[:, bass.ds(first, GT), :].rearrange("p (b t) n -> p b (t n)", b=2),
                                              s_ps[:, :, 0:COMP_AT]).then_inc(scores_kept, 1)
                        nc.vector.tensor_copy(comp[:, bass.ds(first, GT), :].rearrange("p (b t) n -> p b (t n)", b=2),
                                              s_ps[:, :, COMP_AT:COMP_AT + 8]).then_inc(scores_kept, 1)

                groups(dve, step)
                dve.wait_ge(scores_kept, 2 * GROUPS)
                nc.vector.tensor_tensor(comp[:, :, :], comp[:, :, :], cb2[:, :].unsqueeze(1).broadcast_to([P, TILES, 2]),
                                        ALU.add).then_inc(comp_ready, 1)

                def over(ap):
                    return ap.unsqueeze(2).broadcast_to([P, TILES, TPC])

                def calibrate(of, k):
                    nc.vector.tensor_scalar(value[:, :, :], of, temp[:, :], 88.0, ALU.mult, ALU.min)\
                        .then_inc(pos_ready, 1)
                    dve.wait_ge(exp_kept, k + 1)
                    then(nc.vector.tensor_scalar(pos[:, :, :], pos[:, :, :], 1.0, None, ALU.add))
                    then(nc.vector.reciprocal(pos[:, :, :], pos[:, :, :]))
                    then(nc.vector.tensor_scalar(pos[:, :, :], pos[:, :, :], float(KNOTS - 1), None, ALU.mult))
                    then(nc.vector.tensor_scalar(low[:, :, :], pos[:, :, :], 1.0, None, ALU.is_ge))
                    for n in range(2, KNOTS - 1):
                        then(nc.vector.scalar_tensor_tensor(out=low[:, :, :], in0=pos[:, :, :], scalar=float(n),
                                                            in1=low[:, :, :], op0=ALU.is_ge, op1=ALU.add))
                    then(nc.vector.tensor_tensor(pos[:, :, :], pos[:, :, :], low[:, :, :], ALU.subtract))
                    for n in range(KNOTS - 1):
                        then(nc.vector.tensor_scalar(equal[:, :, :], low[:, :, :], float(n), None, ALU.is_equal))
                        for to, by in ((val, knots), (rise, rises)):
                            if n == 0:
                                then(nc.vector.tensor_scalar(to[:, :, :], equal[:, :, :], by[:, 0:1], None, ALU.mult))
                            else:
                                then(nc.vector.scalar_tensor_tensor(
                                    out=to[:, :, :], in0=equal[:, :, :], scalar=by[:, n:n + 1], in1=to[:, :, :],
                                    op0=ALU.mult, op1=ALU.add))
                    then(nc.vector.tensor_tensor(rise[:, :, :], rise[:, :, :], pos[:, :, :], ALU.mult))
                    then(nc.vector.tensor_tensor(val[:, :, :], val[:, :, :], rise[:, :, :], ALU.add))

                def first_best(to):
                    then(nc.vector.tensor_reduce(top[:, :], val[:, :, :], AX_X, ALU.max))
                    then(nc.vector.tensor_tensor(equal[:, :, :], val[:, :, :], over(top[:, :]), ALU.is_equal))
                    then(nc.vector.tensor_tensor(score[:, :, :], equal[:, :, :],
                                                 rank[:, :].unsqueeze(1).broadcast_to([P, TILES, TPC]), ALU.mult))
                    then(nc.vector.tensor_reduce(top[:, :], score[:, :, :], AX_X, ALU.max))
                    then(nc.vector.tensor_tensor(to[:, :, :], score[:, :, :], over(top[:, :]), ALU.is_equal))

                calibrate(scores[:, :, 0:NC], 0)
                first_best(cluster)
                of_cluster = cluster[:, :, :].unsqueeze(3).broadcast_to([P, TILES, NC, TPC])
                then(nc.vector.tensor_tensor(big[:, :, :].rearrange("p n (c t) -> p n c t", c=NC),
                                             scores[:, :, NC:NS].rearrange("p n (c t) -> p n c t", c=NC),
                                             of_cluster, ALU.mult))
                then(nc.vector.tensor_reduce(score[:, :, :], big[:, :, :].rearrange("p n (c t) -> p n t c", c=NC),
                                             AX_X, ALU.add))
                calibrate(score[:, :, :], 1)
                first_best(local)
                for k in range(2):
                    then(nc.vector.tensor_tensor(onehot[:, :, k, :].rearrange("p n (c t) -> p n c t", c=NC), of_cluster,
                                                 local[:, :, :].unsqueeze(2).broadcast_to([P, TILES, NC, TPC]),
                                                 ALU.mult))

        ohT_ready, ohT_kept, rows_ready, rows_kept = (
            sem(x) for x in ("ohT_ready", "ohT_kept", "rows_ready", "rows_kept"))
        terms, bent_sum, hidden, mag_kept, y_kept = (
            sem(x) for x in ("terms", "bent_sum", "hidden", "mag_kept", "y_kept"))
        stats_kept, mv_kept, var_kept, rstd_kept = (
            [sem(f"{x}{k}") for k in range(2)] for x in ("stats_kept", "mv_kept", "var_kept", "rstd_kept"))
        norm_kept, x_beta_kept, scaled, z_kept, shift_kept, o_kept = (
            sem(x) for x in ("norm_kept", "x_beta_kept", "scaled", "z_kept", "shift_kept", "o_kept"))
        stored = sem("stored")
        SPLINE_GROUPS = TILES // SG

        def steps(eng, step):
            pipeline(eng, step, SPLINE_SLOTS, SPLINE_DEPTH, SPLINE_GROUPS, 0)

        with nc.psum_tensor("ffn_o_ps", [P, 2, 512], F32) as o_ps, \
                nc.psum_tensor("ffn_r_ps", [P, 2, 2, 512], F32) as r_ps, nc.Block() as block:

            @block.sync
            def _(sp):
                def step(st):
                    if st.has(3):
                        sp.wait_ge(o_kept, st.seq(3, SG, SG))
                        tiles = bass.ds(st.seq(3, SG), SG)
                        sp.dma_start(out_tiles[:, tiles, :], x_all[:, tiles, :]).then_inc(stored, 16)

                steps(sp, step)
                sp.wait_ge(stored, 16 * SPLINE_GROUPS)

            @block.tensor
            def _(pe):
                def step(st):
                    if st.has(0):
                        b = st.slot(0) % 2
                        wait(pe, ohT_kept, st.seq(2, c=1))
                        for t in range(SG):
                            last = nc.tensor.transpose(
                                o_ps[:, b, t * P // 2:(t + 1) * P // 2].bitcast(BF16),
                                onehot[:, bass.ds(st.seq(0, SG, t), 1), :, :].rearrange("p n k t -> p (n k t)"),
                                ident_h[:, :])
                        last.then_inc(ohT_ready, 1)
                        pe.wait_ge(ohT_kept, st.seq(0, c=1))
                        wait(pe, rows_kept, st.seq(2, 2, 2))
                        for t in range(SG):
                            to = r_ps[:, b, t // 2, t % 2 * TABLE:(t % 2 + 1) * TABLE]
                            one = ohT[:, st.slot(0), t * P:(t + 1) * P]
                            nc.tensor.matmul(to, one, table_hm[:, :], start=True, stop=False)
                            last = nc.tensor.matmul(to, one, table_l[:, :], start=False, stop=True)
                        last.then_inc(rows_ready, 1)

                steps(pe, step)

            @block.scalar
            def _(act):
                def step(st):
                    if st.has(0):
                        sl = st.slot(0)
                        act.wait_ge(ohT_ready, st.seq(0, c=1))
                        nc.scalar.copy(ohT[:, sl, :], o_ps[:, sl % 2, 0:SG * P // 2].bitcast(BF16)).then_inc(ohT_kept, 1)
                        act.wait_ge(rows_ready, st.seq(0, c=1))
                        wait(act, y_kept, st.seq(SPLINE_SLOTS, SG, SG))
                        for b in range(2):
                            nc.scalar.copy(rows[:, sl, 2 * b:2 * b + 2, :].rearrange("p t n -> p (t n)"),
                                           r_ps[:, sl % 2, b, 0:2 * TABLE]).then_inc(rows_kept, 1)
                    if st.has(3):
                        sl = st.slot(3)
                        act.wait_ge(shift_kept, st.seq(3, c=1))
                        for t in range(SG):
                            x = x_all[:, bass.ds(st.seq(3, SG, t), 1), :].rearrange("p t c -> p (t c)")
                            nc.scalar.activation(x, z[:, sl, t, :], ACT.Identity, bias=shift[:, sl, t:t + 1],
                                                 scale=rstd[:, 1, sl, t:t + 1]).then_inc(o_kept, 1)

                steps(act, step)

            @block.gpsimd
            def _(pool):
                def root(st, lag, k):
                    pool.wait_ge(var_kept[k], st.seq(lag, c=1))
                    nc.gpsimd.tensor_tensor(rstd[:, k, st.slot(lag), :], var[:, k, :], mem["minus_half"][:, 0:SG],
                                            ALU.pow).then_inc(rstd_kept[k], 1)

                def step(st):
                    if st.has(1):
                        root(st, 1, 0)
                    if st.has(2):
                        sl = st.slot(2)
                        wait(pool, z_kept, st.seq(2))
                        nc.gpsimd.tensor_tensor(x_beta[:, :, :], x_all[:, bass.ds(st.seq(2, SG), SG), :],
                                                beta[:, :].unsqueeze(1).broadcast_to([P, SG, C]), ALU.add)\
                            .then_inc(x_beta_kept, 1)
                        pool.wait_ge(norm_kept, st.seq(2, SG, SG))
                        nc.gpsimd.tensor_tensor(z[:, sl, :, :], z[:, sl, :, :],
                                                gamma[:, :].unsqueeze(1).broadcast_to([P, SG, C]), ALU.mult)\
                            .then_inc(scaled, 1)
                        pool.wait_ge(scaled, st.seq(2, c=1))
                        pool.wait_ge(x_beta_kept, st.seq(2, c=1))
                        nc.gpsimd.tensor_tensor(z[:, sl, :, :], z[:, sl, :, :], x_beta[:, :, :], ALU.add)\
                            .then_inc(z_kept, 1)
                    if st.has(3):
                        root(st, 3, 1)

                steps(pool, step)

            @block.vector
            def _(dve):
                def measure(st, lag, k, of):
                    for t in range(SG):
                        nc.vector.bn_stats(stats[:, k, t, :], of[:, st.slot(lag), t, :]).then_inc(stats_kept[k], 1)
                    dve.wait_ge(stats_kept[k], st.seq(lag, SG, SG))
                    apart(dve, mem)
                    for t in range(SG):
                        nc.vector.bn_aggr(mv[:, k, st.slot(lag), t, :], stats[:, k, t, :]).then_inc(mv_kept[k], 1)
                    dve.wait_ge(mv_kept[k], st.seq(lag, SG, SG))
                    wait(dve, rstd_kept[k], st.seq(lag))
                    nc.vector.tensor_scalar(var[:, k, :], mv[:, k, st.slot(lag), :, 1], EPS, None, ALU.add)\
                        .then_inc(var_kept[k], 1)

                def bend(st):
                    sl = st.slot(1)
                    dve.wait_ge(rows_kept, st.seq(1, 2, 2))
                    for k in range(2):
                        nc.vector.tensor_tensor(bent[:, k, :, :], rows[:, sl, :, W1 + k * GRID:W1 + (k + 1) * GRID],
                                                comp[:, bass.ds(st.seq(1, SG), SG), k:k + 1].broadcast_to([P, SG, GRID]),
                                                ALU.mult).then_inc(terms, 1)
                    dve.wait_ge(terms, st.seq(1, 2, 2))
                    nc.vector.tensor_tensor(bent[:, 0, :, :], bent[:, 0, :, :], bent[:, 1, :, :], ALU.add)\
                        .then_inc(bent_sum, 1)
                    dve.wait_ge(bent_sum, st.seq(1, 2, 1))
                    nc.vector.tensor_tensor(bent[:, 0, :, :], bent[:, 0, :, :], rows[:, sl, :, B1:B1 + GRID], ALU.add)\
                        .then_inc(bent_sum, 1)
                    dve.wait_ge(bent_sum, st.seq(1, 2, 2))
                    nc.vector.scalar_tensor_tensor(out=bent[:, 1, :, :], in0=bent[:, 0, :, :], scalar=0.0,
                                                   in1=rows[:, sl, :, W2:W2 + GRID], op0=ALU.max, op1=ALU.mult)\
                        .then_inc(hidden, 1)
                    dve.wait_ge(hidden, st.seq(1, c=1))
                    nc.vector.tensor_reduce(mag[:, :], bent[:, 1, :, :], AX_X, ALU.add).then_inc(mag_kept, 1)
                    dve.wait_ge(mag_kept, st.seq(1, 3, 1))
                    nc.vector.tensor_tensor(mag[:, :], mag[:, :], rows[:, sl, :, B2], ALU.add).then_inc(mag_kept, 1)
                    dve.wait_ge(mag_kept, st.seq(1, 3, 2))
                    nc.vector.tensor_scalar(mag[:, :], mag[:, :], out_scale[:, :], None, ALU.mult).then_inc(mag_kept, 1)
                    dve.wait_ge(mag_kept, st.seq(1, 3, 3))
                    for t in range(SG):
                        nc.vector.scalar_tensor_tensor(
                            out=y[:, sl, t, :], in0=rows[:, sl, t, DIR:TABLE], scalar=mag[:, t:t + 1],
                            in1=x_all[:, bass.ds(st.seq(1, SG, t), 1), :].rearrange("p t c -> p (t c)"),
                            op0=ALU.mult, op1=ALU.add).then_inc(y_kept, 1)
                    dve.wait_ge(y_kept, st.seq(1, SG, SG))

                def normalise(st):
                    sl = st.slot(2)
                    dve.wait_ge(rstd_kept[0], st.seq(2, c=1))
                    wait(dve, o_kept, st.seq(SPLINE_DEPTH, SG, SG))
                    for t in range(SG):
                        nc.vector.tensor_scalar(z[:, sl, t, :], y[:, sl, t, :], mv[:, 0, sl, t, 0:1],
                                                rstd[:, 0, sl, t:t + 1], ALU.subtract, ALU.mult).then_inc(norm_kept, 1)

                def measure_z(st):
                    dve.wait_ge(z_kept, st.seq(3, c=1))
                    measure(st, 3, 1, z)

                def shifts(st):
                    sl = st.slot(3)
                    dve.wait_ge(rstd_kept[1], st.seq(3, c=1))
                    nc.vector.scalar_tensor_tensor(out=shift[:, sl, :], in0=mv[:, 1, sl, :, 0], scalar=-1.0,
                                                   in1=rstd[:, 1, sl, :], op0=ALU.mult, op1=ALU.mult)\
                        .then_inc(shift_kept, 1)

                def step(st):
                    if st.has(3):
                        measure_z(st)
                    if st.has(2):
                        normalise(st)
                    if st.has(1):
                        bend(st)
                        measure(st, 1, 0, y)
                    if st.has(3):
                        shifts(st)

                steps(dve, step)



def prepare(nc, mem, w):
    with ExitStack() as ctx:
        def sb(label, shape, dt=F32):
            return ctx.enter_context(nc.sbuf_tensor(f"prep_{label}", shape, dt))

        def sem(label):
            return nc.alloc_semaphore(name=f"prep_{label}")

        w_raw = [sb(f"w_raw{n}", [P, 3, C]) for n in range(2)]
        a_T = sb("a_T", [R, 2, D])
        b_r = sb("b_r", [R, 2, D])
        a_rep = sb("a_rep", [R, 2, H, D])
        b_rep = sb("b_rep", [R, 2, H, D])
        b_col = sb("b_col", [P, 2])
        bv_wide = sb("bv_wide", [P, P])
        diagonal = sb("diagonal", [P, P])
        lora = sb("lora", [P, 2, P])
        lora_diag = sb("lora_diag", [P, 2, P])
        g_q = sb("g_q", [P, P])
        g_v = sb("g_v", [P, P])
        wT = sb("wT", [P, 2, P])
        ps = ctx.enter_context(nc.psum_tensor("prep_ps", [P, 4, 512], F32))

        loaded, consts, zeroed, masked = sem("loaded"), sem("consts"), sem("zeroed"), sem("masked")
        repeated, lora_ready, lora_kept, diag_kept, folded = (
            sem(x) for x in ("repeated", "lora_ready", "lora_kept", "diag_kept", "folded"))
        wT_ready, wT_kept, new_ready, new_kept = (sem(x) for x in ("wT_ready", "wT_kept", "new_ready", "new_kept"))
        ALL = 1 + 4 + 2 + D + 6
        block = ctx.enter_context(nc.Block())

        @block.sync
        def _(sp):
            sp.dma_start(w_raw[0][:, :, :], w["L0_attn_w_qkv"].rearrange("c (s f) -> c s f", s=3)).then_inc(loaded, 16)
            for s, k in enumerate(("q", "v")):
                sp.dma_start(a_T[:, s, :], w[f"L0_attn_a_{k}"].rearrange("d r -> r d"),
                             allow_slow_non_contiguous=True).then_inc(loaded, 16)
                sp.dma_start(b_r[:, s, :], w[f"L0_attn_b_{k}"]).then_inc(loaded, 16)
            bias = w["L0_attn_b_qkv"].rearrange("(s f one) -> s f one", s=3, one=1)
            sp.dma_start(b_col[:, 0:1], bias[0]).then_inc(loaded, 16)
            sp.dma_start(b_col[:, 1:2], bias[2]).then_inc(loaded, 16)
            perm = w["L0_attn_b_qkv"].rearrange("(s h d one) -> s d h one", s=3, d=D, one=1)
            for d in range(D):
                sp.dma_start(mem["bqk0"][H * d:H * (d + 1), 1:2], perm[1, d],
                             allow_slow_non_contiguous=True).then_inc(loaded, 16)
            sp.dma_start(mem["wo0"][:, :], w["L0_attn_w_proj"]).then_inc(loaded, 16)
            bo = w["L0_attn_b_proj"]
            sp.dma_start(mem["bo0"][:, :], bass.AP(bo.tensor, bo.offset, [[0, P], [1, C]])).then_inc(loaded, 16)
            sp.dma_start(w_raw[1][:, :, :], w["L1_attn_w_qkv"].rearrange("c (s f) -> c s f", s=3)).then_inc(loaded, 16)
            for k in ("cos", "sin"):
                sp.dma_start(mem[k][:, :], w[k]).then_inc(loaded, 16)
            sp.dma_start(mem["wo1"][:, :], w["L1_attn_w_proj"]).then_inc(loaded, 16)
            sp.wait_ge(loaded, 16 * ALL)



        @block.gpsimd
        def _(pool):
            for t in (mem["ident"], mem["ident_h"], mem["mask_qk"], mem["mask_kq"]):
                nc.gpsimd.memset(t[:], 0.0).then_inc(zeroed, 1)
            nc.gpsimd.memset(diagonal[:, :], 1.0).then_inc(zeroed, 1)
            nc.gpsimd.memset(mem["minus_half"][:, :], -0.5).then_inc(consts, 1)
            pool.wait_ge(zeroed, 5)
            for t in (mem["ident"], mem["ident_h"]):
                nc.gpsimd.affine_select(out=t[:, :], in_=t[:, :], compare_op=ALU.not_equal, fill=1.0, base=0,
                                        pattern=[[-1, P]], channel_multiplier=1).then_inc(consts, 1)
            nc.gpsimd.affine_select(out=mem["mask_qk"][:], in_=mem["mask_qk"][:], compare_op=ALU.is_ge, fill=MASKED,
                                    base=0, pattern=[[0, 2], [-1, P]], channel_multiplier=1).then_inc(consts, 1)
            nc.gpsimd.affine_select(out=mem["mask_kq"][:], in_=mem["mask_kq"][:], compare_op=ALU.is_ge, fill=MASKED,
                                    base=0, pattern=[[0, 2], [1, P]], channel_multiplier=-1).then_inc(consts, 1)
            nc.gpsimd.affine_select(out=diagonal[:, :], in_=diagonal[:, :], compare_op=ALU.is_ge, fill=0.0,
                                    base=0, pattern=[[-D, H], [0, D]], channel_multiplier=1).then_inc(masked, 1)
            pool.wait_ge(masked, 1)
            nc.gpsimd.affine_select(out=diagonal[:, :], in_=diagonal[:, :], compare_op=ALU.is_ge, fill=0.0,
                                    base=D - 1, pattern=[[D, H], [0, D]], channel_multiplier=-1).then_inc(consts, 1)

        @block.vector
        def _(dve):
            dve.wait_ge(loaded, 16 * ALL)
            for s in range(2):
                nc.vector.tensor_copy(a_rep[:, s, :, :], a_T[:, s, :].unsqueeze(1).broadcast_to([R, H, D]))\
                    .then_inc(repeated, 1)
                nc.vector.tensor_copy(b_rep[:, s, :, :], b_r[:, s, :].unsqueeze(1).broadcast_to([R, H, D]))\
                    .then_inc(repeated, 1)
            nc.vector.tensor_copy(bv_wide[:, :], b_col[:, 1:2].broadcast_to([P, P])).then_inc(repeated, 1)
            heads_last = "p (h d) -> p d h"
            for to, of in ((mem["wqk0"][:, 1, :], w_raw[0][:, 1, :]), (mem["wqk1"][:, 0, :], w_raw[1][:, 0, :]),
                           (mem["wqk1"][:, 1, :], w_raw[1][:, 1, :])):
                nc.vector.tensor_copy(to.rearrange("p (d h) -> p d h", d=D), of.rearrange(heads_last, d=D))\
                    .then_inc(repeated, 1)
            nc.vector.tensor_copy(mem["wv1"][:, :], w_raw[1][:, 2, :]).then_inc(repeated, 1)
            dve.wait_ge(consts, 6)
            dve.wait_ge(lora_ready, 1)
            for s in range(2):
                nc.vector.scalar_tensor_tensor(out=lora[:, s, :], in0=ps[:, s, 0:P], scalar=LORA_SCALE,
                                               in1=diagonal[:, :], op0=ALU.mult, op1=ALU.mult).then_inc(lora_kept, 1)
            dve.wait_ge(lora_kept, 2)
            nc.vector.tensor_tensor(g_q[:, :].rearrange("p (d h) -> p d h", d=D),
                                    lora[:, 0, :].rearrange(heads_last, d=D),
                                    mem["ident"][:, :].rearrange(heads_last, d=D), ALU.add).then_inc(folded, 1)
            nc.vector.tensor_tensor(g_v[:, :], lora[:, 1, :], mem["ident"][:, :], ALU.add).then_inc(folded, 1)
            dve.wait_ge(wT_ready, 1)
            for s in range(2):
                nc.vector.tensor_copy(wT[:, s, :], ps[:, 2, s * P:(s + 1) * P]).then_inc(wT_kept, 1)
            dve.wait_ge(new_ready, 1)
            for to, of in ((mem["wqk0"][:, 0, :], ps[:, 3, 0:P]), (mem["wv0"][:, :], ps[:, 3, P:2 * P]),
                           (mem["bv0"][:, :], ps[:, 3, 2 * P:3 * P]), (mem["bqk0"][:, 0:1], ps[:, 3, 3 * P:3 * P + 1])):
                nc.vector.tensor_copy(to, of).then_inc(new_kept, 1)

        @block.tensor
        def _(pe):
            pe.wait_ge(repeated, 9)
            for s in range(2):
                last = nc.tensor.matmul(ps[:, s, 0:P], a_rep[:, s, :, :].rearrange("r h d -> r (h d)"),
                                        b_rep[:, s, :, :].rearrange("r h d -> r (h d)"), start=True, stop=True)
            last.then_inc(lora_ready, 1)
            pe.wait_ge(consts, 6)
            for s, of in enumerate((0, 2)):
                last = nc.tensor.transpose(ps[:, 2, s * P:(s + 1) * P], w_raw[0][:, of, :], mem["ident"][:, :])
            last.then_inc(wT_ready, 1)
            pe.wait_ge(folded, 2)
            pe.wait_ge(wT_kept, 2)
            nc.tensor.matmul(ps[:, 3, 0:P], wT[:, 0, :], g_q[:, :], start=True, stop=True)
            nc.tensor.matmul(ps[:, 3, P:2 * P], wT[:, 1, :], g_v[:, :], start=True, stop=True)
            nc.tensor.matmul(ps[:, 3, 2 * P:3 * P], bv_wide[:, :], g_v[:, :], start=True, stop=True)
            nc.tensor.matmul(ps[:, 3, 3 * P:3 * P + 1], g_q[:, :], b_col[:, 0:1], start=True, stop=True)\
                .then_inc(new_ready, 1)

        @block.scalar
        def _(act):
            for g in range(8):
                n = TILES // 8
                act.dma_start(mem["x_all"][:, g * n:(g + 1) * n, :], w["x_tiles"][:, g * n:(g + 1) * n, :])\
                    .then_inc(mem["x_all_loaded"], 16)


def build(nc, w, out):
    with ExitStack() as ctx:
        def sb(label, shape, dt=F32):
            return ctx.enter_context(nc.sbuf_tensor(label, shape, dt))

        mem = {"x_all": sb("x_all", [P, TILES, C]), "ident": sb("ident", [P, P]), "ident_h": sb("ident_h", [P, P], BF16),
               "mask_qk": sb("mask_qk", [P, 2, P], BF16), "mask_kq": sb("mask_kq", [P, 2, P], BF16),
               "cos": sb("cos", [P, N]), "sin": sb("sin", [P, N]),
               "minus_half": sb("minus_half", [P, TILES])}
        for n in range(2):
            mem |= {f"wqk{n}": sb(f"wqk{n}", [P, 2, P]), f"wv{n}": sb(f"wv{n}", [P, C]), f"wo{n}": sb(f"wo{n}", [P, C])}
        mem |= {"bqk0": sb("bqk0", [P, 2]), "bv0": sb("bv0", [P, C]), "bo0": sb("bo0", [P, C])}
        mem["apart"] = ctx.enter_context(nc.semaphore("apart"))
        mem["x_all_loaded"] = ctx.enter_context(nc.semaphore("x_all_loaded"))
        w = dict(w, x_tiles=w["L0_attn_x"].rearrange("b (t p) c -> p (b t) c", p=P))
        prepare(nc, mem, w)

        def layer(n):
            return mem | {k: mem.get(f"{k}{n}") for k in ("wqk", "wv", "wo", "bqk", "bv", "bo")}

        out_tiles = out.rearrange("b (t p) c -> p (b t) c", p=P)
        snap = nc.snapshot_sems()
        attention(nc, "attn0", layer(0), False, w["x_tiles"], True, False)
        nc.clear_and_free_semaphores(nc.allocated_since(snap))
        nc.all_engine_barrier()
        moe(nc, mem, w)
        attention(nc, "attn1", layer(1), True, None, False, True)
        spline_ffn(nc, mem, w, out_tiles)


def rotary_tables():
    half = D // 2
    theta = (1.0 / 10000.0 ** (np.arange(half, dtype=np.float32) / np.float32(half))).astype(np.float32)
    freqs = np.arange(N, dtype=np.float32)[:, None] * theta[None, :]
    cos, sin = (np.repeat(np.repeat(f(freqs).astype(np.float32), 2, axis=1).T, H, axis=0) for f in (np.cos, np.sin))
    sin[:P // 2] *= -1
    return np.ascontiguousarray(cos), np.ascontiguousarray(sin)



def kernel(**inputs):
    import concourse.bacc as _bacc
    from concourse import mybir as _mybir
    from concourse.bass_utils import run_bass_kernel_spmd as _run

    nc = _bacc.Bacc("TRN2", target_bir_lowering=False, num_devices=1)
    inputs = {k: np.ascontiguousarray(v) for k, v in inputs.items()}
    inputs["cos"], inputs["sin"] = rotary_tables()
    arrays = {f"in_{k}_dram": v for k, v in inputs.items()}
    w = {k: nc.dram_tensor(f"in_{k}_dram", v.shape, _mybir.dt.from_np(v.dtype), kind="ExternalInput").ap()
         for k, v in inputs.items()}
    out = nc.dram_tensor("out_0_dram", (B, N, C), _mybir.dt.float32, kind="ExternalOutput").ap()
    build(nc, w, out)
    r = _run(nc, [arrays], core_ids=[0])
    return r.results[0]["out_0_dram"]
```

```python
from contextlib import ExitStack

import concourse.bass as bass
import numpy as np
from concourse import mybir

F32 = mybir.dt.float32
BF16 = mybir.dt.bfloat16
I32 = mybir.dt.int32
ALU = mybir.AluOpType
ACT = mybir.ActivationFunctionType
AX_X = mybir.AxisListType.X

P = 128
B, N, C = 32, 256, 128
H, D = 16, 8
R = 16
TILES = B * N // P
TB = N // P
LORA_SCALE = 32.0 / R
EPS = 1e-5
MASKED = -1e30

PARTS = 3
KROWS = PARTS * PARTS * D
MROWS = 2
NH = H // 2
SLOTS = 3
AT = {"attn0": dict(act_xT=0, act_mT1=1, act_qk=2, act_oT=3, act_onT=10, act_mT0=10,
                    dve_o=6, dve_split0=8, dve_v=7, dve_y=13, dve_var=14, dve_ln=15,
                    pe_xT=0, pe_mT1=2, pe_pv3=3, pe_qk=2, pe_oT=6, pe_pv=6, pe_v=5, pe_onT=8, pe_mT0=10, pe_y=13),
      "attn1": dict(act_xT=0, act_mT1=1, act_qk=2, act_oT=3, act_onT=10, act_mT0=10,
                    dve_o=5, dve_split0=8, dve_v=7, dve_y=12, dve_var=15, dve_ln=15,
                    pe_xT=0, pe_mT1=1, pe_pv3=2, pe_qk=1, pe_oT=4, pe_pv=6, pe_v=4, pe_onT=8, pe_mT0=11, pe_y=12)}
DEPTH = 5


def strided(ap, dims):
    return bass.AP(ap.tensor, ap.offset, [list(ap.ap[0])] + dims)


class Step:

    def __init__(self, i, off, slots, total):
        self.i, self.off, self.slots, self.total, self.loop = i, off, slots, total, not isinstance(i, int)

    def has(self, lag):
        return self.loop or 0 <= self.off - lag < self.total

    def seq(self, lag, k=1, c=0):
        return self.i * (self.slots * k) + (k * (self.off - lag) + c)

    def slot(self, lag):
        return (self.off - lag) % self.slots

    def turn(self, lag, k=16, c=0):
        return self.i * k + (k * ((self.off - lag) // self.slots + 1) + c)


def apart(eng, mem):
    eng.sem_inc(mem["apart"], 1)


def wait(eng, sem, value):
    if not isinstance(value, int) or value > 0:
        eng.wait_ge(sem, value)


def pipeline(eng, step, slots=SLOTS, depth=DEPTH, total=B, ahead=1):
    first = depth
    loops = (total - ahead - first) // slots
    for s in range(first):
        step(Step(0, s, slots, total))
    with eng.Fori(0, loops) as i:
        for r in range(slots):
            step(Step(i, first + r, slots, total))
    for s in range(first + slots * loops, total + depth - 1):
        step(Step(0, s, slots, total))


def attention(nc, name, mem, causal, x_dram, lora, rope):
    at = AT[name]
    x_all, wqk, wv, wo, bqk, bv, bo = (mem[k] for k in ("x_all", "wqk", "wv", "wo", "bqk", "bv", "bo"))
    ident, ident_h, mask_qk, mask_kq = (mem[k] for k in ("ident", "ident_h", "mask_qk", "mask_kq"))
    scale = float(D) ** -0.5
    W = N // 2 + N if causal else 2 * N
    QKOPS = 4 if rope else 2

    with ExitStack() as ctx:
        def sb(label, shape, dt=F32):
            return ctx.enter_context(nc.sbuf_tensor(f"{name}_{label}", shape, dt))

        def sem(label):
            return nc.alloc_semaphore(name=f"{name}_{label}")

        scratch = nc.dram_tensor(f"{name}_scratch", (SLOTS, 2, PARTS, P, N), BF16, kind="Internal").ap()
        x_in = sb("x_in", [P, SLOTS, TB, C])
        xT = sb("xT", [P, SLOTS, N])
        qk = sb("qk", [P, 2, N])
        q_half = sb("q_half", [P, 2, N]) if rope else None
        rest = sb("rest", [P, 2, N])
        parts = sb("parts", [P, 2, PARTS, N], BF16)
        q_st = sb("q_st", [P, SLOTS, H, N], BF16)
        k_st = sb("k_st", [P, SLOTS, H, N], BF16)
        negmax = sb("negmax", [P, TB, H])
        mparts = sb("mparts", [P, 2, TB, MROWS, NH], BF16)
        mT_sb = sb("mT_sb", [MROWS * NH, 2, N], BF16)
        v_sb = sb("v_sb", [P, SLOTS, TB, H * 32])
        probs = sb("probs", [P, 2, 4, 2 * N])
        oT_sb = sb("oT_sb", [P, 2 * N])
        rden = sb("rden", [P, TB, H])
        o_sb = sb("o_sb", [P, TB, C])
        onT_sb = sb("onT_sb", [P, N])
        x_res = sb("x_res", [P, TB, C])
        y_sb = sb("y_sb", [P, TB, C])
        stats = sb("stats", [P, TB, 6])
        mv = sb("mv", [P, TB, 2])
        var = sb("var", [P, TB])
        rstd = sb("rstd", [P, TB])

        row_ps = ctx.enter_context(nc.psum_tensor(f"{name}_row_ps", [P, 3, 512], F32))
        col_ps = ctx.enter_context(nc.psum_tensor(f"{name}_col_ps", [P, 2, 512], F32))
        out_ps = ctx.enter_context(nc.psum_tensor(f"{name}_out_ps", [P, 512], F32))
        in_ps = ctx.enter_context(nc.psum_tensor(f"{name}_in_ps", [P, 512], F32))
        fin_ps = ctx.enter_context(nc.psum_tensor(f"{name}_fin_ps", [P, 512], F32))

        x_loaded = [sem(f"x_loaded{j}") for j in range(SLOTS)]
        parts_stored = [sem(f"parts_stored{j}") for j in range(SLOTS)]
        q_stacked = [sem(f"q_stacked{j}") for j in range(SLOTS)]
        k_stacked = [sem(f"k_stacked{j}") for j in range(SLOTS)]
        m_placed = [[sem(f"m_placed{g}{j}") for j in range(SLOTS)] for g in range(2)]
        xT_ready, qk_ready, v_ready, rows_ready, mT_ready, cols_ready, pv_ready, o_ready, onT_ready, y_ready = (
            sem(x) for x in ("xT_ready", "qk_ready", "v_ready", "rows_ready", "mT_ready", "cols_ready", "pv_ready",
                             "o_ready", "onT_ready", "y_ready"))
        xT_kept, qk_kept, v_kept, max_kept, mhi_kept, mparts_kept, mT_kept, probs_kept, oT_kept = (
            sem(x) for x in ("xT_kept", "qk_kept", "v_kept", "max_kept", "mhi_kept", "mparts_kept", "mT_kept",
                             "probs_kept", "oT_kept"))
        rden_kept, o_kept, onT_kept, y_kept, stats_kept, mv_kept, x_res_kept, var_kept, rstd_kept, ln_kept = (
            sem(x) for x in ("rden_kept", "o_kept", "onT_kept", "y_kept", "stats_kept", "mv_kept", "x_res_kept",
                             "var_kept", "rstd_kept", "ln_kept"))
        cos_done, sin_done, turned = (sem(x) for x in ("cos_done", "sin_done", "turned"))
        hi_kept, rest_kept, mid_kept, lo_kept = (sem(x) for x in ("hi_kept", "rest_kept", "mid_kept", "lo_kept"))
        v_cleared, k_ones = sem("v_cleared"), sem("k_ones")
        block = ctx.enter_context(nc.Block())

        def head(n):
            u, j = n // 4, n % 4
            return NH * (u // 2) + 2 * j + u % 2

        UNITS, ROW_BANKS = NH * TB, 3

        def row_bank(st, u):
            return (UNITS * st.off + u) % ROW_BANKS

        @block.sync
        def _(sp):
            def load_x(st, lag):
                wait(sp, xT_ready, st.seq(lag, c=1 - SLOTS))
                src = x_all[:, bass.ds(st.seq(lag, TB), TB), :] if x_dram is None else \
                    x_dram[:, bass.ds(st.seq(lag, TB), TB), :]
                sp.dma_start(x_in[:, st.slot(lag), :, :], src).then_inc(x_loaded[st.slot(lag)], 16)

            def step(st):
                if st.has(-1):
                    load_x(st, -1)
                if st.has(3):
                    sp.wait_ge(mT_kept, st.seq(3, 2, 2))
                    sl = st.slot(3)
                    sp.dma_start(q_st[KROWS:KROWS + MROWS, sl, NH:H, :], mT_sb[:, 1, :]).then_inc(m_placed[1][sl], 16)
                if st.has(0):
                    sl = st.slot(0)
                    sp.wait_ge(lo_kept, st.seq(0, c=1))
                    apart(sp, mem)
                    wait(sp, q_stacked[sl], st.turn(SLOTS, 48))
                    apart(sp, mem)
                    wait(sp, k_stacked[sl], st.turn(SLOTS, 16))
                    sp.dma_start(scratch[sl].rearrange("s j p n -> p (s j) n"),
                                 parts[:, :, :, :].rearrange("p s j n -> p (s j) n")).then_inc(parts_stored[sl], 16)
                if st.has(2):
                    sp.wait_ge(mT_kept, st.seq(2, 2, 1))
                    sl = st.slot(2)
                    sp.dma_start(q_st[KROWS:KROWS + MROWS, sl, 0:NH, :], mT_sb[:, 0, :]).then_inc(m_placed[0][sl], 16)
                if st.has(0):
                    sl = st.slot(0)
                    sp.wait_ge(k_ones, 1)
                    sp.wait_ge(parts_stored[sl], st.turn(0))
                    apart(sp, mem)
                    wait(sp, cols_ready, st.seq(SLOTS, H, H))
                    q_src = scratch[sl, 0].rearrange("j (d h) n -> j d (h n)", d=D)
                    k_src = scratch[sl, 1].rearrange("j (d h) n -> (j d) (h n)", d=D)
                    for j in range(PARTS):
                        rows = slice(PARTS * D * j, PARTS * D * (j + 1))
                        src = q_src[j]
                        thrice = bass.AP(src.tensor, src.offset, [[0, PARTS]] + [list(x) for x in src.ap])
                        sp.dma_start(q_st[rows, sl, :, :].rearrange("p h n -> p (h n)"), thrice)\
                            .then_inc(q_stacked[sl], 16)
                    thrice = bass.AP(k_src.tensor, k_src.offset, [[0, PARTS]] + [list(x) for x in k_src.ap])
                    sp.dma_start(k_st[0:KROWS, sl, :, :].rearrange("p h n -> p (h n)"), thrice)\
                        .then_inc(k_stacked[sl], 16)

            load_x(Step(0, 0, SLOTS, B), 0)
            pipeline(sp, step)

        @block.gpsimd
        def _(pool):
            nc.gpsimd.memset(k_st[64:96, :, :, :], 1.0).then_inc(k_ones, 1)
            pool.wait_ge(k_ones, 1)
            nc.gpsimd.memset(v_sb[:, :, :, :], 0.0).then_inc(v_cleared, 1)
            pool.wait_ge(v_cleared, 1)
            for a in range(2):
                one = v_sb[:, :, :, :].rearrange("p s t (q c) -> p (s t q) c", c=64)[:, :, 41 * a + D:41 * a + D + 1]
                nc.gpsimd.memset(one, 1.0).then_inc(v_cleared, 1)
            if x_dram is not None:
                pool.wait_ge(mem["x_all_loaded"], 16 * 8)

            def step(st):
                if st.has(4) and x_dram is not None:
                    wait(pool, y_kept, st.seq(4))
                    nc.gpsimd.tensor_tensor(x_res[:, :, :], x_all[:, bass.ds(st.seq(4, TB), TB), :],
                                            bo[:, :].unsqueeze(1).broadcast_to([P, TB, C]), ALU.add)\
                        .then_inc(x_res_kept, 1)
                if st.has(0):
                    pool.wait_ge(qk_kept, st.seq(0, QKOPS, QKOPS))
                    if rope:
                        pool.wait_ge(qk_kept, st.seq(0, QKOPS, QKOPS))
                        cos, sin = (mem[k][:, :].unsqueeze(1).broadcast_to([P, 2, N]) for k in ("cos", "sin"))
                        nc.gpsimd.tensor_tensor(q_half[:, :, :], q_half[:, :, :], sin, ALU.mult).then_inc(sin_done, 1)
                        nc.gpsimd.tensor_tensor(qk[:, :, :], qk[:, :, :], cos, ALU.mult).then_inc(cos_done, 1)
                        pool.wait_ge(sin_done, st.seq(0, c=1))
                        pool.wait_ge(cos_done, st.seq(0, c=1))
                        nc.gpsimd.tensor_tensor(qk[:, :, :], qk[:, :, :], q_half[:, :, :], ALU.add)\
                            .then_inc(turned, 1)
                        pool.wait_ge(turned, st.seq(0, c=1))
                    if st.has(1):
                        pool.wait_ge(parts_stored[st.slot(1)], st.turn(1))
                    apart(pool, mem)
                    nc.gpsimd.tensor_scalar(parts[:, :, 0, :], qk[:, :, :], 1.0, 0.0, ALU.mult, ALU.add)\
                        .then_inc(hi_kept, 1)
                    pool.wait_ge(hi_kept, st.seq(0, c=1))
                    nc.gpsimd.tensor_tensor(rest[:, :, :], qk[:, :, :], parts[:, :, 0, :], ALU.subtract)\
                        .then_inc(rest_kept, 1)
                    pool.wait_ge(rest_kept, st.seq(0, c=1))
                    apart(pool, mem)
                    nc.gpsimd.tensor_scalar(parts[:, :, 1, :], rest[:, :, :], 1.0, 0.0, ALU.mult, ALU.add)\
                        .then_inc(mid_kept, 1)
                    pool.wait_ge(mid_kept, st.seq(0, c=1))
                    nc.gpsimd.tensor_tensor(parts[:, :, 2, :], rest[:, :, :], parts[:, :, 1, :], ALU.subtract)\
                        .then_inc(lo_kept, 1)
                if st.has(4):
                    pool.wait_ge(var_kept, st.seq(4, c=1))
                    nc.gpsimd.tensor_tensor(rstd[:, :], var[:, :], mem["minus_half"][:, 0:TB], ALU.pow)\
                        .then_inc(rstd_kept, 1)

            pipeline(pool, step)

        @block.scalar
        def _(act):
            def step(st):
                for n in range(H):
                    if st.has(3):
                        u, j = n // 4, n % 4
                        act.wait_ge(cols_ready, st.seq(3, H, n + 1))
                        if j == 0:
                            wait(act, pv_ready, st.seq(3, 4, u - 1))
                        nc.scalar.activation(probs[:, u % 2, j, 0:W], col_ps[:, n % 2, 0:W], ACT.Exp,
                                             scale=scale).then_inc(probs_kept, 1)
                    if n == at["act_xT"] and st.has(0):
                        act.wait_ge(xT_ready, st.seq(0, c=1))
                        wait(act, v_ready, st.seq(SLOTS, c=1))
                        nc.scalar.copy(xT[:, st.slot(0), :], in_ps[:, 0:N]).then_inc(xT_kept, 1)
                    if n == at["act_mT1"] and st.has(3):
                        act.wait_ge(mT_ready, st.seq(3, 2, 2))
                        if st.has(4):
                            act.wait_ge(m_placed[1][st.slot(4)], st.turn(4))
                        nc.scalar.copy(mT_sb[:, 1, :], fin_ps[0:MROWS * NH, 0:N // 2].bitcast(BF16))\
                            .then_inc(mT_kept, 1)
                    if n == at["act_qk"] and st.has(0):
                        act.wait_ge(qk_ready, st.seq(0, c=1))
                        wait(act, rest_kept, st.seq(0))
                        if rope:
                            for to, of in ((0, P // 2), (P // 2, 0)):
                                nc.scalar.copy(q_half[to:to + P // 2, :, :].rearrange("p s n -> p (s n)"),
                                               in_ps[of:of + P // 2, :]).then_inc(qk_kept, 1)
                        for s in range(2):
                            if lora:
                                nc.scalar.activation(qk[:, s, :], in_ps[:, s * N:(s + 1) * N], ACT.Identity,
                                                     bias=bqk[:, s:s + 1]).then_inc(qk_kept, 1)
                            else:
                                nc.scalar.copy(qk[:, s, :], in_ps[:, s * N:(s + 1) * N]).then_inc(qk_kept, 1)
                    if n == at["act_oT"] and st.has(4):
                        act.wait_ge(pv_ready, st.seq(4, 4, 4))
                        wait(act, o_ready, st.seq(4))
                        nc.scalar.copy(oT_sb[:, :], out_ps[:, :]).then_inc(oT_kept, 1)
                    if n == at["act_onT"] and st.has(4):
                        act.wait_ge(onT_ready, st.seq(4, c=1))
                        wait(act, y_ready, st.seq(4))
                        nc.scalar.copy(onT_sb[:, :], fin_ps[:, 0:N]).then_inc(onT_kept, 1)
                    if n == at["act_mT0"] and st.has(2):
                        act.wait_ge(mT_ready, st.seq(2, 2, 1))
                        if st.has(3):
                            act.wait_ge(m_placed[0][st.slot(3)], st.turn(3))
                        nc.scalar.copy(mT_sb[:, 0, :], in_ps[0:MROWS * NH, 0:N // 2].bitcast(BF16))\
                            .then_inc(mT_kept, 1)

            pipeline(act, step)

        @block.vector
        def _(dve):
            def row_max(st, u):
                p, t = u // TB, u % TB
                if u % NH == 0:
                    wait(dve, mparts_kept, st.seq(2, 2, u // NH - 1))
                dve.wait_ge(rows_ready, st.seq(2, UNITS, u + 1))
                keys = (t + 1) * P if causal else N
                nc.vector.tensor_reduce(
                    negmax[:, t, 2 * p:2 * p + 2],
                    row_ps[:, row_bank(st, u), 0:2 * keys].rearrange("p (a k) -> p a k", a=2),
                    AX_X, ALU.max, negate=True).then_inc(max_kept, 1)

            def split_max(st, g):
                dve.wait_ge(max_kept, st.seq(2, UNITS, UNITS // 2 * (g + 1)))
                wait(dve, mT_ready, st.seq(3, 2, g + 1))
                half = negmax[:, :, NH * g:NH * (g + 1)]
                nc.vector.tensor_copy(mparts[:, g, :, 0, :], half).then_inc(mhi_kept, 1)
                dve.wait_ge(mhi_kept, st.seq(2, 2, g + 1))
                nc.vector.tensor_tensor(mparts[:, g, :, 1, :], half, mparts[:, g, :, 0, :], ALU.subtract)\
                    .then_inc(mparts_kept, 1)

            def keep_v(st):
                dve.wait_ge(v_ready, st.seq(2, c=1))
                wait(dve, pv_ready, st.seq(2 + SLOTS, 4, 4))
                dve.wait_ge(v_cleared, 3)
                for t in range(TB):
                    to = strided(v_sb[:, st.slot(2), t, 0:1], [[64, H // 2], [41, 2], [1, D]])
                    of = in_ps[:, t * C:(t + 1) * C].rearrange("p (q a d) -> p q a d", a=2, d=D)
                    if lora:
                        nc.vector.tensor_tensor(to, of, bv[:, :].rearrange("p (q a d) -> p q a d", a=2, d=D),
                                                ALU.add).then_inc(v_kept, 1)
                    else:
                        nc.vector.tensor_copy(to, of).then_inc(v_kept, 1)

            def normalise_o(st):
                dve.wait_ge(o_ready, st.seq(4, c=1))
                wait(dve, onT_ready, st.seq(4))
                nc.vector.reciprocal(rden[:, :, :].rearrange("p t (j a) -> p (t j) a", a=2),
                                     strided(fin_ps[:, D:D + 1], [[32, 2 * NH], [D + 1, 2]])).then_inc(rden_kept, 1)
                dve.wait_ge(rden_kept, st.seq(4, c=1))
                for t in range(TB):
                    nc.vector.tensor_tensor(
                        o_sb[:, t, :].rearrange("p (j a d) -> p j a d", a=2, d=D),
                        strided(fin_ps[:, 256 * t:256 * t + 1], [[32, NH], [D + 1, 2], [1, D]]),
                        rden[:, t, :].rearrange("p (j a) -> p j a", a=2).unsqueeze(3).broadcast_to([P, NH, 2, D]),
                        ALU.mult).then_inc(o_kept, 1)

            def add_residual(st):
                dve.wait_ge(y_ready, st.seq(4, c=1))
                if x_dram is not None:
                    dve.wait_ge(x_res_kept, st.seq(4, c=1))
                    x_old = x_res[:, :, :]
                else:
                    x_old = x_all[:, bass.ds(st.seq(4, TB), TB), :]
                nc.vector.tensor_tensor(y_sb[:, :, :], fin_ps[:, 0:N].rearrange("p (t c) -> p t c", t=TB), x_old,
                                        ALU.add).then_inc(y_kept, 1)
                dve.wait_ge(y_kept, st.seq(4, c=1))
                for t in range(TB):
                    nc.vector.bn_stats(stats[:, t, :], y_sb[:, t, :]).then_inc(stats_kept, 1)

            def variance(st):
                dve.wait_ge(stats_kept, st.seq(4, TB, TB))
                apart(dve, mem)
                for t in range(TB):
                    nc.vector.bn_aggr(mv[:, t, :], stats[:, t, :]).then_inc(mv_kept, 1)
                dve.wait_ge(mv_kept, st.seq(4, TB, TB))
                wait(dve, rstd_kept, st.seq(4))
                nc.vector.tensor_scalar(var[:, :], mv[:, :, 1], EPS, None, ALU.add).then_inc(var_kept, 1)

            def layer_norm(st):
                dve.wait_ge(rstd_kept, st.seq(4, c=1))
                for t in range(TB):
                    nc.vector.tensor_scalar(x_all[:, bass.ds(st.seq(4, TB, t), 1), :].rearrange("p t c -> p (t c)"),
                                            y_sb[:, t, :], mv[:, t, 0:1], rstd[:, t:t + 1],
                                            ALU.subtract, ALU.mult).then_inc(ln_kept, 1)

            def step(st):
                for n in range(H):
                    if st.has(2):
                        row_max(st, n)
                    if n == at["dve_o"] and st.has(4):
                        normalise_o(st)
                    if n == at["dve_split0"] and st.has(2):
                        split_max(st, 0)
                    if n == at["dve_v"] and st.has(2):
                        keep_v(st)
                    if n == at["dve_y"] and st.has(4):
                        add_residual(st)
                    if n == 15 and st.has(2):
                        split_max(st, 1)
                    if n == at["dve_var"] and st.has(4):
                        variance(st)
                    if n == at["dve_ln"] and st.has(4):
                        layer_norm(st)

            pipeline(dve, step)

        @block.tensor
        def _(pe):
            def transpose_x(st):
                pe.wait_ge(x_loaded[st.slot(0)], st.turn(0))
                if st.has(3):
                    pe.wait_ge(mT_kept, st.seq(3, 2, 1))
                elif st.has(1):
                    pe.wait_ge(qk_kept, st.seq(1, QKOPS, QKOPS))
                for t in range(TB):
                    last = nc.tensor.transpose(in_ps[:, t * P:(t + 1) * P], x_in[:, st.slot(0), t, :], ident[:, :])
                last.then_inc(xT_ready, 1)

            def transpose_max(st, lag, g):
                if g == 0:
                    pe.wait_ge(v_kept, st.seq(2, TB, TB))
                elif st.has(5):
                    pe.wait_ge(y_kept, st.seq(5, c=1))
                elif st.has(4):
                    pe.wait_ge(mT_kept, st.seq(4, 2, 2))
                pe.wait_ge(mparts_kept, st.seq(lag, 2, g + 1))
                for t in range(TB):
                    last = nc.tensor.transpose(
                        (fin_ps if g else in_ps)[0:MROWS * NH, t * P // 2:(t + 1) * P // 2].bitcast(BF16),
                        mparts[:, g, t, :, :].rearrange("p m h -> p (m h)"), ident_h[:, :])
                last.then_inc(mT_ready, 1)

            def project_qk(st):
                pe.wait_ge(xT_kept, st.seq(0, c=1))
                for s in range(2):
                    last = nc.tensor.matmul(in_ps[:, s * N:(s + 1) * N], wqk[:, s, :], xT[:, st.slot(0), :],
                                            start=True, stop=True)
                last.then_inc(qk_ready, 1)

            def transpose_o(st):
                if st.has(3):
                    pe.wait_ge(mT_kept, st.seq(3, 2, 2))
                elif st.has(5):
                    pe.wait_ge(y_kept, st.seq(5, c=1))
                pe.wait_ge(oT_kept, st.seq(4, c=1))
                for t in range(TB):
                    for g in range(2):
                        last = nc.tensor.transpose(fin_ps[:, (2 * t + g) * P:(2 * t + g + 1) * P],
                                                   oT_sb[:, g * N + t * P:g * N + (t + 1) * P], ident[:, :])
                last.then_inc(o_ready, 1)

            def project_v(st):
                if st.has(0):
                    pe.wait_ge(qk_kept, st.seq(0, QKOPS, QKOPS))
                else:
                    pe.wait_ge(mT_kept, st.seq(3, 2, 1))
                for t in range(TB):
                    last = nc.tensor.matmul(in_ps[:, t * C:(t + 1) * C], xT[:, st.slot(2), t * P:(t + 1) * P],
                                            wv[:, :], start=True, stop=True)
                last.then_inc(v_ready, 1)

            def transpose_on(st):
                pe.wait_ge(o_kept, st.seq(4, TB, TB))
                for t in range(TB):
                    last = nc.tensor.transpose(fin_ps[:, t * P:(t + 1) * P], o_sb[:, t, :], ident[:, :])
                last.then_inc(onT_ready, 1)

            def project_o(st):
                pe.wait_ge(onT_kept, st.seq(4, c=1))
                for t in range(TB):
                    last = nc.tensor.matmul(fin_ps[:, t * C:(t + 1) * C], onT_sb[:, t * P:(t + 1) * P], wo[:, :],
                                            start=True, stop=True)
                last.then_inc(y_ready, 1)

            def score_rows(st, u):
                sl = st.slot(2)
                p, t = u // TB, u % TB
                if u == 0:
                    pe.wait_ge(q_stacked[sl], st.turn(2, 48))
                    pe.wait_ge(k_stacked[sl], st.turn(2, 16))
                wait(pe, max_kept, st.seq(2, UNITS, u + 1 - ROW_BANKS))
                bank = row_ps[:, row_bank(st, u), :]
                keys = (t + 1) * P if causal else N
                if causal:
                    seen = bank[:, 0:2 * keys].rearrange("p (a k) -> p a k", a=2)
                    nc.tensor.matmul(seen[:, :, keys - P:keys], ident_h[:, :], mask_qk[:, :, :],
                                     start=True, stop=False, skip_group_check=True)
                for a in range(2):
                    h = 2 * p + a
                    last = nc.tensor.matmul(bank[:, a * keys:(a + 1) * keys],
                                            q_st[0:KROWS, sl, h, t * P:(t + 1) * P], k_st[0:KROWS, sl, h, 0:keys],
                                            start=not causal, stop=True, skip_group_check=causal)
                last.then_inc(rows_ready, 1)

            def score_cols(st, n):
                sl, h = st.slot(3), head(n)
                if n == 0:
                    pe.wait_ge(m_placed[0][sl], st.turn(3))
                if n == H // 2:
                    pe.wait_ge(m_placed[1][sl], st.turn(3))
                wait(pe, probs_kept, st.seq(3, H, n - 1))
                bank = col_ps[:, n % 2, :]
                rows = KROWS + MROWS
                if causal:
                    seen = bank[:, 0:2 * N].rearrange("p (a q) -> p a q", a=2)
                    nc.tensor.matmul(seen[:, :, 0:P], ident_h[:, :], mask_kq[:, :, :],
                                     start=True, stop=False, skip_group_check=True)
                for t in range(TB):
                    first = t * P if causal else 0
                    last = nc.tensor.matmul(bank[:, t * N:(t + 1) * N - first],
                                            k_st[0:rows, sl, h, t * P:(t + 1) * P], q_st[0:rows, sl, h, first:N],
                                            start=not causal, stop=True, skip_group_check=causal)
                last.then_inc(cols_ready, 1)

            def sum_values(st, lag, u):
                g, a = u // 2, u % 2
                if u == 0:
                    wait(pe, oT_kept, st.seq(lag))
                    pe.wait_ge(v_kept, st.seq(lag, TB, TB))
                pe.wait_ge(probs_kept, st.seq(lag, H, 4 * u + 4))
                for t in range(TB):
                    first = t * P if causal else 0
                    for j in range(4):
                        h = head(4 * u + j)
                        last = nc.tensor.matmul(out_ps[32 * j:32 * j + 32, g * N + first:(g + 1) * N],
                                                v_sb[:, st.slot(lag), t, 32 * h:32 * h + 32],
                                                probs[:, u % 2, j, t * N:(t + 1) * N - first],
                                                start=a == 0 and t == 0, stop=a == 1 and t == TB - 1,
                                                skip_group_check=True)
                last.then_inc(pv_ready, 1)

            def step(st):
                for n in range(H):
                    if st.has(3):
                        score_cols(st, n)
                    if st.has(2):
                        score_rows(st, n)
                    if n == at["pe_xT"] and st.has(0):
                        transpose_x(st)
                    if n == at["pe_mT1"] and st.has(3):
                        transpose_max(st, 3, 1)
                    if n == at["pe_pv3"] and st.has(4):
                        sum_values(st, 4, 3)
                    if n == at["pe_qk"] and st.has(0):
                        project_qk(st)
                    if n == at["pe_oT"] and st.has(4):
                        transpose_o(st)
                    if n in (at["pe_pv"], at["pe_pv"] + 4, at["pe_pv"] + 8) and st.has(3):
                        sum_values(st, 3, (n - at["pe_pv"]) // 4)
                    if n == at["pe_v"] and st.has(2):
                        project_v(st)
                    if n == at["pe_onT"] and st.has(4):
                        transpose_on(st)
                    if n == at["pe_mT0"] and st.has(2):
                        transpose_max(st, 2, 0)
                    if n == at["pe_y"] and st.has(4):
                        project_o(st)

            pipeline(pe, step)



E = 8
CAP = int(1.25 * B * N / E)
GT = 8
GROUPS = TILES // GT
MT = 4


def groups(eng, step):
    pipeline(eng, step, 2, 4, GROUPS, 0)


def moe(nc, mem, w):
    x_all, x_mid, ident = mem["x_all"], mem["x_mid"], mem["ident"]
    with ExitStack() as ctx:
        def sb(label, shape, dt=F32):
            return ctx.enter_context(nc.sbuf_tensor(f"moe_{label}", shape, dt))

        def sem(label):
            return nc.alloc_semaphore(name=f"moe_{label}")

        gate_T = sb("gate_T", [P, 32])
        gates_sb = sb("gates_sb", [P, 2, 2 * P])
        rank = sb("rank", [P, E])
        ones = sb("ones", [P, P])
        xs = sb("xs", [P, 2, GT, C])
        xT = sb("xT", [P, 2, GT * P])
        logits = sb("logits", [P, TILES, E])
        probs = sb("probs", [P, TILES, E])
        left = sb("left", [P, TILES, E])
        equal = sb("equal", [P, TILES, E])
        score = sb("score", [P, TILES, E])
        chosen = [sb(f"chosen{k}", [P, TILES, E]) for k in range(2)]
        top = sb("top", [P, TILES])
        total = sb("total", [P, TILES])
        counts = sb("counts", [P, E])
        keep = sb("keep", [P, E])
        any_kept = sb("any_kept", [P, 1])
        flag = sb("flag", [P, 1], I32)
        weight = sb("weight", [P, TILES, E])
        stats = sb("stats", [P, 2, GT, 6])
        mv = sb("mv", [P, 2, GT, 2])
        mean = sb("mean", [P, TILES])
        var = sb("var", [P, TILES])
        rstd = sb("rstd", [P, TILES])
        shift = sb("shift", [P, TILES])
        minus_one = sb("minus_one", [P, TILES])
        e_w = sb("e_w", [P, 2, E, C])
        e_wT = sb("e_wT", [P, 2, E, C])
        e_b = sb("e_b", [P, 2, E, C])
        e_x = sb("e_x", [P, MT, C])
        e_xT = sb("e_xT", [P, MT * P])
        e_pre = sb("e_pre", [P, MT, C])
        e_h = sb("e_h", [P, MT, C])
        e_hT = sb("e_hT", [P, MT * P])
        e_y = sb("e_y", [P, MT, C])
        e_acc = sb("e_acc", [P, MT, C])

        t_ps = ctx.enter_context(nc.psum_tensor("moe_t_ps", [P, 2, 2, 512], F32))
        g_ps = ctx.enter_context(nc.psum_tensor("moe_g_ps", [P, 2, 512], F32))
        l_ps = ctx.enter_context(nc.psum_tensor("moe_l_ps", [P, 2, 512], F32))

        loaded, consts, xs_loaded = sem("loaded"), sem("consts"), [sem(f"xs_loaded{j}") for j in range(2)]
        xT_ready, xT_kept, gates_ready, gates_kept, logits_ready, logits_kept = (
            sem(x) for x in ("xT_ready", "xT_kept", "gates_ready", "gates_kept", "logits_ready", "logits_kept"))
        shifted, exp_kept, routed, counts_ready, flag_kept = (
            sem(x) for x in ("shifted", "exp_kept", "routed", "counts_ready", "flag_kept"))
        mean_kept = sem("mean_kept")
        stats_kept, mv_kept, var_kept, rstd_kept, scaled, ln_kept = (
            sem(x) for x in ("stats_kept", "mv_kept", "var_kept", "rstd_kept", "scaled", "ln_kept"))
        e_loaded, e_x_loaded, ewT_ready, ewT_kept = (
            sem(x) for x in ("e_loaded", "e_x_loaded", "ewT_ready", "ewT_kept"))
        exT_ready, exT_kept, h_ready, pre_kept, h_kept, hT_ready, hT_kept, y_ready = (
            sem(x) for x in ("exT_ready", "exT_kept", "h_ready", "pre_kept", "h_kept", "hT_ready", "hT_kept",
                             "y_ready"))
        y_kept, acc_kept, cleared, experts_done = (sem(x) for x in ("y_kept", "acc_kept", "cleared", "experts_done"))

        COUNTED = 15

        def measure(dve, st, group, counted):
            tiles, j = bass.ds(group * GT, GT), st.slot(0)
            for t in range(GT):
                nc.vector.bn_stats(stats[:, j, t, :], x_all[:, bass.ds(group * GT + t, 1), :].rearrange(
                    "p t c -> p (t c)")).then_inc(stats_kept, 1)
            dve.wait_ge(stats_kept, (group + (counted + 1)) * GT)
            apart(dve, mem)
            for t in range(GT):
                nc.vector.bn_aggr(mv[:, j, t, :], stats[:, j, t, :]).then_inc(mv_kept, 1)
            dve.wait_ge(mv_kept, (group + (counted + 1)) * GT)
            nc.vector.tensor_copy(mean[:, tiles], mv[:, j, :, 0]).then_inc(mean_kept, 1)
            nc.vector.tensor_scalar(var[:, tiles], mv[:, j, :, 1], EPS, None, ALU.add).then_inc(var_kept, 1)

        with nc.Block() as block:

            @block.sync
            def _(sp):
                sp.wait_ge(consts, E + 3)
                sp.dma_start(gate_T[:, 0:E], w["L0_ffn_gate_w"].rearrange("e c -> c e"),
                             allow_slow_non_contiguous=True).then_inc(loaded, 16)

                def step(st):
                    if st.has(0):
                        j = st.slot(0)
                        wait(sp, xT_ready, st.seq(1))
                        sp.dma_start(xs[:, j, :, :], x_all[:, bass.ds(st.seq(0, GT), GT), :])\
                            .then_inc(xs_loaded[j], 16)

                groups(sp, step)

            @block.gpsimd
            def _(pool):
                for e in range(E):
                    nc.gpsimd.memset(rank[:, e:e + 1], float(E - e)).then_inc(consts, 1)
                nc.gpsimd.memset(ones[:, :], 1.0).then_inc(consts, 1)
                nc.gpsimd.memset(gate_T[:, :], 0.0).then_inc(consts, 1)
                nc.gpsimd.memset(minus_one[:, :], -1.0).then_inc(consts, 1)

                def step(st):
                    if st.has(0):
                        pool.wait_ge(var_kept, st.seq(0, c=1))
                        tiles = bass.ds(st.seq(0, GT), GT)
                        nc.gpsimd.tensor_tensor(rstd[:, tiles], var[:, tiles], mem["minus_half"][:, 0:GT], ALU.pow)\
                            .then_inc(rstd_kept, 1)

                groups(pool, step)
                pool.wait_ge(rstd_kept, GROUPS)
                pool.wait_ge(mean_kept, GROUPS)
                nc.gpsimd.tensor_tensor(shift[:, :], mean[:, :], rstd[:, :], ALU.mult).then_inc(scaled, 1)
                pool.wait_ge(scaled, 1)
                nc.gpsimd.tensor_tensor(shift[:, :], shift[:, :], minus_one[:, :], ALU.mult).then_inc(scaled, 1)

            @block.tensor
            def _(pe):
                pe.wait_ge(loaded, 16)

                def step(st):
                    if st.has(0):
                        j = st.slot(0)
                        pe.wait_ge(xs_loaded[j], st.turn(0))
                        wait(pe, xT_kept, st.seq(1, 2))
                        for t in range(GT):
                            last = nc.tensor.transpose(t_ps[:, j, t // 4, t % 4 * P:(t % 4 + 1) * P], xs[:, j, t, :],
                                                       ident[:, :])
                        last.then_inc(xT_ready, 1)
                    if st.has(1):
                        j = st.slot(1)
                        pe.wait_ge(xT_kept, st.seq(1, 2, 2))
                        wait(pe, gates_kept, st.seq(2))
                        for g in range(4):
                            last = nc.tensor.matmul(g_ps[32 * g:32 * g + 32, j, 0:2 * P], gate_T[:, :],
                                                    xT[:, j, 2 * g * P:(2 * g + 2) * P], start=True, stop=True,
                                                    skip_group_check=True)
                        last.then_inc(gates_ready, 1)
                    if st.has(2):
                        j = st.slot(2)
                        pe.wait_ge(gates_kept, st.seq(2, c=1))
                        wait(pe, logits_kept, st.seq(3))
                        for t in range(2):
                            last = nc.tensor.transpose(l_ps[:, j, t * P:(t + 1) * P], gates_sb[:, j, t * P:(t + 1) * P],
                                                       ident[:, :])
                        last.then_inc(logits_ready, 1)

                groups(pe, step)
                pe.wait_ge(routed, COUNTED)
                nc.tensor.matmul(g_ps[:, 0, 0:E], ones[:, :], counts[:, :], start=True, stop=True)\
                    .then_inc(counts_ready, 1)

            @block.scalar
            def _(act):
                def step(st):
                    if st.has(0):
                        j = st.slot(0)
                        act.wait_ge(xT_ready, st.seq(0, c=1))
                        wait(act, gates_ready, st.seq(1))
                        for b in range(2):
                            nc.scalar.copy(xT[:, j, b * 512:(b + 1) * 512], t_ps[:, j, b, :]).then_inc(xT_kept, 1)
                    if st.has(1):
                        j = st.slot(1)
                        act.wait_ge(gates_ready, st.seq(1, c=1))
                        wait(act, logits_ready, st.seq(2))
                        nc.scalar.copy(gates_sb[:, j, :], g_ps[:, j, 0:2 * P]).then_inc(gates_kept, 1)

                groups(act, step)
                act.wait_ge(shifted, 1)
                nc.scalar.activation(probs[:, :, :], left[:, :, :], ACT.Exp).then_inc(exp_kept, 1)
                act.wait_ge(scaled, 2)
                with act.Fori(0, TILES // GT) as i:
                    for t in range(GT):
                        tile = bass.ds(i * GT + t, 1)
                        nc.scalar.activation(x_mid[:, tile, :].rearrange("p t c -> p (t c)"),
                                             x_all[:, tile, :].rearrange("p t c -> p (t c)"), ACT.Identity,
                                             bias=shift[:, tile], scale=rstd[:, tile]).then_inc(ln_kept, 1)

            @block.vector
            def _(dve):
                done = [0]

                def then(ins):
                    ins.then_inc(routed, 1)
                    done[0] += 1
                    dve.wait_ge(routed, done[0])

                def over_experts(ap):
                    return ap.unsqueeze(2).broadcast_to([P, TILES, E])

                def step(st):
                    if st.has(2):
                        dve.wait_ge(logits_ready, st.seq(2, c=1))
                        of = l_ps[:, st.slot(2), 0:2 * P].rearrange("p (t g m) -> p t g m", t=2, m=32)
                        nc.vector.tensor_copy(
                            logits[:, bass.ds(st.seq(2, GT), GT), :].rearrange("p (g t) e -> p t g e", t=2),
                            of[:, :, :, 0:E]).then_inc(logits_kept, 1)
                    if st.has(0):
                        measure(dve, st, st.seq(0), 0)

                groups(dve, step)
                dve.wait_ge(logits_kept, GROUPS)
                dve.wait_ge(consts, E + 3)
                then(nc.vector.tensor_reduce(top[:, :], logits[:, :, :], AX_X, ALU.max))
                nc.vector.tensor_tensor(left[:, :, :], logits[:, :, :], over_experts(top[:, :]), ALU.subtract)\
                    .then_inc(shifted, 1)
                dve.wait_ge(exp_kept, 1)
                then(nc.vector.tensor_reduce(total[:, :], probs[:, :, :], AX_X, ALU.add))
                then(nc.vector.reciprocal(top[:, :], total[:, :]))
                then(nc.vector.tensor_tensor(probs[:, :, :], probs[:, :, :], over_experts(top[:, :]), ALU.mult))
                of = probs
                for k in range(2):
                    then(nc.vector.tensor_reduce(top[:, :], of[:, :, :], AX_X, ALU.max))
                    then(nc.vector.tensor_tensor(equal[:, :, :], of[:, :, :], over_experts(top[:, :]), ALU.is_equal))
                    then(nc.vector.tensor_tensor(score[:, :, :], equal[:, :, :],
                                                 rank[:, :].unsqueeze(1).broadcast_to([P, TILES, E]), ALU.mult))
                    then(nc.vector.tensor_reduce(top[:, :], score[:, :, :], AX_X, ALU.max))
                    then(nc.vector.tensor_tensor(chosen[k][:, :, :], score[:, :, :], over_experts(top[:, :]),
                                                 ALU.is_equal))
                    if k == 0:
                        nc.vector.scalar_tensor_tensor(out=left[:, :, :], in0=chosen[0][:, :, :], scalar=-2.0,
                                                       in1=probs[:, :, :], op0=ALU.mult, op1=ALU.add)\
                            .then_inc(shifted, 1)
                        dve.wait_ge(shifted, 2)
                        of = left
                nc.vector.tensor_tensor(chosen[0][:, :, :], chosen[0][:, :, :], chosen[1][:, :, :], ALU.add)\
                    .then_inc(shifted, 1)
                dve.wait_ge(shifted, 3)
                then(nc.vector.tensor_reduce(counts[:, :], chosen[0][:, :, :].rearrange("p t e -> p e t"), AX_X,
                                             ALU.add))
                assert done[0] == COUNTED
                dve.wait_ge(counts_ready, 1)
                then(nc.vector.tensor_scalar(keep[:, :], g_ps[:, 0, 0:E], float(CAP), None, ALU.is_le))
                then(nc.vector.tensor_reduce(any_kept[:, :], keep[:, :], AX_X, ALU.max))
                nc.vector.tensor_copy(flag[:, :], any_kept[:, :]).then_inc(flag_kept, 1)

        FREE = 1
        with nc.Block() as block:

            @block.sync
            def _(sp):
                with sp.If(sp.value_load(flag[0:1, 0:1], min_val=0, max_val=1) > 0):
                    for n, k in enumerate(("1", "2")):
                        sp.dma_start(e_w[:, n, :, :], w[f"L0_ffn_w{k}"].rearrange("e o i -> o e i"))\
                            .then_inc(e_loaded, 16)
                        b = w[f"L0_ffn_b{k}"]
                        sp.dma_start(e_b[:, n, :, :].rearrange("p e c -> p (e c)"),
                                     bass.AP(b.tensor, b.offset, [[0, P], [1, E * C]])).then_inc(e_loaded, 16)
                    with sp.Fori(0, TILES // MT) as g:
                        sp.wait_ge(experts_done, g + FREE)
                        sp.dma_start(e_x[:, :, :], x_all[:, bass.ds(g * MT, MT), :]).then_inc(e_x_loaded, 16)
                with sp.Else():
                    sp.nop()
                sp.nop()

            @block.tensor
            def _(pe):
                with pe.If(pe.value_load(flag[0:1, 0:1], min_val=0, max_val=1) > 0):
                    for s in (h_ready, hT_ready, y_ready):
                        pe.sem_inc(s, FREE)
                    pe.wait_ge(e_loaded, 64)
                    for n in range(2):
                        for half in range(2):
                            k = 2 * n + half
                            if k >= 2:
                                pe.wait_ge(ewT_kept, k - 1)
                            for q in range(E // 2):
                                last = nc.tensor.transpose(t_ps[:, 0, k % 2, q * P:(q + 1) * P],
                                                           e_w[:, n, half * E // 2 + q, :], ident[:, :])
                            last.then_inc(ewT_ready, 1)
                    pe.wait_ge(ewT_kept, 4)
                    with pe.Fori(0, TILES // MT) as g:
                        pe.wait_ge(e_x_loaded, g * 16 + 16)
                        pe.wait_ge(exT_kept, g + FREE)
                        for t in range(MT):
                            last = nc.tensor.transpose(t_ps[:, 0, 0, t * P:(t + 1) * P], e_x[:, t, :], ident[:, :])
                        last.then_inc(exT_ready, 1)
                        pe.wait_ge(exT_kept, g + (1 + FREE))
                        apart(pe, mem)
                        with pe.Fori(0, E) as e:
                            pe.wait_ge(pre_kept, g * E + e + FREE)
                            for t in range(MT):
                                last = nc.tensor.matmul(t_ps[:, 0, 1, t * P:(t + 1) * P], e_xT[:, t * P:(t + 1) * P],
                                                        e_wT[:, 0, bass.ds(e, 1), :].rearrange("p e c -> p (e c)"),
                                                        start=True, stop=True)
                            last.then_inc(h_ready, 1)
                            pe.wait_ge(h_kept, g * E + (e + (1 + FREE)))
                            pe.wait_ge(hT_kept, g * E + e + FREE)
                            for t in range(MT):
                                last = nc.tensor.transpose(t_ps[:, 1, 0, t * P:(t + 1) * P], e_h[:, t, :],
                                                           ident[:, :])
                            last.then_inc(hT_ready, 1)
                            pe.wait_ge(hT_kept, g * E + (e + (1 + FREE)))
                            pe.wait_ge(y_kept, g * E + e + FREE)
                            for t in range(MT):
                                last = nc.tensor.matmul(t_ps[:, 1, 1, t * P:(t + 1) * P], e_hT[:, t * P:(t + 1) * P],
                                                        e_wT[:, 1, bass.ds(e, 1), :].rearrange("p e c -> p (e c)"),
                                                        start=True, stop=True)
                            last.then_inc(y_ready, 1)
                with pe.Else():
                    pe.nop()
                pe.nop()

            @block.gpsimd
            def _(pool):
                with pool.If(pool.value_load(flag[0:1, 0:1], min_val=0, max_val=1) > 0):
                    pool.wait_ge(var_kept, 2 * GROUPS)
                    nc.gpsimd.tensor_tensor(rstd[:, :], var[:, :], mem["minus_half"][:, :], ALU.pow)\
                        .then_inc(rstd_kept, 1)
                with pool.Else():
                    pool.nop()
                pool.nop()

            @block.scalar
            def _(act):
                with act.If(act.value_load(flag[0:1, 0:1], min_val=0, max_val=1) > 0):
                    for s in (exT_kept, h_kept, hT_kept):
                        act.sem_inc(s, FREE)
                    for k in range(4):
                        act.wait_ge(ewT_ready, k + 1)
                        nc.scalar.copy(e_wT[:, k // 2, k % 2 * 4:k % 2 * 4 + 4, :].rearrange("p e c -> p (e c)"),
                                       t_ps[:, 0, k % 2, :]).then_inc(ewT_kept, 1)
                    with act.Fori(0, TILES // MT) as g:
                        act.wait_ge(exT_ready, g + 1)
                        act.wait_ge(h_ready, g * E + FREE)
                        nc.scalar.copy(e_xT[:, :], t_ps[:, 0, 0, :]).then_inc(exT_kept, 1)
                        with act.Fori(0, E) as e:
                            act.wait_ge(pre_kept, g * E + (e + (1 + FREE)))
                            act.wait_ge(hT_ready, g * E + e + FREE)
                            nc.scalar.activation(e_h[:, :, :], e_pre[:, :, :], ACT.Silu).then_inc(h_kept, 1)
                            act.wait_ge(hT_ready, g * E + (e + (1 + FREE)))
                            act.wait_ge(y_ready, g * E + e + FREE)
                            nc.scalar.copy(e_hT[:, :], t_ps[:, 1, 0, :]).then_inc(hT_kept, 1)
                with act.Else():
                    act.nop()
                act.nop()

            @block.vector
            def _(dve):
                with dve.If(dve.value_load(flag[0:1, 0:1], min_val=0, max_val=1) > 0):
                    for s in (pre_kept, y_kept, experts_done):
                        dve.sem_inc(s, FREE)
                    nc.vector.tensor_tensor(weight[:, :, :], chosen[0][:, :, :], probs[:, :, :], ALU.mult)\
                        .then_inc(shifted, 1)
                    dve.wait_ge(shifted, 4)
                    nc.vector.tensor_tensor(weight[:, :, :], weight[:, :, :],
                                            keep[:, :].unsqueeze(1).broadcast_to([P, TILES, E]), ALU.mult)\
                        .then_inc(shifted, 1)
                    dve.wait_ge(shifted, 5)
                    dve.wait_ge(e_loaded, 64)
                    with dve.Fori(0, TILES // MT) as g:
                        dve.wait_ge(experts_done, g + FREE)
                        nc.vector.memset(e_acc[:, :, :], 0.0).then_inc(cleared, 1)
                        dve.wait_ge(cleared, g + 1)
                        apart(dve, mem)
                        with dve.Fori(0, E) as e:
                            dve.wait_ge(h_ready, g * E + (e + (1 + FREE)))
                            dve.wait_ge(h_kept, g * E + e + FREE)
                            nc.vector.tensor_tensor(
                                e_pre[:, :, :], t_ps[:, 0, 1, :].rearrange("p (t c) -> p t c", c=C),
                                e_b[:, 0, bass.ds(e, 1), :].broadcast_to([P, MT, C]), ALU.add).then_inc(pre_kept, 1)
                            dve.wait_ge(y_ready, g * E + (e + (1 + FREE)))
                            nc.vector.tensor_tensor(
                                e_y[:, :, :], t_ps[:, 1, 1, :].rearrange("p (t c) -> p t c", c=C),
                                e_b[:, 1, bass.ds(e, 1), :].broadcast_to([P, MT, C]), ALU.add).then_inc(y_kept, 1)
                            dve.wait_ge(y_kept, g * E + (e + (1 + FREE)))
                            for t in range(MT):
                                nc.vector.scalar_tensor_tensor(
                                    out=e_acc[:, t, :], in0=e_y[:, t, :],
                                    scalar=weight[:, bass.ds(g * MT + t, 1), bass.ds(e, 1)].rearrange(
                                        "p t e -> p (t e)"),
                                    in1=e_acc[:, t, :], op0=ALU.mult, op1=ALU.add).then_inc(acc_kept, 1)
                            dve.wait_ge(acc_kept, g * (E * MT) + e * MT + MT)
                        dve.wait_ge(e_x_loaded, g * 16 + 16)
                        nc.vector.tensor_tensor(x_all[:, bass.ds(g * MT, MT), :], x_all[:, bass.ds(g * MT, MT), :],
                                                e_acc[:, :, :], ALU.add).then_inc(experts_done, 1)
                    dve.wait_ge(experts_done, TILES // MT + FREE)
                    with dve.Fori(0, GROUPS) as g:
                        measure(dve, Step(0, 0, 2, GROUPS), g, GROUPS)
                    dve.wait_ge(rstd_kept, GROUPS + 1)
                    dve.wait_ge(mean_kept, 2 * GROUPS)
                    with dve.Fori(0, TILES) as t:
                        tile = bass.ds(t, 1)
                        nc.vector.tensor_scalar(x_mid[:, tile, :].rearrange("p t c -> p (t c)"),
                                                x_all[:, tile, :].rearrange("p t c -> p (t c)"),
                                                mean[:, tile], rstd[:, tile], ALU.subtract, ALU.mult)\
                            .then_inc(ln_kept, 1)
                with dve.Else():
                    dve.nop()
                dve.nop()



NT = 64
TPC = 8
NC = NT // TPC
COMP = 32
GRID = 16
KNOTS = 8
W1, B1, W2, B2, DIR = 0, 2 * GRID, 3 * GRID, 4 * GRID, 4 * GRID + 1
TABLE = DIR + C
NS = NC + NT
AT_H = P - COMP
SG = 4
SPLINE_SLOTS = 4
SPLINE_DEPTH = 4


def spline_ffn(nc, mem, w, out_tiles):
    x_all, ident, ident_h = mem["x_all"], mem["ident"], mem["ident_h"]
    with ExitStack() as ctx:
        def sb(label, shape, dt=F32):
            return ctx.enter_context(nc.sbuf_tensor(f"ffn_{label}", shape, dt))

        def sem(label):
            return nc.alloc_semaphore(name=f"ffn_{label}")

        raw = sb("raw", [NT, C])
        rawT = sb("rawT", [P, NT])
        above = sb("above", [P, NT])
        below = sb("below", [P, NT])
        sums = sb("sums", [P, NC])
        sigs = sb("sigs", [P, P])
        knots = sb("knots", [P, KNOTS])
        rises = sb("rises", [P, KNOTS - 1])
        temp = sb("temp", [P, 1])
        cb1 = sb("cb1", [P, 1])
        cw2 = sb("cw2", [P, 32])
        cb2 = sb("cb2", [P, 2])
        table = sb("table", [P, TABLE])
        table_rest = sb("table_rest", [P, TABLE])
        table_hm = sb("table_hm", [P, TABLE], BF16)
        table_l = sb("table_l", [P, TABLE], BF16)
        gamma = sb("gamma", [P, C])
        beta = sb("beta", [P, C])
        out_scale = sb("out_scale", [P, 1])
        rank = sb("rank", [P, TPC])
        xs = sb("xs", [P, 2, SG, C])
        xT = sb("xT", [P, 2, SG * P])
        sT = sb("sT", [NS, 2, SG * P])
        hT = sb("hT", [P, 2, SG * P])
        compT = sb("compT", [P, 2, P])
        scores = sb("scores", [P, TILES, NS])
        comp = sb("comp", [P, TILES, 2])
        big = sb("big", [P, TILES, NT])
        onehot = sb("onehot", [P, TILES, 2, NT], BF16)
        value, pos, low, val, rise, equal, score, cluster, local = (
            sb(x, [P, TILES, TPC]) for x in ("value", "pos", "low", "val", "rise", "equal", "score", "cluster",
                                            "local"))
        top = sb("top", [P, TILES])
        ohT = sb("ohT", [P, SPLINE_SLOTS, SG * P], BF16)
        rows = sb("rows", [P, SPLINE_SLOTS, SG, TABLE])
        bent = sb("bent", [P, 2, SG, GRID])
        mag = sb("mag", [P, SG])
        y = sb("y", [P, SPLINE_SLOTS, SG, C])
        z = sb("z", [P, SPLINE_SLOTS, SG, C])
        x_beta = sb("x_beta", [P, SG, C])
        stats = sb("stats", [P, 2, SG, 6])
        mv = sb("mv", [P, 2, SPLINE_SLOTS, SG, 2])
        var = sb("var", [P, 2, SG])
        rstd = sb("rstd", [P, 2, SPLINE_SLOTS, SG])
        shift = sb("shift", [P, SPLINE_SLOTS, SG])

        loaded, consts, rawT_ready, chain, tables_kept = (
            sem(x) for x in ("loaded", "consts", "rawT_ready", "chain", "tables_kept"))
        xs_loaded = [sem(f"xs_loaded{j}") for j in range(2)]
        xT_ready, xT_kept, products_ready, h_kept, sT_kept = (
            sem(x) for x in ("xT_ready", "xT_kept", "products_ready", "h_kept", "sT_kept"))
        compT_ready, compT_kept, scores_ready, scores_kept = (
            sem(x) for x in ("compT_ready", "compT_kept", "scores_ready", "scores_kept"))
        pos_ready, exp_kept, comp_ready, comp_kept, cleared = (
            sem(x) for x in ("pos_ready", "exp_kept", "comp_ready", "comp_kept", "cleared"))
        LOADS = 10 + 2 * 5
        SPLINE_GROUPS = TILES // SG

        def scored(eng, step):
            pipeline(eng, step, 2, 5, SPLINE_GROUPS, 0)

        with nc.psum_tensor("ffn_t_ps", [P, 2, 512], F32) as t_ps, \
                nc.psum_tensor("ffn_p_ps", [P, 2, 512], F32) as p_ps, \
                nc.psum_tensor("ffn_c_ps", [P, 2, 512], F32) as c_ps, \
                nc.psum_tensor("ffn_s_ps", [P, 2, 512], F32) as s_ps, nc.Block() as block:

            COMP_AT = SG * NS

            @block.sync
            def _(sp):
                def wide(ap, n):
                    return bass.AP(ap.tensor, ap.offset, [[0, P], [1, n]])

                def column(ap):
                    return ap.rearrange("(n one) -> n one", one=1)

                sp.wait_ge(cleared, 2)
                for to, of in ((raw[:, :], w["L1_ffn_signatures_raw"]), (knots[:, :], wide(w["L1_ffn_knot_values"], KNOTS)),
                               (temp[:, :], wide(w["L1_ffn_temperature"], 1)),
                               (sigs[:, AT_H:P], w["L1_ffn_compress_w1"]),
                               (cb1[AT_H:P, :], column(w["L1_ffn_compress_b1"])),
                               (cw2[AT_H:P, 0:2], w["L1_ffn_compress_w2"]),
                               (cb2[:, :], wide(w["L1_ffn_compress_b2"], 2)),
                               (gamma[:, :], wide(w["L1_ffn_norm_gamma"], C)), (beta[:, :], wide(w["L1_ffn_norm_beta"], C)),
                               (out_scale[:, :], wide(w["L1_ffn_output_scale"], 1))):
                    sp.dma_start(to, of).then_inc(loaded, 16)
                for half in range(2):
                    rows_ = slice(half * NT, (half + 1) * NT)
                    for at, of in ((W1, w["L1_ffn_spline_w1"].rearrange("t i g -> t (i g)")), (B1, w["L1_ffn_spline_b1"]),
                                   (W2, w["L1_ffn_spline_w2"].rearrange("t g one -> t (g one)")),
                                   (B2, w["L1_ffn_spline_b2"]), (DIR, w["L1_ffn_directions"])):
                        sp.dma_start(table[rows_, at:at + of.shape[1]], of).then_inc(loaded, 16)

                def step(st):
                    if st.has(0):
                        j = st.slot(0)
                        wait(sp, xT_ready, st.seq(1))
                        sp.dma_start(xs[:, j, :, :], x_all[:, bass.ds(st.seq(0, SG), SG), :])\
                            .then_inc(xs_loaded[j], 16)

                scored(sp, step)

            @block.gpsimd
            def _(pool):
                nc.gpsimd.memset(sigs[:, NS:P], 0.0).then_inc(cleared, 1)
                nc.gpsimd.memset(cw2[:, :], 0.0).then_inc(cleared, 1)
                for e in range(TPC):
                    nc.gpsimd.memset(rank[:, e:e + 1], float(TPC - e)).then_inc(consts, 1)
                pool.wait_ge(consts, TPC)
                nc.gpsimd.memset(table_l[NT:P, :], 0.0).then_inc(consts, 1)

            @block.tensor
            def _(pe):
                pe.wait_ge(loaded, 16 * LOADS)
                nc.tensor.transpose(t_ps[:, 0, 0:NT], raw[:, :], ident[0:NT, 0:NT]).then_inc(rawT_ready, 1)

                def step(st):
                    if st.has(0):
                        j = st.slot(0)
                        pe.wait_ge(xs_loaded[j], st.turn(0))
                        wait(pe, xT_kept, st.seq(1))
                        for t in range(SG):
                            last = nc.tensor.transpose(t_ps[:, j, t * P:(t + 1) * P], xs[:, j, t, :], ident[:, :])
                        last.then_inc(xT_ready, 1)
                    if st.has(1):
                        j = st.slot(1)
                        pe.wait_ge(xT_kept, st.seq(1, c=1))
                        wait(pe, h_kept, st.seq(2))
                        wait(pe, sT_kept, st.seq(2))
                        nc.tensor.matmul(p_ps[:, j, :], sigs[:, :], xT[:, j, :], start=True, stop=True)\
                            .then_inc(products_ready, 1)
                    if st.has(2):
                        j = st.slot(2)
                        pe.wait_ge(h_kept, st.seq(2, c=1))
                        wait(pe, compT_kept, st.seq(3))
                        apart(pe, mem)
                        for t in range(SG):
                            last = nc.tensor.matmul(c_ps[32 * t:32 * t + 32, j, 0:P], cw2[AT_H:P, :],
                                                    hT[AT_H:P, j, t * P:(t + 1) * P], start=True, stop=True,
                                                    tile_position=(AT_H, 32 * t), skip_group_check=True)
                        last.then_inc(compT_ready, 1)
                    if st.has(3):
                        j = st.slot(3)
                        pe.wait_ge(sT_kept, st.seq(3, c=1))
                        pe.wait_ge(compT_kept, st.seq(3, c=1))
                        wait(pe, scores_kept, st.seq(4, 2))
                        for t in range(SG):
                            nc.tensor.transpose(s_ps[:, j, t * NS:(t + 1) * NS], sT[:, j, t * P:(t + 1) * P],
                                                ident[0:NS, 0:NS])
                        nc.tensor.transpose(s_ps[:, j, COMP_AT:COMP_AT + P], compT[:, j, :], ident[:, :])\
                            .then_inc(scores_ready, 1)

                pe.wait_ge(tables_kept, 1)
                scored(pe, step)

            @block.scalar
            def _(act):
                def step(st):
                    if st.has(0):
                        j = st.slot(0)
                        act.wait_ge(xT_ready, st.seq(0, c=1))
                        wait(act, products_ready, st.seq(1))
                        nc.scalar.copy(xT[:, j, :], t_ps[:, j, :]).then_inc(xT_kept, 1)
                    if st.has(1):
                        j = st.slot(1)
                        act.wait_ge(products_ready, st.seq(1, c=1))
                        wait(act, compT_ready, st.seq(2))
                        nc.scalar.activation(hT[AT_H:P, j, :], p_ps[AT_H:P, j, :], ACT.Gelu, bias=cb1[AT_H:P, :])\
                            .then_inc(h_kept, 1)
                    if st.has(2):
                        j = st.slot(2)
                        act.wait_ge(compT_ready, st.seq(2, c=1))
                        wait(act, scores_ready, st.seq(3))
                        nc.scalar.copy(compT[:, j, :], c_ps[:, j, 0:P]).then_inc(compT_kept, 1)

                scored(act, step)
                act.wait_ge(comp_ready, 1)
                nc.scalar.activation(comp[:, :, :], comp[:, :, :], ACT.Tanh).then_inc(comp_kept, 1)
                for k in range(2):
                    act.wait_ge(pos_ready, k + 1)
                    nc.scalar.activation(pos[:, :, :], value[:, :, :], ACT.Exp).then_inc(exp_kept, 1)

            @block.vector
            def _(dve):
                done = [0]

                def then(ins):
                    ins.then_inc(chain, 1)
                    done[0] += 1
                    dve.wait_ge(chain, done[0])

                dve.wait_ge(rawT_ready, 1)
                dve.wait_ge(consts, TPC + 1)
                then(nc.vector.tensor_copy(rawT[:, :], t_ps[:, 0, 0:NT]))
                then(nc.vector.tensor_scalar(above[:, :], rawT[:, :], 0.3, None, ALU.is_gt))
                then(nc.vector.tensor_scalar(below[:, :], rawT[:, :], -0.3, None, ALU.is_lt))
                then(nc.vector.tensor_tensor(above[:, :], above[:, :], below[:, :], ALU.subtract))
                then(nc.vector.tensor_tensor(above[:, :], above[:, :], rawT[:, :], ALU.subtract))
                then(nc.vector.tensor_tensor(sigs[:, NC:NS], rawT[:, :], above[:, :], ALU.add))
                by_tile = sigs[:, NC:NS].rearrange("p (c t) -> p t c", t=TPC)
                then(nc.vector.tensor_tensor(sums[:, :], by_tile[:, 0, :], by_tile[:, 1, :], ALU.add))
                for t in range(2, TPC):
                    then(nc.vector.tensor_tensor(sums[:, :], sums[:, :], by_tile[:, t, :], ALU.add))
                then(nc.vector.tensor_scalar(above[:, 0:NC], sums[:, :], 0.0, None, ALU.is_gt))
                then(nc.vector.tensor_scalar(below[:, 0:NC], sums[:, :], 0.0, None, ALU.is_lt))
                nc.vector.tensor_tensor(sigs[:, 0:NC], above[:, 0:NC], below[:, 0:NC], ALU.subtract)\
                    .then_inc(tables_kept, 1)
                then(nc.vector.tensor_tensor(rises[:, :], knots[:, 1:KNOTS], knots[:, 0:KNOTS - 1], ALU.subtract))
                then(nc.vector.tensor_scalar(temp[:, :], temp[:, :], 1e-6, None, ALU.add))
                then(nc.vector.reciprocal(temp[:, :], temp[:, :]))
                then(nc.vector.tensor_scalar(temp[:, :], temp[:, :], -1.0, None, ALU.mult))
                then(nc.vector.tensor_copy(table_hm[:, :], table[:, :]))
                then(nc.vector.tensor_tensor(table_rest[:, :], table[:, :], table_hm[:, :], ALU.subtract))
                then(nc.vector.tensor_copy(table_hm[NT:P, :], table_rest[NT:P, :]))
                then(nc.vector.tensor_copy(table_l[0:NT, :], table_rest[0:NT, :]))
                then(nc.vector.tensor_tensor(table_rest[0:NT, :], table_rest[0:NT, :], table_l[0:NT, :], ALU.subtract))
                then(nc.vector.tensor_copy(table_l[0:NT, :], table_rest[0:NT, :]))

                def step(st):
                    if st.has(3):
                        j, tiles = st.slot(3), bass.ds(st.seq(3, SG), SG)
                        dve.wait_ge(scores_ready, st.seq(3, c=1))
                        nc.vector.tensor_copy(scores[:, tiles, :].rearrange("p t n -> p (t n)"),
                                              s_ps[:, j, 0:COMP_AT]).then_inc(scores_kept, 1)
                        nc.vector.tensor_copy(comp[:, tiles, :], s_ps[:, j, COMP_AT:COMP_AT + P].rearrange(
                            "p (t m) -> p t m", m=32)[:, :, 0:2]).then_inc(scores_kept, 1)
                    if st.has(1):
                        j = st.slot(1)
                        dve.wait_ge(products_ready, st.seq(1, c=1))
                        wait(dve, scores_ready, st.seq(2))
                        nc.vector.tensor_copy(sT[:, j, :], p_ps[0:NS, j, :]).then_inc(sT_kept, 1)

                scored(dve, step)
                dve.wait_ge(scores_kept, 2 * SPLINE_GROUPS)
                nc.vector.tensor_tensor(comp[:, :, :], comp[:, :, :], cb2[:, :].unsqueeze(1).broadcast_to([P, TILES, 2]),
                                        ALU.add).then_inc(comp_ready, 1)

                def over(ap):
                    return ap.unsqueeze(2).broadcast_to([P, TILES, TPC])

                def calibrate(of, k):
                    nc.vector.tensor_scalar(value[:, :, :], of, temp[:, :], 88.0, ALU.mult, ALU.min)\
                        .then_inc(pos_ready, 1)
                    dve.wait_ge(exp_kept, k + 1)
                    then(nc.vector.tensor_scalar(pos[:, :, :], pos[:, :, :], 1.0, None, ALU.add))
                    then(nc.vector.reciprocal(pos[:, :, :], pos[:, :, :]))
                    then(nc.vector.tensor_scalar(pos[:, :, :], pos[:, :, :], float(KNOTS - 1), None, ALU.mult))
                    then(nc.vector.tensor_scalar(low[:, :, :], pos[:, :, :], 1.0, None, ALU.is_ge))
                    for n in range(2, KNOTS - 1):
                        then(nc.vector.scalar_tensor_tensor(out=low[:, :, :], in0=pos[:, :, :], scalar=float(n),
                                                            in1=low[:, :, :], op0=ALU.is_ge, op1=ALU.add))
                    then(nc.vector.tensor_tensor(pos[:, :, :], pos[:, :, :], low[:, :, :], ALU.subtract))
                    for n in range(KNOTS - 1):
                        then(nc.vector.tensor_scalar(equal[:, :, :], low[:, :, :], float(n), None, ALU.is_equal))
                        for to, by in ((val, knots), (rise, rises)):
                            if n == 0:
                                then(nc.vector.tensor_scalar(to[:, :, :], equal[:, :, :], by[:, 0:1], None, ALU.mult))
                            else:
                                then(nc.vector.scalar_tensor_tensor(
                                    out=to[:, :, :], in0=equal[:, :, :], scalar=by[:, n:n + 1], in1=to[:, :, :],
                                    op0=ALU.mult, op1=ALU.add))
                    then(nc.vector.tensor_tensor(rise[:, :, :], rise[:, :, :], pos[:, :, :], ALU.mult))
                    then(nc.vector.tensor_tensor(val[:, :, :], val[:, :, :], rise[:, :, :], ALU.add))

                def first_best(to):
                    then(nc.vector.tensor_reduce(top[:, :], val[:, :, :], AX_X, ALU.max))
                    then(nc.vector.tensor_tensor(equal[:, :, :], val[:, :, :], over(top[:, :]), ALU.is_equal))
                    then(nc.vector.tensor_tensor(score[:, :, :], equal[:, :, :],
                                                 rank[:, :].unsqueeze(1).broadcast_to([P, TILES, TPC]), ALU.mult))
                    then(nc.vector.tensor_reduce(top[:, :], score[:, :, :], AX_X, ALU.max))
                    then(nc.vector.tensor_tensor(to[:, :, :], score[:, :, :], over(top[:, :]), ALU.is_equal))

                calibrate(scores[:, :, 0:NC], 0)
                first_best(cluster)
                of_cluster = cluster[:, :, :].unsqueeze(3).broadcast_to([P, TILES, NC, TPC])
                then(nc.vector.tensor_tensor(big[:, :, :].rearrange("p n (c t) -> p n c t", c=NC),
                                             scores[:, :, NC:NS].rearrange("p n (c t) -> p n c t", c=NC),
                                             of_cluster, ALU.mult))
                then(nc.vector.tensor_reduce(score[:, :, :], big[:, :, :].rearrange("p n (c t) -> p n t c", c=NC),
                                             AX_X, ALU.add))
                calibrate(score[:, :, :], 1)
                first_best(local)
                for k in range(2):
                    then(nc.vector.tensor_tensor(onehot[:, :, k, :].rearrange("p n (c t) -> p n c t", c=NC), of_cluster,
                                                 local[:, :, :].unsqueeze(2).broadcast_to([P, TILES, NC, TPC]),
                                                 ALU.mult))

        ohT_ready, ohT_kept, rows_ready, rows_kept = (
            sem(x) for x in ("ohT_ready", "ohT_kept", "rows_ready", "rows_kept"))
        terms, bent_sum, hidden, mag_kept, y_kept = (
            sem(x) for x in ("terms", "bent_sum", "hidden", "mag_kept", "y_kept"))
        stats_kept, mv_kept, var_kept, rstd_kept = (
            [sem(f"{x}{k}") for k in range(2)] for x in ("stats_kept", "mv_kept", "var_kept", "rstd_kept"))
        norm_kept, x_beta_kept, scaled, z_kept, shift_kept, o_kept = (
            sem(x) for x in ("norm_kept", "x_beta_kept", "scaled", "z_kept", "shift_kept", "o_kept"))
        stored = sem("stored")

        def steps(eng, step):
            pipeline(eng, step, SPLINE_SLOTS, SPLINE_DEPTH, SPLINE_GROUPS, 0)

        with nc.psum_tensor("ffn_o_ps", [P, 2, 512], F32) as o_ps, \
                nc.psum_tensor("ffn_r_ps", [P, 2, 2, 512], F32) as r_ps, nc.Block() as block:

            @block.sync
            def _(sp):
                def step(st):
                    if st.has(3):
                        sp.wait_ge(o_kept, st.seq(3, SG, SG))
                        tiles = bass.ds(st.seq(3, SG), SG)
                        sp.dma_start(out_tiles[:, tiles, :], x_all[:, tiles, :]).then_inc(stored, 16)

                steps(sp, step)
                sp.wait_ge(stored, 16 * SPLINE_GROUPS)

            @block.tensor
            def _(pe):
                def step(st):
                    if st.has(0):
                        b = st.slot(0) % 2
                        wait(pe, ohT_kept, st.seq(2, c=1))
                        for t in range(SG):
                            last = nc.tensor.transpose(
                                o_ps[:, b, t * P // 2:(t + 1) * P // 2].bitcast(BF16),
                                onehot[:, bass.ds(st.seq(0, SG, t), 1), :, :].rearrange("p n k t -> p (n k t)"),
                                ident_h[:, :])
                        last.then_inc(ohT_ready, 1)
                        pe.wait_ge(ohT_kept, st.seq(0, c=1))
                        wait(pe, rows_kept, st.seq(2, 2, 2))
                        for t in range(SG):
                            to = r_ps[:, b, t // 2, t % 2 * TABLE:(t % 2 + 1) * TABLE]
                            one = ohT[:, st.slot(0), t * P:(t + 1) * P]
                            nc.tensor.matmul(to, one, table_hm[:, :], start=True, stop=False)
                            last = nc.tensor.matmul(to, one, table_l[:, :], start=False, stop=True)
                        last.then_inc(rows_ready, 1)

                steps(pe, step)

            @block.scalar
            def _(act):
                def step(st):
                    if st.has(0):
                        sl = st.slot(0)
                        act.wait_ge(ohT_ready, st.seq(0, c=1))
                        nc.scalar.copy(ohT[:, sl, :], o_ps[:, sl % 2, 0:SG * P // 2].bitcast(BF16)).then_inc(ohT_kept, 1)
                        act.wait_ge(rows_ready, st.seq(0, c=1))
                        wait(act, y_kept, st.seq(SPLINE_SLOTS, SG, SG))
                        for b in range(2):
                            nc.scalar.copy(rows[:, sl, 2 * b:2 * b + 2, :].rearrange("p t n -> p (t n)"),
                                           r_ps[:, sl % 2, b, 0:2 * TABLE]).then_inc(rows_kept, 1)
                    if st.has(3):
                        sl = st.slot(3)
                        act.wait_ge(shift_kept, st.seq(3, c=1))
                        for t in range(SG):
                            x = x_all[:, bass.ds(st.seq(3, SG, t), 1), :].rearrange("p t c -> p (t c)")
                            nc.scalar.activation(x, z[:, sl, t, :], ACT.Identity, bias=shift[:, sl, t:t + 1],
                                                 scale=rstd[:, 1, sl, t:t + 1]).then_inc(o_kept, 1)

                steps(act, step)

            @block.gpsimd
            def _(pool):
                def root(st, lag, k):
                    pool.wait_ge(var_kept[k], st.seq(lag, c=1))
                    nc.gpsimd.tensor_tensor(rstd[:, k, st.slot(lag), :], var[:, k, :], mem["minus_half"][:, 0:SG],
                                            ALU.pow).then_inc(rstd_kept[k], 1)

                def step(st):
                    if st.has(2):
                        sl = st.slot(2)
                        wait(pool, z_kept, st.seq(2))
                        nc.gpsimd.tensor_tensor(x_beta[:, :, :], x_all[:, bass.ds(st.seq(2, SG), SG), :],
                                                beta[:, :].unsqueeze(1).broadcast_to([P, SG, C]), ALU.add)\
                            .then_inc(x_beta_kept, 1)
                    if st.has(3):
                        root(st, 3, 1)
                    if st.has(2):
                        pool.wait_ge(norm_kept, st.seq(2, SG, SG))
                        nc.gpsimd.tensor_tensor(z[:, sl, :, :], z[:, sl, :, :],
                                                gamma[:, :].unsqueeze(1).broadcast_to([P, SG, C]), ALU.mult)\
                            .then_inc(scaled, 1)
                        pool.wait_ge(scaled, st.seq(2, c=1))
                        pool.wait_ge(x_beta_kept, st.seq(2, c=1))
                        nc.gpsimd.tensor_tensor(z[:, sl, :, :], z[:, sl, :, :], x_beta[:, :, :], ALU.add)\
                            .then_inc(z_kept, 1)
                    if st.has(1):
                        root(st, 1, 0)

                steps(pool, step)

            @block.vector
            def _(dve):
                def measure(st, lag, k, of):
                    for t in range(SG):
                        nc.vector.bn_stats(stats[:, k, t, :], of[:, st.slot(lag), t, :]).then_inc(stats_kept[k], 1)
                    dve.wait_ge(stats_kept[k], st.seq(lag, SG, SG))
                    apart(dve, mem)
                    for t in range(SG):
                        nc.vector.bn_aggr(mv[:, k, st.slot(lag), t, :], stats[:, k, t, :]).then_inc(mv_kept[k], 1)
                    dve.wait_ge(mv_kept[k], st.seq(lag, SG, SG))
                    wait(dve, rstd_kept[k], st.seq(lag))
                    nc.vector.tensor_scalar(var[:, k, :], mv[:, k, st.slot(lag), :, 1], EPS, None, ALU.add)\
                        .then_inc(var_kept[k], 1)

                def bend(st):
                    sl = st.slot(1)
                    dve.wait_ge(rows_kept, st.seq(1, 2, 2))
                    for k in range(2):
                        nc.vector.tensor_tensor(bent[:, k, :, :], rows[:, sl, :, W1 + k * GRID:W1 + (k + 1) * GRID],
                                                comp[:, bass.ds(st.seq(1, SG), SG), k:k + 1].broadcast_to([P, SG, GRID]),
                                                ALU.mult).then_inc(terms, 1)
                    dve.wait_ge(terms, st.seq(1, 2, 2))
                    nc.vector.tensor_tensor(bent[:, 0, :, :], bent[:, 0, :, :], bent[:, 1, :, :], ALU.add)\
                        .then_inc(bent_sum, 1)
                    dve.wait_ge(bent_sum, st.seq(1, 2, 1))
                    nc.vector.tensor_tensor(bent[:, 0, :, :], bent[:, 0, :, :], rows[:, sl, :, B1:B1 + GRID], ALU.add)\
                        .then_inc(bent_sum, 1)
                    dve.wait_ge(bent_sum, st.seq(1, 2, 2))
                    nc.vector.scalar_tensor_tensor(out=bent[:, 1, :, :], in0=bent[:, 0, :, :], scalar=0.0,
                                                   in1=rows[:, sl, :, W2:W2 + GRID], op0=ALU.max, op1=ALU.mult)\
                        .then_inc(hidden, 1)
                    dve.wait_ge(hidden, st.seq(1, c=1))
                    nc.vector.tensor_reduce(mag[:, :], bent[:, 1, :, :], AX_X, ALU.add).then_inc(mag_kept, 1)
                    dve.wait_ge(mag_kept, st.seq(1, 3, 1))
                    nc.vector.tensor_tensor(mag[:, :], mag[:, :], rows[:, sl, :, B2], ALU.add).then_inc(mag_kept, 1)
                    dve.wait_ge(mag_kept, st.seq(1, 3, 2))
                    nc.vector.tensor_scalar(mag[:, :], mag[:, :], out_scale[:, :], None, ALU.mult).then_inc(mag_kept, 1)
                    dve.wait_ge(mag_kept, st.seq(1, 3, 3))
                    for t in range(SG):
                        nc.vector.scalar_tensor_tensor(
                            out=y[:, sl, t, :], in0=rows[:, sl, t, DIR:TABLE], scalar=mag[:, t:t + 1],
                            in1=x_all[:, bass.ds(st.seq(1, SG, t), 1), :].rearrange("p t c -> p (t c)"),
                            op0=ALU.mult, op1=ALU.add).then_inc(y_kept, 1)
                    dve.wait_ge(y_kept, st.seq(1, SG, SG))

                def normalise(st):
                    sl = st.slot(2)
                    dve.wait_ge(rstd_kept[0], st.seq(2, c=1))
                    wait(dve, o_kept, st.seq(SPLINE_DEPTH, SG, SG))
                    for t in range(SG):
                        nc.vector.tensor_scalar(z[:, sl, t, :], y[:, sl, t, :], mv[:, 0, sl, t, 0:1],
                                                rstd[:, 0, sl, t:t + 1], ALU.subtract, ALU.mult).then_inc(norm_kept, 1)

                def measure_z(st):
                    dve.wait_ge(z_kept, st.seq(3, c=1))
                    measure(st, 3, 1, z)

                def shifts(st):
                    sl = st.slot(3)
                    dve.wait_ge(rstd_kept[1], st.seq(3, c=1))
                    nc.vector.scalar_tensor_tensor(out=shift[:, sl, :], in0=mv[:, 1, sl, :, 0], scalar=-1.0,
                                                   in1=rstd[:, 1, sl, :], op0=ALU.mult, op1=ALU.mult)\
                        .then_inc(shift_kept, 1)

                def step(st):
                    if st.has(3):
                        measure_z(st)
                    if st.has(2):
                        normalise(st)
                    if st.has(1):
                        bend(st)
                        measure(st, 1, 0, y)
                    if st.has(3):
                        shifts(st)

                steps(dve, step)



def prepare(nc, mem, w):
    with ExitStack() as ctx:
        def sb(label, shape, dt=F32):
            return ctx.enter_context(nc.sbuf_tensor(f"prep_{label}", shape, dt))

        def sem(label):
            return nc.alloc_semaphore(name=f"prep_{label}")

        w_raw = [sb(f"w_raw{n}", [P, 3, C]) for n in range(2)]
        a_T = sb("a_T", [R, 2, D])
        b_r = sb("b_r", [R, 2, D])
        a_rep = sb("a_rep", [R, 2, H, D])
        b_rep = sb("b_rep", [R, 2, H, D])
        b_col = sb("b_col", [P, 2])
        bv_wide = sb("bv_wide", [P, P])
        diagonal = sb("diagonal", [P, P])
        lora = sb("lora", [P, 2, P])
        lora_diag = sb("lora_diag", [P, 2, P])
        g_q = sb("g_q", [P, P])
        g_v = sb("g_v", [P, P])
        wT = sb("wT", [P, 2, P])
        ps = ctx.enter_context(nc.psum_tensor("prep_ps", [P, 4, 512], F32))

        loaded, consts, zeroed, masked = sem("loaded"), sem("consts"), sem("zeroed"), sem("masked")
        repeated, lora_ready, lora_kept, diag_kept, folded = (
            sem(x) for x in ("repeated", "lora_ready", "lora_kept", "diag_kept", "folded"))
        wT_ready, wT_kept, new_ready, new_kept = (sem(x) for x in ("wT_ready", "wT_kept", "new_ready", "new_kept"))
        ALL = 1 + 4 + 2 + D + 6
        block = ctx.enter_context(nc.Block())

        @block.sync
        def _(sp):
            sp.dma_start(w_raw[0][:, :, :], w["L0_attn_w_qkv"].rearrange("c (s f) -> c s f", s=3)).then_inc(loaded, 16)
            for s, k in enumerate(("q", "v")):
                sp.dma_start(a_T[:, s, :], w[f"L0_attn_a_{k}"].rearrange("d r -> r d"),
                             allow_slow_non_contiguous=True).then_inc(loaded, 16)
                sp.dma_start(b_r[:, s, :], w[f"L0_attn_b_{k}"]).then_inc(loaded, 16)
            bias = w["L0_attn_b_qkv"].rearrange("(s f one) -> s f one", s=3, one=1)
            sp.dma_start(b_col[:, 0:1], bias[0]).then_inc(loaded, 16)
            sp.dma_start(b_col[:, 1:2], bias[2]).then_inc(loaded, 16)
            perm = w["L0_attn_b_qkv"].rearrange("(s h d one) -> s d h one", s=3, d=D, one=1)
            for d in range(D):
                sp.dma_start(mem["bqk0"][H * d:H * (d + 1), 1:2], perm[1, d],
                             allow_slow_non_contiguous=True).then_inc(loaded, 16)
            sp.dma_start(mem["wo0"][:, :], w["L0_attn_w_proj"]).then_inc(loaded, 16)
            bo = w["L0_attn_b_proj"]
            sp.dma_start(mem["bo0"][:, :], bass.AP(bo.tensor, bo.offset, [[0, P], [1, C]])).then_inc(loaded, 16)
            sp.dma_start(w_raw[1][:, :, :], w["L1_attn_w_qkv"].rearrange("c (s f) -> c s f", s=3)).then_inc(loaded, 16)
            for k in ("cos", "sin"):
                sp.dma_start(mem[k][:, :], w[k]).then_inc(loaded, 16)
            sp.dma_start(mem["wo1"][:, :], w["L1_attn_w_proj"]).then_inc(loaded, 16)
            sp.wait_ge(loaded, 16 * ALL)



        @block.gpsimd
        def _(pool):
            for t in (mem["ident"], mem["ident_h"], mem["mask_qk"], mem["mask_kq"]):
                nc.gpsimd.memset(t[:], 0.0).then_inc(zeroed, 1)
            nc.gpsimd.memset(diagonal[:, :], 1.0).then_inc(zeroed, 1)
            nc.gpsimd.memset(mem["minus_half"][:, :], -0.5).then_inc(consts, 1)
            pool.wait_ge(zeroed, 5)
            for t in (mem["ident"], mem["ident_h"]):
                nc.gpsimd.affine_select(out=t[:, :], in_=t[:, :], compare_op=ALU.not_equal, fill=1.0, base=0,
                                        pattern=[[-1, P]], channel_multiplier=1).then_inc(consts, 1)
            nc.gpsimd.affine_select(out=mem["mask_qk"][:], in_=mem["mask_qk"][:], compare_op=ALU.is_ge, fill=MASKED,
                                    base=0, pattern=[[0, 2], [-1, P]], channel_multiplier=1).then_inc(consts, 1)
            nc.gpsimd.affine_select(out=mem["mask_kq"][:], in_=mem["mask_kq"][:], compare_op=ALU.is_ge, fill=MASKED,
                                    base=0, pattern=[[0, 2], [1, P]], channel_multiplier=-1).then_inc(consts, 1)
            nc.gpsimd.affine_select(out=diagonal[:, :], in_=diagonal[:, :], compare_op=ALU.is_ge, fill=0.0,
                                    base=0, pattern=[[-D, H], [0, D]], channel_multiplier=1).then_inc(masked, 1)
            pool.wait_ge(masked, 1)
            nc.gpsimd.affine_select(out=diagonal[:, :], in_=diagonal[:, :], compare_op=ALU.is_ge, fill=0.0,
                                    base=D - 1, pattern=[[D, H], [0, D]], channel_multiplier=-1).then_inc(consts, 1)

        @block.vector
        def _(dve):
            dve.wait_ge(loaded, 16 * ALL)
            for s in range(2):
                nc.vector.tensor_copy(a_rep[:, s, :, :], a_T[:, s, :].unsqueeze(1).broadcast_to([R, H, D]))\
                    .then_inc(repeated, 1)
                nc.vector.tensor_copy(b_rep[:, s, :, :], b_r[:, s, :].unsqueeze(1).broadcast_to([R, H, D]))\
                    .then_inc(repeated, 1)
            nc.vector.tensor_copy(bv_wide[:, :], b_col[:, 1:2].broadcast_to([P, P])).then_inc(repeated, 1)
            heads_last = "p (h d) -> p d h"
            for to, of in ((mem["wqk0"][:, 1, :], w_raw[0][:, 1, :]), (mem["wqk1"][:, 0, :], w_raw[1][:, 0, :]),
                           (mem["wqk1"][:, 1, :], w_raw[1][:, 1, :])):
                nc.vector.tensor_copy(to.rearrange("p (d h) -> p d h", d=D), of.rearrange(heads_last, d=D))\
                    .then_inc(repeated, 1)
            nc.vector.tensor_copy(mem["wv1"][:, :], w_raw[1][:, 2, :]).then_inc(repeated, 1)
            dve.wait_ge(consts, 6)
            dve.wait_ge(lora_ready, 1)
            for s in range(2):
                nc.vector.scalar_tensor_tensor(out=lora[:, s, :], in0=ps[:, s, 0:P], scalar=LORA_SCALE,
                                               in1=diagonal[:, :], op0=ALU.mult, op1=ALU.mult).then_inc(lora_kept, 1)
            dve.wait_ge(lora_kept, 2)
            nc.vector.tensor_tensor(g_q[:, :].rearrange("p (d h) -> p d h", d=D),
                                    lora[:, 0, :].rearrange(heads_last, d=D),
                                    mem["ident"][:, :].rearrange(heads_last, d=D), ALU.add).then_inc(folded, 1)
            nc.vector.tensor_tensor(g_v[:, :], lora[:, 1, :], mem["ident"][:, :], ALU.add).then_inc(folded, 1)
            dve.wait_ge(wT_ready, 1)
            for s in range(2):
                nc.vector.tensor_copy(wT[:, s, :], ps[:, 2, s * P:(s + 1) * P]).then_inc(wT_kept, 1)
            dve.wait_ge(new_ready, 1)
            for to, of in ((mem["wqk0"][:, 0, :], ps[:, 3, 0:P]), (mem["wv0"][:, :], ps[:, 3, P:2 * P]),
                           (mem["bv0"][:, :], ps[:, 3, 2 * P:3 * P]), (mem["bqk0"][:, 0:1], ps[:, 3, 3 * P:3 * P + 1])):
                nc.vector.tensor_copy(to, of).then_inc(new_kept, 1)

        @block.tensor
        def _(pe):
            pe.wait_ge(repeated, 9)
            for s in range(2):
                last = nc.tensor.matmul(ps[:, s, 0:P], a_rep[:, s, :, :].rearrange("r h d -> r (h d)"),
                                        b_rep[:, s, :, :].rearrange("r h d -> r (h d)"), start=True, stop=True)
            last.then_inc(lora_ready, 1)
            pe.wait_ge(consts, 6)
            for s, of in enumerate((0, 2)):
                last = nc.tensor.transpose(ps[:, 2, s * P:(s + 1) * P], w_raw[0][:, of, :], mem["ident"][:, :])
            last.then_inc(wT_ready, 1)
            pe.wait_ge(folded, 2)
            pe.wait_ge(wT_kept, 2)
            nc.tensor.matmul(ps[:, 3, 0:P], wT[:, 0, :], g_q[:, :], start=True, stop=True)
            nc.tensor.matmul(ps[:, 3, P:2 * P], wT[:, 1, :], g_v[:, :], start=True, stop=True)
            nc.tensor.matmul(ps[:, 3, 2 * P:3 * P], bv_wide[:, :], g_v[:, :], start=True, stop=True)
            nc.tensor.matmul(ps[:, 3, 3 * P:3 * P + 1], g_q[:, :], b_col[:, 0:1], start=True, stop=True)\
                .then_inc(new_ready, 1)

        @block.scalar
        def _(act):
            for g in range(8):
                n = TILES // 8
                act.dma_start(mem["x_all"][:, g * n:(g + 1) * n, :], w["x_tiles"][:, g * n:(g + 1) * n, :])\
                    .then_inc(mem["x_all_loaded"], 16)


def build(nc, w, out):
    with ExitStack() as ctx:
        def sb(label, shape, dt=F32):
            return ctx.enter_context(nc.sbuf_tensor(label, shape, dt))

        mem = {"x_all": sb("x_all", [P, TILES, C]), "x_mid": sb("x_mid", [P, TILES, C]),
               "ident": sb("ident", [P, P]), "ident_h": sb("ident_h", [P, P], BF16),
               "mask_qk": sb("mask_qk", [P, 2, P], BF16), "mask_kq": sb("mask_kq", [P, 2, P], BF16),
               "cos": sb("cos", [P, N]), "sin": sb("sin", [P, N]),
               "minus_half": sb("minus_half", [P, TILES])}
        for n in range(2):
            mem |= {f"wqk{n}": sb(f"wqk{n}", [P, 2, P]), f"wv{n}": sb(f"wv{n}", [P, C]), f"wo{n}": sb(f"wo{n}", [P, C])}
        mem |= {"bqk0": sb("bqk0", [P, 2]), "bv0": sb("bv0", [P, C]), "bo0": sb("bo0", [P, C])}
        mem["apart"] = ctx.enter_context(nc.semaphore("apart"))
        mem["x_all_loaded"] = ctx.enter_context(nc.semaphore("x_all_loaded"))
        w = dict(w, x_tiles=w["L0_attn_x"].rearrange("b (t p) c -> p (b t) c", p=P))
        prepare(nc, mem, w)

        def layer(n):
            return mem | {k: mem.get(f"{k}{n}") for k in ("wqk", "wv", "wo", "bqk", "bv", "bo")}

        out_tiles = out.rearrange("b (t p) c -> p (b t) c", p=P)
        snap = nc.snapshot_sems()
        attention(nc, "attn0", layer(0), False, w["x_tiles"], True, False)
        nc.clear_and_free_semaphores(nc.allocated_since(snap))
        nc.all_engine_barrier()
        moe(nc, mem, w)
        mem["x_all"] = mem["x_mid"]
        attention(nc, "attn1", layer(1), True, None, False, True)
        spline_ffn(nc, mem, w, out_tiles)


def rotary_tables():
    half = D // 2
    theta = (1.0 / 10000.0 ** (np.arange(half, dtype=np.float32) / np.float32(half))).astype(np.float32)
    freqs = np.arange(N, dtype=np.float32)[:, None] * theta[None, :]
    cos, sin = (np.repeat(np.repeat(f(freqs).astype(np.float32), 2, axis=1).T, H, axis=0) for f in (np.cos, np.sin))
    sin[:P // 2] *= -1
    return np.ascontiguousarray(cos), np.ascontiguousarray(sin)



def kernel(**inputs):
    import concourse.bacc as _bacc
    from concourse import mybir as _mybir
    from concourse.bass_utils import run_bass_kernel_spmd as _run

    nc = _bacc.Bacc("TRN2", target_bir_lowering=False, num_devices=1)
    inputs = {k: np.ascontiguousarray(v) for k, v in inputs.items()}
    inputs["cos"], inputs["sin"] = rotary_tables()
    arrays = {f"in_{k}_dram": v for k, v in inputs.items()}
    w = {k: nc.dram_tensor(f"in_{k}_dram", v.shape, _mybir.dt.from_np(v.dtype), kind="ExternalInput").ap()
         for k, v in inputs.items()}
    out = nc.dram_tensor("out_0_dram", (B, N, C), _mybir.dt.float32, kind="ExternalOutput").ap()
    build(nc, w, out)
    r = _run(nc, [arrays], core_ids=[0])
    return r.results[0]["out_0_dram"]
```

```python
from contextlib import ExitStack

import concourse.bass as bass
import numpy as np
from concourse import mybir

F32 = mybir.dt.float32
BF16 = mybir.dt.bfloat16
I32 = mybir.dt.int32
ALU = mybir.AluOpType
ACT = mybir.ActivationFunctionType
AX_X = mybir.AxisListType.X

P = 128
B, N, C = 32, 256, 128
H, D = 16, 8
R = 16
TILES = B * N // P
TB = N // P
LORA_SCALE = 32.0 / R
EPS = 1e-5
MASKED = -1e30

PARTS = 3
KROWS = PARTS * PARTS * D
MROWS = 2
NH = H // 2
SLOTS = 3
AT = {"attn0": dict(act_xT=0, act_mT1=1, act_qk=2, act_oT=3, act_onT=8, act_mT0=11,
                    dve_o=6, dve_split0=8, dve_v=7, dve_y=13, dve_var=14, dve_ln=15,
                    pe_xT=0, pe_mT1=2, pe_pv3=3, pe_qk=2, pe_oT=5, pe_pv=6, pe_v=4, pe_onT=8, pe_mT0=10, pe_y=13),
      "attn1": dict(act_xT=0, act_mT1=0, act_qk=1, act_oT=2, act_onT=10, act_mT0=11,
                    dve_o=3, dve_split0=9, dve_v=5, dve_y=12, dve_var=14, dve_ln=15,
                    pe_xT=0, pe_mT1=1, pe_pv3=2, pe_qk=1, pe_oT=4, pe_pv=6, pe_v=3, pe_onT=10, pe_mT0=11, pe_y=12)}
DEPTH = 5


def strided(ap, dims):
    return bass.AP(ap.tensor, ap.offset, [list(ap.ap[0])] + dims)


class Step:

    def __init__(self, i, off, slots, total):
        self.i, self.off, self.slots, self.total, self.loop = i, off, slots, total, not isinstance(i, int)

    def has(self, lag):
        return self.loop or 0 <= self.off - lag < self.total

    def seq(self, lag, k=1, c=0):
        return self.i * (self.slots * k) + (k * (self.off - lag) + c)

    def slot(self, lag):
        return (self.off - lag) % self.slots

    def turn(self, lag, k=16, c=0):
        return self.i * k + (k * ((self.off - lag) // self.slots + 1) + c)


def apart(eng, mem):
    eng.sem_inc(mem["apart"], 1)


def wait(eng, sem, value):
    if not isinstance(value, int) or value > 0:
        eng.wait_ge(sem, value)


def pipeline(eng, step, slots=SLOTS, depth=DEPTH, total=B, ahead=1):
    first = depth
    loops = (total - ahead - first) // slots
    for s in range(first):
        step(Step(0, s, slots, total))
    with eng.Fori(0, loops) as i:
        for r in range(slots):
            step(Step(i, first + r, slots, total))
    for s in range(first + slots * loops, total + depth - 1):
        step(Step(0, s, slots, total))


def attention(nc, name, mem, causal, x_dram, lora, rope):
    at = AT[name]
    x_all, wqk, wv, wo, bqk, bv, bo = (mem[k] for k in ("x_all", "wqk", "wv", "wo", "bqk", "bv", "bo"))
    ident, ident_h, mask_qk, mask_kq = (mem[k] for k in ("ident", "ident_h", "mask_qk", "mask_kq"))
    scale = float(D) ** -0.5
    W = N // 2 + N if causal else 2 * N
    QKOPS = 4 if rope else 2

    with ExitStack() as ctx:
        def sb(label, shape, dt=F32):
            return ctx.enter_context(nc.sbuf_tensor(f"{name}_{label}", shape, dt))

        def sem(label):
            return nc.alloc_semaphore(name=f"{name}_{label}")

        scratch = nc.dram_tensor(f"{name}_scratch", (SLOTS, 2, PARTS, P, N), BF16, kind="Internal").ap()
        x_in = sb("x_in", [P, SLOTS, TB, C])
        xT = sb("xT", [P, SLOTS, N])
        qk = sb("qk", [P, 2, N])
        q_half = sb("q_half", [P, 2, N]) if rope else None
        rest = sb("rest", [P, 2, N])
        parts = sb("parts", [P, 2, PARTS, N], BF16)
        q_st = sb("q_st", [P, SLOTS, H, N], BF16)
        k_st = sb("k_st", [P, SLOTS, H, N], BF16)
        negmax = sb("negmax", [P, TB, H])
        mparts = sb("mparts", [P, 2, TB, MROWS, NH], BF16)
        mT_sb = sb("mT_sb", [MROWS * NH, 2, N], BF16)
        v_sb = sb("v_sb", [P, SLOTS, TB, H * 32])
        probs = sb("probs", [P, 2, 4, 2 * N])
        oT_sb = sb("oT_sb", [P, 2 * N])
        rden = sb("rden", [P, TB, H])
        o_sb = sb("o_sb", [P, TB, C])
        onT_sb = sb("onT_sb", [P, N])
        x_res = sb("x_res", [P, TB, C])
        y_sb = sb("y_sb", [P, TB, C])
        stats = sb("stats", [P, TB, 6])
        mv = sb("mv", [P, TB, 2])
        var = sb("var", [P, TB])
        rstd = sb("rstd", [P, TB])

        row_ps = ctx.enter_context(nc.psum_tensor(f"{name}_row_ps", [P, 3, 512], F32))
        col_ps = ctx.enter_context(nc.psum_tensor(f"{name}_col_ps", [P, 2, 512], F32))
        out_ps = ctx.enter_context(nc.psum_tensor(f"{name}_out_ps", [P, 512], F32))
        in_ps = ctx.enter_context(nc.psum_tensor(f"{name}_in_ps", [P, 512], F32))
        fin_ps = ctx.enter_context(nc.psum_tensor(f"{name}_fin_ps", [P, 512], F32))

        x_loaded = [sem(f"x_loaded{j}") for j in range(SLOTS)]
        parts_stored = [sem(f"parts_stored{j}") for j in range(SLOTS)]
        q_stacked = [sem(f"q_stacked{j}") for j in range(SLOTS)]
        k_stacked = [sem(f"k_stacked{j}") for j in range(SLOTS)]
        m_placed = [[sem(f"m_placed{g}{j}") for j in range(SLOTS)] for g in range(2)]
        xT_ready, qk_ready, v_ready, rows_ready, mT_ready, cols_ready, pv_ready, o_ready, onT_ready, y_ready = (
            sem(x) for x in ("xT_ready", "qk_ready", "v_ready", "rows_ready", "mT_ready", "cols_ready", "pv_ready",
                             "o_ready", "onT_ready", "y_ready"))
        xT_kept, qk_kept, v_kept, max_kept, mhi_kept, mparts_kept, mT_kept, probs_kept, oT_kept = (
            sem(x) for x in ("xT_kept", "qk_kept", "v_kept", "max_kept", "mhi_kept", "mparts_kept", "mT_kept",
                             "probs_kept", "oT_kept"))
        rden_kept, o_kept, onT_kept, y_kept, stats_kept, mv_kept, x_res_kept, var_kept, rstd_kept, ln_kept = (
            sem(x) for x in ("rden_kept", "o_kept", "onT_kept", "y_kept", "stats_kept", "mv_kept", "x_res_kept",
                             "var_kept", "rstd_kept", "ln_kept"))
        cos_done, sin_done, turned = (sem(x) for x in ("cos_done", "sin_done", "turned"))
        hi_kept, rest_kept, mid_kept, lo_kept = (sem(x) for x in ("hi_kept", "rest_kept", "mid_kept", "lo_kept"))
        v_cleared, k_ones = sem("v_cleared"), sem("k_ones")
        block = ctx.enter_context(nc.Block())

        def head(n):
            u, j = n // 4, n % 4
            return NH * (u // 2) + 2 * j + u % 2

        UNITS, ROW_BANKS = NH * TB, 3

        def row_bank(st, u):
            return (UNITS * st.off + u) % ROW_BANKS

        @block.sync
        def _(sp):
            def load_x(st, lag):
                wait(sp, xT_ready, st.seq(lag, c=1 - SLOTS))
                src = x_all[:, bass.ds(st.seq(lag, TB), TB), :] if x_dram is None else \
                    x_dram[:, bass.ds(st.seq(lag, TB), TB), :]
                sp.dma_start(x_in[:, st.slot(lag), :, :], src).then_inc(x_loaded[st.slot(lag)], 16)

            def step(st):
                if st.has(-1):
                    load_x(st, -1)
                if st.has(3):
                    sp.wait_ge(mT_kept, st.seq(3, 2, 2))
                    sl = st.slot(3)
                    sp.dma_start(q_st[KROWS:KROWS + MROWS, sl, NH:H, :], mT_sb[:, 1, :]).then_inc(m_placed[1][sl], 16)
                if st.has(0):
                    sl = st.slot(0)
                    sp.wait_ge(lo_kept, st.seq(0, c=1))
                    apart(sp, mem)
                    wait(sp, q_stacked[sl], st.turn(SLOTS, 48))
                    apart(sp, mem)
                    wait(sp, k_stacked[sl], st.turn(SLOTS, 16))
                    sp.dma_start(scratch[sl].rearrange("s j p n -> p (s j) n"),
                                 parts[:, :, :, :].rearrange("p s j n -> p (s j) n")).then_inc(parts_stored[sl], 16)
                if st.has(2):
                    sp.wait_ge(mT_kept, st.seq(2, 2, 1))
                    sl = st.slot(2)
                    sp.dma_start(q_st[KROWS:KROWS + MROWS, sl, 0:NH, :], mT_sb[:, 0, :]).then_inc(m_placed[0][sl], 16)
                if st.has(0):
                    sl = st.slot(0)
                    sp.wait_ge(k_ones, 1)
                    sp.wait_ge(parts_stored[sl], st.turn(0))
                    apart(sp, mem)
                    wait(sp, cols_ready, st.seq(SLOTS, H, H))
                    q_src = scratch[sl, 0].rearrange("j (d h) n -> j d (h n)", d=D)
                    k_src = scratch[sl, 1].rearrange("j (d h) n -> (j d) (h n)", d=D)
                    for j in range(PARTS):
                        rows = slice(PARTS * D * j, PARTS * D * (j + 1))
                        src = q_src[j]
                        thrice = bass.AP(src.tensor, src.offset, [[0, PARTS]] + [list(x) for x in src.ap])
                        sp.dma_start(q_st[rows, sl, :, :].rearrange("p h n -> p (h n)"), thrice)\
                            .then_inc(q_stacked[sl], 16)
                    thrice = bass.AP(k_src.tensor, k_src.offset, [[0, PARTS]] + [list(x) for x in k_src.ap])
                    sp.dma_start(k_st[0:KROWS, sl, :, :].rearrange("p h n -> p (h n)"), thrice)\
                        .then_inc(k_stacked[sl], 16)

            load_x(Step(0, 0, SLOTS, B), 0)
            pipeline(sp, step)

        @block.gpsimd
        def _(pool):
            nc.gpsimd.memset(k_st[64:96, :, :, :], 1.0).then_inc(k_ones, 1)
            pool.wait_ge(k_ones, 1)
            nc.gpsimd.memset(v_sb[:, :, :, :], 0.0).then_inc(v_cleared, 1)
            pool.wait_ge(v_cleared, 1)
            for a in range(2):
                one = v_sb[:, :, :, :].rearrange("p s t (q c) -> p (s t q) c", c=64)[:, :, 41 * a + D:41 * a + D + 1]
                nc.gpsimd.memset(one, 1.0).then_inc(v_cleared, 1)
            if x_dram is not None:
                pool.wait_ge(mem["x_all_loaded"], 16 * 4)

            def step(st):
                if st.has(4) and x_dram is not None:
                    wait(pool, y_kept, st.seq(4))
                    nc.gpsimd.tensor_tensor(x_res[:, :, :], x_all[:, bass.ds(st.seq(4, TB), TB), :],
                                            bo[:, :].unsqueeze(1).broadcast_to([P, TB, C]), ALU.add)\
                        .then_inc(x_res_kept, 1)
                if st.has(0):
                    pool.wait_ge(qk_kept, st.seq(0, QKOPS, QKOPS))
                    if rope:
                        pool.wait_ge(qk_kept, st.seq(0, QKOPS, QKOPS))
                        cos, sin = (mem[k][:, :].unsqueeze(1).broadcast_to([P, 2, N]) for k in ("cos", "sin"))
                        nc.gpsimd.tensor_tensor(q_half[:, :, :], q_half[:, :, :], sin, ALU.mult).then_inc(sin_done, 1)
                        nc.gpsimd.tensor_tensor(qk[:, :, :], qk[:, :, :], cos, ALU.mult).then_inc(cos_done, 1)
                        pool.wait_ge(sin_done, st.seq(0, c=1))
                        pool.wait_ge(cos_done, st.seq(0, c=1))
                        nc.gpsimd.tensor_tensor(qk[:, :, :], qk[:, :, :], q_half[:, :, :], ALU.add)\
                            .then_inc(turned, 1)
                        pool.wait_ge(turned, st.seq(0, c=1))
                    if st.has(1):
                        pool.wait_ge(parts_stored[st.slot(1)], st.turn(1))
                    apart(pool, mem)
                    nc.gpsimd.tensor_scalar(parts[:, :, 0, :], qk[:, :, :], 1.0, 0.0, ALU.mult, ALU.add)\
                        .then_inc(hi_kept, 1)
                    pool.wait_ge(hi_kept, st.seq(0, c=1))
                    nc.gpsimd.tensor_tensor(rest[:, :, :], qk[:, :, :], parts[:, :, 0, :], ALU.subtract)\
                        .then_inc(rest_kept, 1)
                    pool.wait_ge(rest_kept, st.seq(0, c=1))
                    apart(pool, mem)
                    nc.gpsimd.tensor_scalar(parts[:, :, 1, :], rest[:, :, :], 1.0, 0.0, ALU.mult, ALU.add)\
                        .then_inc(mid_kept, 1)
                    pool.wait_ge(mid_kept, st.seq(0, c=1))
                    nc.gpsimd.tensor_tensor(parts[:, :, 2, :], rest[:, :, :], parts[:, :, 1, :], ALU.subtract)\
                        .then_inc(lo_kept, 1)
                if st.has(4):
                    pool.wait_ge(var_kept, st.seq(4, c=1))
                    nc.gpsimd.tensor_tensor(rstd[:, :], var[:, :], mem["minus_half"][:, 0:TB], ALU.pow)\
                        .then_inc(rstd_kept, 1)

            pipeline(pool, step)

        @block.scalar
        def _(act):
            def step(st):
                for n in range(H):
                    if st.has(3):
                        u, j = n // 4, n % 4
                        act.wait_ge(cols_ready, st.seq(3, H, n + 1))
                        if j == 0:
                            wait(act, pv_ready, st.seq(3, 4, u - 1))
                        nc.scalar.activation(probs[:, u % 2, j, 0:W], col_ps[:, n % 2, 0:W], ACT.Exp,
                                             scale=scale).then_inc(probs_kept, 1)
                    if n == at["act_xT"] and st.has(0):
                        act.wait_ge(xT_ready, st.seq(0, c=1))
                        wait(act, v_ready, st.seq(SLOTS, c=1))
                        nc.scalar.copy(xT[:, st.slot(0), :], in_ps[:, 0:N]).then_inc(xT_kept, 1)
                    if n == at["act_mT1"] and st.has(3):
                        act.wait_ge(mT_ready, st.seq(3, 2, 2))
                        if st.has(4):
                            act.wait_ge(m_placed[1][st.slot(4)], st.turn(4))
                        nc.scalar.copy(mT_sb[:, 1, :], fin_ps[0:MROWS * NH, 0:N // 2].bitcast(BF16))\
                            .then_inc(mT_kept, 1)
                    if n == at["act_qk"] and st.has(0):
                        act.wait_ge(qk_ready, st.seq(0, c=1))
                        wait(act, rest_kept, st.seq(0))
                        if rope:
                            for to, of in ((0, P // 2), (P // 2, 0)):
                                nc.scalar.copy(q_half[to:to + P // 2, :, :].rearrange("p s n -> p (s n)"),
                                               in_ps[of:of + P // 2, :]).then_inc(qk_kept, 1)
                        for s in range(2):
                            if lora:
                                nc.scalar.activation(qk[:, s, :], in_ps[:, s * N:(s + 1) * N], ACT.Identity,
                                                     bias=bqk[:, s:s + 1]).then_inc(qk_kept, 1)
                            else:
                                nc.scalar.copy(qk[:, s, :], in_ps[:, s * N:(s + 1) * N]).then_inc(qk_kept, 1)
                    if n == at["act_oT"] and st.has(4):
                        act.wait_ge(pv_ready, st.seq(4, 4, 4))
                        wait(act, o_ready, st.seq(4))
                        nc.scalar.copy(oT_sb[:, :], out_ps[:, :]).then_inc(oT_kept, 1)
                    if n == at["act_onT"] and st.has(4):
                        act.wait_ge(onT_ready, st.seq(4, c=1))
                        wait(act, y_ready, st.seq(4))
                        nc.scalar.copy(onT_sb[:, :], fin_ps[:, 0:N]).then_inc(onT_kept, 1)
                    if n == at["act_mT0"] and st.has(2):
                        act.wait_ge(mT_ready, st.seq(2, 2, 1))
                        if st.has(3):
                            act.wait_ge(m_placed[0][st.slot(3)], st.turn(3))
                        nc.scalar.copy(mT_sb[:, 0, :], in_ps[0:MROWS * NH, 0:N // 2].bitcast(BF16))\
                            .then_inc(mT_kept, 1)

            pipeline(act, step)

        @block.vector
        def _(dve):
            def row_max(st, u):
                p, t = u // TB, u % TB
                if u % NH == 0:
                    wait(dve, mparts_kept, st.seq(2, 2, u // NH - 1))
                dve.wait_ge(rows_ready, st.seq(2, UNITS, u + 1))
                keys = (t + 1) * P if causal else N
                nc.vector.tensor_reduce(
                    negmax[:, t, 2 * p:2 * p + 2],
                    row_ps[:, row_bank(st, u), 0:2 * keys].rearrange("p (a k) -> p a k", a=2),
                    AX_X, ALU.max, negate=True).then_inc(max_kept, 1)

            def split_max(st, g):
                dve.wait_ge(max_kept, st.seq(2, UNITS, UNITS // 2 * (g + 1)))
                wait(dve, mT_ready, st.seq(3, 2, g + 1))
                half = negmax[:, :, NH * g:NH * (g + 1)]
                nc.vector.tensor_copy(mparts[:, g, :, 0, :], half).then_inc(mhi_kept, 1)
                dve.wait_ge(mhi_kept, st.seq(2, 2, g + 1))
                nc.vector.tensor_tensor(mparts[:, g, :, 1, :], half, mparts[:, g, :, 0, :], ALU.subtract)\
                    .then_inc(mparts_kept, 1)

            def keep_v(st):
                dve.wait_ge(v_ready, st.seq(2, c=1))
                wait(dve, pv_ready, st.seq(2 + SLOTS, 4, 4))
                dve.wait_ge(v_cleared, 3)
                for t in range(TB):
                    to = strided(v_sb[:, st.slot(2), t, 0:1], [[64, H // 2], [41, 2], [1, D]])
                    of = in_ps[:, t * C:(t + 1) * C].rearrange("p (q a d) -> p q a d", a=2, d=D)
                    if lora:
                        nc.vector.tensor_tensor(to, of, bv[:, :].rearrange("p (q a d) -> p q a d", a=2, d=D),
                                                ALU.add).then_inc(v_kept, 1)
                    else:
                        nc.vector.tensor_copy(to, of).then_inc(v_kept, 1)

            def normalise_o(st):
                dve.wait_ge(o_ready, st.seq(4, c=1))
                wait(dve, onT_ready, st.seq(4))
                nc.vector.reciprocal(rden[:, :, :].rearrange("p t (j a) -> p (t j) a", a=2),
                                     strided(fin_ps[:, D:D + 1], [[32, 2 * NH], [D + 1, 2]])).then_inc(rden_kept, 1)
                dve.wait_ge(rden_kept, st.seq(4, c=1))
                for t in range(TB):
                    nc.vector.tensor_tensor(
                        o_sb[:, t, :].rearrange("p (j a d) -> p j a d", a=2, d=D),
                        strided(fin_ps[:, 256 * t:256 * t + 1], [[32, NH], [D + 1, 2], [1, D]]),
                        rden[:, t, :].rearrange("p (j a) -> p j a", a=2).unsqueeze(3).broadcast_to([P, NH, 2, D]),
                        ALU.mult).then_inc(o_kept, 1)

            def add_residual(st):
                dve.wait_ge(y_ready, st.seq(4, c=1))
                if x_dram is not None:
                    dve.wait_ge(x_res_kept, st.seq(4, c=1))
                    x_old = x_res[:, :, :]
                else:
                    x_old = x_all[:, bass.ds(st.seq(4, TB), TB), :]
                nc.vector.tensor_tensor(y_sb[:, :, :], fin_ps[:, 0:N].rearrange("p (t c) -> p t c", t=TB), x_old,
                                        ALU.add).then_inc(y_kept, 1)
                dve.wait_ge(y_kept, st.seq(4, c=1))
                for t in range(TB):
                    nc.vector.bn_stats(stats[:, t, :], y_sb[:, t, :]).then_inc(stats_kept, 1)

            def variance(st):
                dve.wait_ge(stats_kept, st.seq(4, TB, TB))
                apart(dve, mem)
                for t in range(TB):
                    nc.vector.bn_aggr(mv[:, t, :], stats[:, t, :]).then_inc(mv_kept, 1)
                dve.wait_ge(mv_kept, st.seq(4, TB, TB))
                wait(dve, rstd_kept, st.seq(4))
                nc.vector.tensor_scalar(var[:, :], mv[:, :, 1], EPS, None, ALU.add).then_inc(var_kept, 1)

            def layer_norm(st):
                dve.wait_ge(rstd_kept, st.seq(4, c=1))
                for t in range(TB):
                    nc.vector.tensor_scalar(x_all[:, bass.ds(st.seq(4, TB, t), 1), :].rearrange("p t c -> p (t c)"),
                                            y_sb[:, t, :], mv[:, t, 0:1], rstd[:, t:t + 1],
                                            ALU.subtract, ALU.mult).then_inc(ln_kept, 1)

            def step(st):
                for n in range(H):
                    if st.has(2):
                        row_max(st, n)
                    if n == at["dve_o"] and st.has(4):
                        normalise_o(st)
                    if n == at["dve_split0"] and st.has(2):
                        split_max(st, 0)
                    if n == at["dve_v"] and st.has(2):
                        keep_v(st)
                    if n == at["dve_y"] and st.has(4):
                        add_residual(st)
                    if n == 15 and st.has(2):
                        split_max(st, 1)
                    if n == at["dve_var"] and st.has(4):
                        variance(st)
                    if n == at["dve_ln"] and st.has(4):
                        layer_norm(st)

            pipeline(dve, step)

        @block.tensor
        def _(pe):
            def transpose_x(st):
                pe.wait_ge(x_loaded[st.slot(0)], st.turn(0))
                if st.has(3):
                    pe.wait_ge(mT_kept, st.seq(3, 2, 1))
                elif st.has(1):
                    pe.wait_ge(qk_kept, st.seq(1, QKOPS, QKOPS))
                for t in range(TB):
                    last = nc.tensor.transpose(in_ps[:, t * P:(t + 1) * P], x_in[:, st.slot(0), t, :], ident[:, :])
                last.then_inc(xT_ready, 1)

            def transpose_max(st, lag, g):
                if g == 0:
                    pe.wait_ge(v_kept, st.seq(2, TB, TB))
                elif st.has(5):
                    pe.wait_ge(y_kept, st.seq(5, c=1))
                elif st.has(4):
                    pe.wait_ge(mT_kept, st.seq(4, 2, 2))
                pe.wait_ge(mparts_kept, st.seq(lag, 2, g + 1))
                for t in range(TB):
                    last = nc.tensor.transpose(
                        (fin_ps if g else in_ps)[0:MROWS * NH, t * P // 2:(t + 1) * P // 2].bitcast(BF16),
                        mparts[:, g, t, :, :].rearrange("p m h -> p (m h)"), ident_h[:, :])
                last.then_inc(mT_ready, 1)

            def project_qk(st):
                pe.wait_ge(xT_kept, st.seq(0, c=1))
                for s in range(2):
                    last = nc.tensor.matmul(in_ps[:, s * N:(s + 1) * N], wqk[:, s, :], xT[:, st.slot(0), :],
                                            start=True, stop=True)
                last.then_inc(qk_ready, 1)

            def transpose_o(st):
                if st.has(3):
                    pe.wait_ge(mT_kept, st.seq(3, 2, 2))
                elif st.has(5):
                    pe.wait_ge(y_kept, st.seq(5, c=1))
                pe.wait_ge(oT_kept, st.seq(4, c=1))
                for t in range(TB):
                    for g in range(2):
                        last = nc.tensor.transpose(fin_ps[:, (2 * t + g) * P:(2 * t + g + 1) * P],
                                                   oT_sb[:, g * N + t * P:g * N + (t + 1) * P], ident[:, :])
                last.then_inc(o_ready, 1)

            def project_v(st):
                if st.has(0):
                    pe.wait_ge(qk_kept, st.seq(0, QKOPS, QKOPS))
                else:
                    pe.wait_ge(mT_kept, st.seq(3, 2, 1))
                for t in range(TB):
                    last = nc.tensor.matmul(in_ps[:, t * C:(t + 1) * C], xT[:, st.slot(2), t * P:(t + 1) * P],
                                            wv[:, :], start=True, stop=True)
                last.then_inc(v_ready, 1)

            def transpose_on(st):
                pe.wait_ge(o_kept, st.seq(4, TB, TB))
                for t in range(TB):
                    last = nc.tensor.transpose(fin_ps[:, t * P:(t + 1) * P], o_sb[:, t, :], ident[:, :])
                last.then_inc(onT_ready, 1)

            def project_o(st):
                pe.wait_ge(onT_kept, st.seq(4, c=1))
                for t in range(TB):
                    last = nc.tensor.matmul(fin_ps[:, t * C:(t + 1) * C], onT_sb[:, t * P:(t + 1) * P], wo[:, :],
                                            start=True, stop=True)
                last.then_inc(y_ready, 1)

            def score_rows(st, u):
                sl = st.slot(2)
                p, t = u // TB, u % TB
                if u == 0:
                    pe.wait_ge(q_stacked[sl], st.turn(2, 48))
                    pe.wait_ge(k_stacked[sl], st.turn(2, 16))
                wait(pe, max_kept, st.seq(2, UNITS, u + 1 - ROW_BANKS))
                bank = row_ps[:, row_bank(st, u), :]
                keys = (t + 1) * P if causal else N
                if causal:
                    seen = bank[:, 0:2 * keys].rearrange("p (a k) -> p a k", a=2)
                    nc.tensor.matmul(seen[:, :, keys - P:keys], ident_h[:, :], mask_qk[:, :, :],
                                     start=True, stop=False, skip_group_check=True)
                for a in range(2):
                    h = 2 * p + a
                    last = nc.tensor.matmul(bank[:, a * keys:(a + 1) * keys],
                                            q_st[0:KROWS, sl, h, t * P:(t + 1) * P], k_st[0:KROWS, sl, h, 0:keys],
                                            start=not causal, stop=True, skip_group_check=causal)
                last.then_inc(rows_ready, 1)

            def score_cols(st, n):
                sl, h = st.slot(3), head(n)
                if n == 0:
                    pe.wait_ge(m_placed[0][sl], st.turn(3))
                if n == H // 2:
                    pe.wait_ge(m_placed[1][sl], st.turn(3))
                wait(pe, probs_kept, st.seq(3, H, n - 1))
                bank = col_ps[:, n % 2, :]
                rows = KROWS + MROWS
                if causal:
                    seen = bank[:, 0:2 * N].rearrange("p (a q) -> p a q", a=2)
                    nc.tensor.matmul(seen[:, :, 0:P], ident_h[:, :], mask_kq[:, :, :],
                                     start=True, stop=False, skip_group_check=True)
                for t in range(TB):
                    first = t * P if causal else 0
                    last = nc.tensor.matmul(bank[:, t * N:(t + 1) * N - first],
                                            k_st[0:rows, sl, h, t * P:(t + 1) * P], q_st[0:rows, sl, h, first:N],
                                            start=not causal, stop=True, skip_group_check=causal)
                last.then_inc(cols_ready, 1)

            def sum_values(st, lag, u):
                g, a = u // 2, u % 2
                if u == 0:
                    wait(pe, oT_kept, st.seq(lag))
                    pe.wait_ge(v_kept, st.seq(lag, TB, TB))
                pe.wait_ge(probs_kept, st.seq(lag, H, 4 * u + 4))
                for t in range(TB):
                    first = t * P if causal else 0
                    for j in range(4):
                        h = head(4 * u + j)
                        last = nc.tensor.matmul(out_ps[32 * j:32 * j + 32, g * N + first:(g + 1) * N],
                                                v_sb[:, st.slot(lag), t, 32 * h:32 * h + 32],
                                                probs[:, u % 2, j, t * N:(t + 1) * N - first],
                                                start=a == 0 and t == 0, stop=a == 1 and t == TB - 1,
                                                skip_group_check=True)
                last.then_inc(pv_ready, 1)

            def step(st):
                for n in range(H):
                    if st.has(3):
                        score_cols(st, n)
                    if st.has(2):
                        score_rows(st, n)
                    if n == at["pe_xT"] and st.has(0):
                        transpose_x(st)
                    if n == at["pe_mT1"] and st.has(3):
                        transpose_max(st, 3, 1)
                    if n == at["pe_pv3"] and st.has(4):
                        sum_values(st, 4, 3)
                    if n == at["pe_qk"] and st.has(0):
                        project_qk(st)
                    if n == at["pe_oT"] and st.has(4):
                        transpose_o(st)
                    if n in (at["pe_pv"], at["pe_pv"] + 4, at["pe_pv"] + 8) and st.has(3):
                        sum_values(st, 3, (n - at["pe_pv"]) // 4)
                    if n == at["pe_v"] and st.has(2):
                        project_v(st)
                    if n == at["pe_onT"] and st.has(4):
                        transpose_on(st)
                    if n == at["pe_mT0"] and st.has(2):
                        transpose_max(st, 2, 0)
                    if n == at["pe_y"] and st.has(4):
                        project_o(st)

            pipeline(pe, step)



E = 8
CAP = int(1.25 * B * N / E)
GT = 8
GROUPS = TILES // GT
LN_SPLIT = 6
MT = 4


def groups(eng, step):
    pipeline(eng, step, 2, 4, GROUPS, 0)


def moe(nc, mem, w):
    x_all, x_mid, ident = mem["x_all"], mem["x_mid"], mem["ident"]
    with ExitStack() as ctx:
        def sb(label, shape, dt=F32):
            return ctx.enter_context(nc.sbuf_tensor(f"moe_{label}", shape, dt))

        def sem(label):
            return nc.alloc_semaphore(name=f"moe_{label}")

        gate_T = sb("gate_T", [P, 32])
        gates_sb = sb("gates_sb", [P, 2, 2 * P])
        rank = sb("rank", [P, E])
        ones = sb("ones", [P, P])
        xs = sb("xs", [P, 2, GT, C])
        xT = sb("xT", [P, 2, GT * P])
        logits = sb("logits", [P, TILES, E])
        probs = sb("probs", [P, TILES, E])
        left = sb("left", [P, TILES, E])
        equal = sb("equal", [P, TILES, E])
        score = sb("score", [P, TILES, E])
        chosen = [sb(f"chosen{k}", [P, TILES, E]) for k in range(2)]
        top = sb("top", [P, TILES])
        total = sb("total", [P, TILES])
        counts = sb("counts", [P, E])
        keep = sb("keep", [P, E])
        any_kept = sb("any_kept", [P, 1])
        flag = sb("flag", [P, 1], I32)
        weight = sb("weight", [P, TILES, E])
        stats = sb("stats", [P, 2, GT, 6])
        mv = sb("mv", [P, 2, GT, 2])
        mean = sb("mean", [P, TILES])
        var = sb("var", [P, TILES])
        rstd = sb("rstd", [P, TILES])
        shift = sb("shift", [P, TILES])
        minus_one = sb("minus_one", [P, TILES])
        e_w = sb("e_w", [P, 2, E, C])
        e_wT = sb("e_wT", [P, 2, E, C])
        e_b = sb("e_b", [P, 2, E, C])
        e_x = sb("e_x", [P, MT, C])
        e_xT = sb("e_xT", [P, MT * P])
        e_pre = sb("e_pre", [P, MT, C])
        e_h = sb("e_h", [P, MT, C])
        e_hT = sb("e_hT", [P, MT * P])
        e_y = sb("e_y", [P, MT, C])
        e_acc = sb("e_acc", [P, MT, C])

        t_ps = ctx.enter_context(nc.psum_tensor("moe_t_ps", [P, 2, 2, 512], F32))
        g_ps = ctx.enter_context(nc.psum_tensor("moe_g_ps", [P, 2, 512], F32))
        l_ps = ctx.enter_context(nc.psum_tensor("moe_l_ps", [P, 2, 512], F32))

        loaded, consts, xs_loaded = sem("loaded"), sem("consts"), [sem(f"xs_loaded{j}") for j in range(2)]
        xT_ready, xT_kept, gates_ready, gates_kept, logits_ready, logits_kept = (
            sem(x) for x in ("xT_ready", "xT_kept", "gates_ready", "gates_kept", "logits_ready", "logits_kept"))
        shifted, exp_kept, routed, counts_ready, flag_kept = (
            sem(x) for x in ("shifted", "exp_kept", "routed", "counts_ready", "flag_kept"))
        mean_kept = sem("mean_kept")
        stats_kept, mv_kept, var_kept, rstd_kept, scaled, ln_kept = (
            sem(x) for x in ("stats_kept", "mv_kept", "var_kept", "rstd_kept", "scaled", "ln_kept"))
        e_loaded, e_x_loaded, ewT_ready, ewT_kept = (
            sem(x) for x in ("e_loaded", "e_x_loaded", "ewT_ready", "ewT_kept"))
        exT_ready, exT_kept, h_ready, pre_kept, h_kept, hT_ready, hT_kept, y_ready = (
            sem(x) for x in ("exT_ready", "exT_kept", "h_ready", "pre_kept", "h_kept", "hT_ready", "hT_kept",
                             "y_ready"))
        y_kept, acc_kept, cleared, experts_done = (sem(x) for x in ("y_kept", "acc_kept", "cleared", "experts_done"))

        COUNTED = 15

        def measure(dve, st, group, counted):
            tiles, j = bass.ds(group * GT, GT), st.slot(0)
            for t in range(GT):
                nc.vector.bn_stats(stats[:, j, t, :], x_all[:, bass.ds(group * GT + t, 1), :].rearrange(
                    "p t c -> p (t c)")).then_inc(stats_kept, 1)
            dve.wait_ge(stats_kept, (group + (counted + 1)) * GT)
            apart(dve, mem)
            for t in range(GT):
                nc.vector.bn_aggr(mv[:, j, t, :], stats[:, j, t, :]).then_inc(mv_kept, 1)
            dve.wait_ge(mv_kept, (group + (counted + 1)) * GT)
            nc.vector.tensor_copy(mean[:, tiles], mv[:, j, :, 0]).then_inc(mean_kept, 1)
            nc.vector.tensor_scalar(var[:, tiles], mv[:, j, :, 1], EPS, None, ALU.add).then_inc(var_kept, 1)

        with nc.Block() as block:

            @block.sync
            def _(sp):

                def step(st):
                    if st.has(0):
                        j = st.slot(0)
                        wait(sp, xT_ready, st.seq(1))
                        sp.dma_start(xs[:, j, :, :], x_all[:, bass.ds(st.seq(0, GT), GT), :])\
                            .then_inc(xs_loaded[j], 16)

                groups(sp, step)
                load_spline(sp, mem, w)

            @block.gpsimd
            def _(pool):
                for e in range(E):
                    nc.gpsimd.memset(rank[:, e:e + 1], float(E - e)).then_inc(consts, 1)
                nc.gpsimd.memset(ones[:, :], 1.0).then_inc(consts, 1)
                nc.gpsimd.memset(gate_T[:, :], 0.0).then_inc(consts, 1)
                nc.gpsimd.memset(minus_one[:, :], -1.0).then_inc(consts, 1)

                def step(st):
                    if st.has(0):
                        pool.wait_ge(var_kept, st.seq(0, c=1))
                        tiles = bass.ds(st.seq(0, GT), GT)
                        nc.gpsimd.tensor_tensor(rstd[:, tiles], var[:, tiles], mem["minus_half"][:, 0:GT], ALU.pow)\
                            .then_inc(rstd_kept, 1)

                groups(pool, step)
                pool.wait_ge(rstd_kept, GROUPS)
                pool.wait_ge(mean_kept, GROUPS)
                nc.gpsimd.tensor_tensor(shift[:, :], mean[:, :], rstd[:, :], ALU.mult).then_inc(scaled, 1)
                pool.wait_ge(scaled, 1)
                nc.gpsimd.tensor_tensor(shift[:, :], shift[:, :], minus_one[:, :], ALU.mult).then_inc(scaled, 1)

            @block.tensor
            def _(pe):
                def step(st):
                    if st.has(0):
                        j = st.slot(0)
                        pe.wait_ge(xs_loaded[j], st.turn(0))
                        wait(pe, xT_kept, st.seq(1, 2))
                        for t in range(GT):
                            last = nc.tensor.transpose(t_ps[:, j, t // 4, t % 4 * P:(t % 4 + 1) * P], xs[:, j, t, :],
                                                       ident[:, :])
                        last.then_inc(xT_ready, 1)
                    if st.has(1):
                        j = st.slot(1)
                        if not st.loop and st.off == 1:
                            pe.wait_ge(loaded, 16)
                        pe.wait_ge(xT_kept, st.seq(1, 2, 2))
                        wait(pe, gates_kept, st.seq(2))
                        for g in range(4):
                            last = nc.tensor.matmul(g_ps[32 * g:32 * g + 32, j, 0:2 * P], gate_T[:, :],
                                                    xT[:, j, 2 * g * P:(2 * g + 2) * P], start=True, stop=True,
                                                    skip_group_check=True)
                        last.then_inc(gates_ready, 1)
                    if st.has(2):
                        j = st.slot(2)
                        pe.wait_ge(gates_kept, st.seq(2, c=1))
                        wait(pe, logits_kept, st.seq(3))
                        for t in range(2):
                            last = nc.tensor.transpose(l_ps[:, j, t * P:(t + 1) * P], gates_sb[:, j, t * P:(t + 1) * P],
                                                       ident[:, :])
                        last.then_inc(logits_ready, 1)

                groups(pe, step)
                pe.wait_ge(routed, COUNTED)
                nc.tensor.matmul(g_ps[:, 0, 0:E], ones[:, :], counts[:, :], start=True, stop=True)\
                    .then_inc(counts_ready, 1)

            @block.scalar
            def _(act):
                act.wait_ge(consts, E + 3)
                act.dma_start(gate_T[:, 0:E], w["L0_ffn_gate_w"].rearrange("e c -> c e"),
                              allow_slow_non_contiguous=True).then_inc(loaded, 16)

                def step(st):
                    if st.has(0):
                        j = st.slot(0)
                        act.wait_ge(xT_ready, st.seq(0, c=1))
                        wait(act, gates_ready, st.seq(1))
                        for b in range(2):
                            nc.scalar.copy(xT[:, j, b * 512:(b + 1) * 512], t_ps[:, j, b, :]).then_inc(xT_kept, 1)
                    if st.has(1):
                        j = st.slot(1)
                        act.wait_ge(gates_ready, st.seq(1, c=1))
                        wait(act, logits_ready, st.seq(2))
                        nc.scalar.copy(gates_sb[:, j, :], g_ps[:, j, 0:2 * P]).then_inc(gates_kept, 1)

                groups(act, step)
                act.wait_ge(shifted, 1)
                nc.scalar.activation(probs[:, :, :], left[:, :, :], ACT.Exp).then_inc(exp_kept, 1)
                act.wait_ge(scaled, 2)
                with act.Fori(0, LN_SPLIT) as i:
                    for t in range(GT):
                        tile = bass.ds(i * GT + t, 1)
                        nc.scalar.activation(x_mid[:, tile, :].rearrange("p t c -> p (t c)"),
                                             x_all[:, tile, :].rearrange("p t c -> p (t c)"), ACT.Identity,
                                             bias=shift[:, tile], scale=rstd[:, tile]).then_inc(ln_kept, 1)

            @block.vector
            def _(dve):
                done = [0]

                def then(ins):
                    ins.then_inc(routed, 1)
                    done[0] += 1
                    dve.wait_ge(routed, done[0])

                def over_experts(ap):
                    return ap.unsqueeze(2).broadcast_to([P, TILES, E])

                def step(st):
                    if st.has(0):
                        measure(dve, st, st.seq(0), 0)
                    if st.has(2):
                        dve.wait_ge(logits_ready, st.seq(2, c=1))
                        of = l_ps[:, st.slot(2), 0:2 * P].rearrange("p (t g m) -> p t g m", t=2, m=32)
                        nc.vector.tensor_copy(
                            logits[:, bass.ds(st.seq(2, GT), GT), :].rearrange("p (g t) e -> p t g e", t=2),
                            of[:, :, :, 0:E]).then_inc(logits_kept, 1)

                groups(dve, step)
                dve.wait_ge(logits_kept, GROUPS)
                dve.wait_ge(consts, E + 3)
                then(nc.vector.tensor_reduce(top[:, :], logits[:, :, :], AX_X, ALU.max))
                nc.vector.tensor_tensor(left[:, :, :], logits[:, :, :], over_experts(top[:, :]), ALU.subtract)\
                    .then_inc(shifted, 1)
                dve.wait_ge(exp_kept, 1)
                then(nc.vector.tensor_reduce(total[:, :], probs[:, :, :], AX_X, ALU.add))
                then(nc.vector.reciprocal(top[:, :], total[:, :]))
                then(nc.vector.tensor_tensor(probs[:, :, :], probs[:, :, :], over_experts(top[:, :]), ALU.mult))
                of = probs
                for k in range(2):
                    then(nc.vector.tensor_reduce(top[:, :], of[:, :, :], AX_X, ALU.max))
                    then(nc.vector.tensor_tensor(equal[:, :, :], of[:, :, :], over_experts(top[:, :]), ALU.is_equal))
                    then(nc.vector.tensor_tensor(score[:, :, :], equal[:, :, :],
                                                 rank[:, :].unsqueeze(1).broadcast_to([P, TILES, E]), ALU.mult))
                    then(nc.vector.tensor_reduce(top[:, :], score[:, :, :], AX_X, ALU.max))
                    then(nc.vector.tensor_tensor(chosen[k][:, :, :], score[:, :, :], over_experts(top[:, :]),
                                                 ALU.is_equal))
                    if k == 0:
                        nc.vector.scalar_tensor_tensor(out=left[:, :, :], in0=chosen[0][:, :, :], scalar=-2.0,
                                                       in1=probs[:, :, :], op0=ALU.mult, op1=ALU.add)\
                            .then_inc(shifted, 1)
                        dve.wait_ge(shifted, 2)
                        of = left
                nc.vector.tensor_tensor(chosen[0][:, :, :], chosen[0][:, :, :], chosen[1][:, :, :], ALU.add)\
                    .then_inc(shifted, 1)
                dve.wait_ge(shifted, 3)
                then(nc.vector.tensor_reduce(counts[:, :], chosen[0][:, :, :].rearrange("p t e -> p e t"), AX_X,
                                             ALU.add))
                assert done[0] == COUNTED
                dve.wait_ge(counts_ready, 1)
                then(nc.vector.tensor_scalar(keep[:, :], g_ps[:, 0, 0:E], float(CAP), None, ALU.is_le))
                then(nc.vector.tensor_reduce(any_kept[:, :], keep[:, :], AX_X, ALU.max))
                nc.vector.tensor_copy(flag[:, :], any_kept[:, :]).then_inc(flag_kept, 1)
                dve.wait_ge(rstd_kept, GROUPS)
                with dve.Fori(LN_SPLIT, GROUPS) as i:
                    for t in range(GT):
                        tile = bass.ds(i * GT + t, 1)
                        nc.vector.tensor_scalar(x_mid[:, tile, :].rearrange("p t c -> p (t c)"),
                                                x_all[:, tile, :].rearrange("p t c -> p (t c)"),
                                                mean[:, tile], rstd[:, tile], ALU.subtract, ALU.mult)\
                            .then_inc(ln_kept, 1)

        FREE = 1
        with nc.Block() as block:

            @block.sync
            def _(sp):
                with sp.If(sp.value_load(flag[0:1, 0:1], min_val=0, max_val=1) > 0):
                    for n, k in enumerate(("1", "2")):
                        sp.dma_start(e_w[:, n, :, :], w[f"L0_ffn_w{k}"].rearrange("e o i -> o e i"))\
                            .then_inc(e_loaded, 16)
                        b = w[f"L0_ffn_b{k}"]
                        sp.dma_start(e_b[:, n, :, :].rearrange("p e c -> p (e c)"),
                                     bass.AP(b.tensor, b.offset, [[0, P], [1, E * C]])).then_inc(e_loaded, 16)
                    with sp.Fori(0, TILES // MT) as g:
                        sp.wait_ge(experts_done, g + FREE)
                        sp.dma_start(e_x[:, :, :], x_all[:, bass.ds(g * MT, MT), :]).then_inc(e_x_loaded, 16)
                with sp.Else():
                    sp.nop()
                sp.nop()

            @block.tensor
            def _(pe):
                with pe.If(pe.value_load(flag[0:1, 0:1], min_val=0, max_val=1) > 0):
                    for s in (h_ready, hT_ready, y_ready):
                        pe.sem_inc(s, FREE)
                    pe.wait_ge(e_loaded, 64)
                    for n in range(2):
                        for half in range(2):
                            k = 2 * n + half
                            if k >= 2:
                                pe.wait_ge(ewT_kept, k - 1)
                            for q in range(E // 2):
                                last = nc.tensor.transpose(t_ps[:, 0, k % 2, q * P:(q + 1) * P],
                                                           e_w[:, n, half * E // 2 + q, :], ident[:, :])
                            last.then_inc(ewT_ready, 1)
                    pe.wait_ge(ewT_kept, 4)
                    with pe.Fori(0, TILES // MT) as g:
                        pe.wait_ge(e_x_loaded, g * 16 + 16)
                        pe.wait_ge(exT_kept, g + FREE)
                        for t in range(MT):
                            last = nc.tensor.transpose(t_ps[:, 0, 0, t * P:(t + 1) * P], e_x[:, t, :], ident[:, :])
                        last.then_inc(exT_ready, 1)
                        pe.wait_ge(exT_kept, g + (1 + FREE))
                        apart(pe, mem)
                        with pe.Fori(0, E) as e:
                            pe.wait_ge(pre_kept, g * E + e + FREE)
                            for t in range(MT):
                                last = nc.tensor.matmul(t_ps[:, 0, 1, t * P:(t + 1) * P], e_xT[:, t * P:(t + 1) * P],
                                                        e_wT[:, 0, bass.ds(e, 1), :].rearrange("p e c -> p (e c)"),
                                                        start=True, stop=True)
                            last.then_inc(h_ready, 1)
                            pe.wait_ge(h_kept, g * E + (e + (1 + FREE)))
                            pe.wait_ge(hT_kept, g * E + e + FREE)
                            for t in range(MT):
                                last = nc.tensor.transpose(t_ps[:, 1, 0, t * P:(t + 1) * P], e_h[:, t, :],
                                                           ident[:, :])
                            last.then_inc(hT_ready, 1)
                            pe.wait_ge(hT_kept, g * E + (e + (1 + FREE)))
                            pe.wait_ge(y_kept, g * E + e + FREE)
                            for t in range(MT):
                                last = nc.tensor.matmul(t_ps[:, 1, 1, t * P:(t + 1) * P], e_hT[:, t * P:(t + 1) * P],
                                                        e_wT[:, 1, bass.ds(e, 1), :].rearrange("p e c -> p (e c)"),
                                                        start=True, stop=True)
                            last.then_inc(y_ready, 1)
                with pe.Else():
                    pe.nop()
                pe.nop()

            @block.gpsimd
            def _(pool):
                with pool.If(pool.value_load(flag[0:1, 0:1], min_val=0, max_val=1) > 0):
                    pool.wait_ge(var_kept, 2 * GROUPS)
                    nc.gpsimd.tensor_tensor(rstd[:, :], var[:, :], mem["minus_half"][:, :], ALU.pow)\
                        .then_inc(rstd_kept, 1)
                with pool.Else():
                    pool.nop()
                pool.nop()

            @block.scalar
            def _(act):
                with act.If(act.value_load(flag[0:1, 0:1], min_val=0, max_val=1) > 0):
                    for s in (exT_kept, h_kept, hT_kept):
                        act.sem_inc(s, FREE)
                    for k in range(4):
                        act.wait_ge(ewT_ready, k + 1)
                        nc.scalar.copy(e_wT[:, k // 2, k % 2 * 4:k % 2 * 4 + 4, :].rearrange("p e c -> p (e c)"),
                                       t_ps[:, 0, k % 2, :]).then_inc(ewT_kept, 1)
                    with act.Fori(0, TILES // MT) as g:
                        act.wait_ge(exT_ready, g + 1)
                        act.wait_ge(h_ready, g * E + FREE)
                        nc.scalar.copy(e_xT[:, :], t_ps[:, 0, 0, :]).then_inc(exT_kept, 1)
                        with act.Fori(0, E) as e:
                            act.wait_ge(pre_kept, g * E + (e + (1 + FREE)))
                            act.wait_ge(hT_ready, g * E + e + FREE)
                            nc.scalar.activation(e_h[:, :, :], e_pre[:, :, :], ACT.Silu).then_inc(h_kept, 1)
                            act.wait_ge(hT_ready, g * E + (e + (1 + FREE)))
                            act.wait_ge(y_ready, g * E + e + FREE)
                            nc.scalar.copy(e_hT[:, :], t_ps[:, 1, 0, :]).then_inc(hT_kept, 1)
                with act.Else():
                    act.nop()
                act.nop()

            @block.vector
            def _(dve):
                with dve.If(dve.value_load(flag[0:1, 0:1], min_val=0, max_val=1) > 0):
                    for s in (pre_kept, y_kept, experts_done):
                        dve.sem_inc(s, FREE)
                    nc.vector.tensor_tensor(weight[:, :, :], chosen[0][:, :, :], probs[:, :, :], ALU.mult)\
                        .then_inc(shifted, 1)
                    dve.wait_ge(shifted, 4)
                    nc.vector.tensor_tensor(weight[:, :, :], weight[:, :, :],
                                            keep[:, :].unsqueeze(1).broadcast_to([P, TILES, E]), ALU.mult)\
                        .then_inc(shifted, 1)
                    dve.wait_ge(shifted, 5)
                    dve.wait_ge(e_loaded, 64)
                    with dve.Fori(0, TILES // MT) as g:
                        dve.wait_ge(experts_done, g + FREE)
                        nc.vector.memset(e_acc[:, :, :], 0.0).then_inc(cleared, 1)
                        dve.wait_ge(cleared, g + 1)
                        apart(dve, mem)
                        with dve.Fori(0, E) as e:
                            dve.wait_ge(h_ready, g * E + (e + (1 + FREE)))
                            dve.wait_ge(h_kept, g * E + e + FREE)
                            nc.vector.tensor_tensor(
                                e_pre[:, :, :], t_ps[:, 0, 1, :].rearrange("p (t c) -> p t c", c=C),
                                e_b[:, 0, bass.ds(e, 1), :].broadcast_to([P, MT, C]), ALU.add).then_inc(pre_kept, 1)
                            dve.wait_ge(y_ready, g * E + (e + (1 + FREE)))
                            nc.vector.tensor_tensor(
                                e_y[:, :, :], t_ps[:, 1, 1, :].rearrange("p (t c) -> p t c", c=C),
                                e_b[:, 1, bass.ds(e, 1), :].broadcast_to([P, MT, C]), ALU.add).then_inc(y_kept, 1)
                            dve.wait_ge(y_kept, g * E + (e + (1 + FREE)))
                            for t in range(MT):
                                nc.vector.scalar_tensor_tensor(
                                    out=e_acc[:, t, :], in0=e_y[:, t, :],
                                    scalar=weight[:, bass.ds(g * MT + t, 1), bass.ds(e, 1)].rearrange(
                                        "p t e -> p (t e)"),
                                    in1=e_acc[:, t, :], op0=ALU.mult, op1=ALU.add).then_inc(acc_kept, 1)
                            dve.wait_ge(acc_kept, g * (E * MT) + e * MT + MT)
                        dve.wait_ge(e_x_loaded, g * 16 + 16)
                        nc.vector.tensor_tensor(x_all[:, bass.ds(g * MT, MT), :], x_all[:, bass.ds(g * MT, MT), :],
                                                e_acc[:, :, :], ALU.add).then_inc(experts_done, 1)
                    dve.wait_ge(experts_done, TILES // MT + FREE)
                    with dve.Fori(0, GROUPS) as g:
                        measure(dve, Step(0, 0, 2, GROUPS), g, GROUPS)
                    dve.wait_ge(rstd_kept, GROUPS + 1)
                    dve.wait_ge(mean_kept, 2 * GROUPS)
                    with dve.Fori(0, TILES) as t:
                        tile = bass.ds(t, 1)
                        nc.vector.tensor_scalar(x_mid[:, tile, :].rearrange("p t c -> p (t c)"),
                                                x_all[:, tile, :].rearrange("p t c -> p (t c)"),
                                                mean[:, tile], rstd[:, tile], ALU.subtract, ALU.mult)\
                            .then_inc(ln_kept, 1)
                with dve.Else():
                    dve.nop()
                dve.nop()



NT = 64
TPC = 8
NC = NT // TPC
COMP = 32
GRID = 16
KNOTS = 8
W1, B1, W2, B2, DIR = 0, 2 * GRID, 3 * GRID, 4 * GRID, 4 * GRID + 1
TABLE = DIR + C
NS = NC + NT
AT_H = P - COMP
SG = 4
RG = 4
SPLINE_SLOTS = 4
SPLINE_DEPTH = 6


def load_spline(eng, mem, w):
    def wide(ap, n):
        return bass.AP(ap.tensor, ap.offset, [[0, P], [1, n]])

    sigs, cb1, cw2, table = (mem[k] for k in ("sigs", "cb1", "cw2", "table"))
    for to, of in ((mem["raw"][:, :], w["L1_ffn_signatures_raw"]),
                   (mem["knots"][:, :], wide(w["L1_ffn_knot_values"], KNOTS)),
                   (mem["temp"][:, :], wide(w["L1_ffn_temperature"], 1)),
                   (sigs[:, AT_H:P], w["L1_ffn_compress_w1"]),
                   (cb1[AT_H:P, :], w["L1_ffn_compress_b1"].rearrange("(n one) -> n one", one=1)),
                   (cw2[AT_H:P, 0:2], w["L1_ffn_compress_w2"]),
                   (mem["cb2"][:, :], wide(w["L1_ffn_compress_b2"], 2)),
                   (mem["gamma"][:, :], wide(w["L1_ffn_norm_gamma"], C)),
                   (mem["beta"][:, :], wide(w["L1_ffn_norm_beta"], C)),
                   (mem["out_scale"][:, :], wide(w["L1_ffn_output_scale"], 1))):
        eng.dma_start(to, of).then_inc(mem["ffn_loaded"], 16)
    for half in range(2):
        rows = slice(half * NT, (half + 1) * NT)
        for at, of in ((W1, w["L1_ffn_spline_w1"].rearrange("t i g -> t (i g)")), (B1, w["L1_ffn_spline_b1"]),
                       (W2, w["L1_ffn_spline_w2"].rearrange("t g one -> t (g one)")),
                       (B2, w["L1_ffn_spline_b2"]), (DIR, w["L1_ffn_directions"])):
            eng.dma_start(table[rows, at:at + of.shape[1]], of).then_inc(mem["ffn_loaded"], 16)


def spline_ffn(nc, mem, w, out_tiles):
    x_all, ident, ident_h = mem["x_mid"], mem["ident"], mem["ident_h"]
    raw, knots, temp, sigs, cb1, cw2, cb2, table, gamma, beta, out_scale = (
        mem[k] for k in ("raw", "knots", "temp", "sigs", "cb1", "cw2", "cb2", "table", "gamma", "beta", "out_scale"))
    x_beta = mem["x_all"]
    with ExitStack() as ctx:
        def sb(label, shape, dt=F32):
            return ctx.enter_context(nc.sbuf_tensor(f"ffn_{label}", shape, dt))

        def sem(label):
            return nc.alloc_semaphore(name=f"ffn_{label}")

        rawT = sb("rawT", [P, NT])
        above = sb("above", [P, NT])
        below = sb("below", [P, NT])
        sums = sb("sums", [P, NC])
        rises = sb("rises", [P, KNOTS - 1])
        table_rest = sb("table_rest", [P, TABLE])
        table_hm = sb("table_hm", [P, TABLE], BF16)
        table_l = sb("table_l", [P, TABLE], BF16)
        rank = sb("rank", [P, TPC])
        xs = sb("xs", [P, 2, SG, C])
        xT = sb("xT", [P, 2, SG * P])
        sT = sb("sT", [NS, 2, SG * P])
        hT = sb("hT", [P, 2, SG * P])
        compT = sb("compT", [P, 2, P])
        scores = sb("scores", [P, TILES, NS])
        comp = sb("comp", [P, TILES, 2])
        big = sb("big", [P, TILES, NT])
        onehot = sb("onehot", [P, TILES, 2, NT], BF16)
        value, pos, low, val, rise, equal, score, cluster, local = (
            sb(x, [P, TILES, TPC]) for x in ("value", "pos", "low", "val", "rise", "equal", "score", "cluster",
                                            "local"))
        top = sb("top", [P, TILES])
        equals = [equal] + [sb(f"equal{n}", [P, TILES, TPC]) for n in (1, 2)]
        ohT = sb("ohT", [P, SPLINE_SLOTS, RG * P], BF16)
        rows = sb("rows", [P, SPLINE_SLOTS, RG, TABLE])
        bent = sb("bent", [P, 2, RG, GRID])
        mag = sb("mag", [P, RG])
        y = sb("y", [P, SPLINE_SLOTS, RG, C])
        z = sb("z", [P, SPLINE_SLOTS, RG, C])
        stats = sb("stats", [P, 2, RG, 6])
        mv = sb("mv", [P, 2, RG, 2])
        var = sb("var", [P, 2, RG])
        rstd = sb("rstd", [P, SPLINE_SLOTS, 2, RG])
        shift = sb("shift", [P, SPLINE_SLOTS, 2, RG])

        consts, rawT_ready, chain, tables_kept = (
            sem(x) for x in ("consts", "rawT_ready", "chain", "tables_kept"))
        xs_loaded = [sem(f"xs_loaded{j}") for j in range(2)]
        xT_ready, xT_kept, products_ready, h_kept, sT_kept = (
            sem(x) for x in ("xT_ready", "xT_kept", "products_ready", "h_kept", "sT_kept"))
        compT_ready, compT_kept, scores_ready, scores_kept = (
            sem(x) for x in ("compT_ready", "compT_kept", "scores_ready", "scores_kept"))
        x_beta_kept, mv_cleared = sem("x_beta_kept"), sem("mv_cleared")
        pos_ready, exp_kept, comp_ready, comp_kept = (
            sem(x) for x in ("pos_ready", "exp_kept", "comp_ready", "comp_kept"))
        LOADS = 10 + 2 * 5
        SPLINE_GROUPS = TILES // SG

        def scored(eng, step):
            pipeline(eng, step, 2, 5, SPLINE_GROUPS, 0)

        with nc.psum_tensor("ffn_t_ps", [P, 2, 512], F32) as t_ps, \
                nc.psum_tensor("ffn_p_ps", [P, 2, 512], F32) as p_ps, \
                nc.psum_tensor("ffn_c_ps", [P, 2, 512], F32) as c_ps, \
                nc.psum_tensor("ffn_s_ps", [P, 2, 512], F32) as s_ps, nc.Block() as block:

            COMP_AT = SG * NS

            @block.sync
            def _(sp):
                def step(st):
                    if st.has(0):
                        j = st.slot(0)
                        wait(sp, xT_ready, st.seq(1))
                        sp.dma_start(xs[:, j, :, :], x_all[:, bass.ds(st.seq(0, SG), SG), :])\
                            .then_inc(xs_loaded[j], 16)

                scored(sp, step)

            @block.gpsimd
            def _(pool):
                for e in range(TPC):
                    nc.gpsimd.memset(rank[:, e:e + 1], float(TPC - e)).then_inc(consts, 1)
                pool.wait_ge(consts, TPC)
                nc.gpsimd.memset(table_l[NT:P, :], 0.0).then_inc(consts, 1)
                pool.wait_ge(consts, TPC + 1)
                nc.gpsimd.memset(mv[:, :, :, :], 0.0).then_inc(mv_cleared, 1)
                pool.wait_ge(mv_cleared, 1)
                pool.wait_ge(mem["ffn_loaded"], 16 * LOADS)
                with pool.Fori(0, TILES // RG) as i:
                    tiles = bass.ds(i * RG, RG)
                    nc.gpsimd.tensor_tensor(x_beta[:, tiles, :], x_all[:, tiles, :],
                                            beta[:, :].unsqueeze(1).broadcast_to([P, RG, C]), ALU.add)\
                        .then_inc(x_beta_kept, 1)

            @block.tensor
            def _(pe):
                pe.wait_ge(mem["ffn_loaded"], 16 * LOADS)
                nc.tensor.transpose(t_ps[:, 0, 0:NT], raw[:, :], ident[0:NT, 0:NT]).then_inc(rawT_ready, 1)

                def step(st):
                    if st.has(0):
                        j = st.slot(0)
                        pe.wait_ge(xs_loaded[j], st.turn(0))
                        wait(pe, xT_kept, st.seq(1))
                        for t in range(SG):
                            last = nc.tensor.transpose(t_ps[:, j, t * P:(t + 1) * P], xs[:, j, t, :], ident[:, :])
                        last.then_inc(xT_ready, 1)
                    if st.has(1):
                        j = st.slot(1)
                        pe.wait_ge(xT_kept, st.seq(1, c=1))
                        wait(pe, h_kept, st.seq(2))
                        wait(pe, sT_kept, st.seq(2))
                        nc.tensor.matmul(p_ps[:, j, :], sigs[:, :], xT[:, j, :], start=True, stop=True)\
                            .then_inc(products_ready, 1)
                    if st.has(2):
                        j = st.slot(2)
                        pe.wait_ge(h_kept, st.seq(2, c=1))
                        wait(pe, compT_kept, st.seq(3))
                        apart(pe, mem)
                        for t in range(SG):
                            last = nc.tensor.matmul(c_ps[32 * t:32 * t + 32, j, 0:P], cw2[AT_H:P, :],
                                                    hT[AT_H:P, j, t * P:(t + 1) * P], start=True, stop=True,
                                                    tile_position=(AT_H, 32 * t), skip_group_check=True)
                        last.then_inc(compT_ready, 1)
                    if st.has(3):
                        j = st.slot(3)
                        pe.wait_ge(sT_kept, st.seq(3, c=1))
                        pe.wait_ge(compT_kept, st.seq(3, c=1))
                        wait(pe, scores_kept, st.seq(4, 2))
                        for t in range(SG):
                            nc.tensor.transpose(s_ps[:, j, t * NS:(t + 1) * NS], sT[:, j, t * P:(t + 1) * P],
                                                ident[0:NS, 0:NS])
                        nc.tensor.transpose(s_ps[:, j, COMP_AT:COMP_AT + P], compT[:, j, :], ident[:, :])\
                            .then_inc(scores_ready, 1)

                pe.wait_ge(tables_kept, 1)
                scored(pe, step)

            @block.scalar
            def _(act):
                def step(st):
                    if st.has(0):
                        j = st.slot(0)
                        act.wait_ge(xT_ready, st.seq(0, c=1))
                        wait(act, products_ready, st.seq(1))
                        nc.scalar.copy(xT[:, j, :], t_ps[:, j, :]).then_inc(xT_kept, 1)
                    if st.has(1):
                        j = st.slot(1)
                        act.wait_ge(products_ready, st.seq(1, c=1))
                        wait(act, compT_ready, st.seq(2))
                        nc.scalar.activation(hT[AT_H:P, j, :], p_ps[AT_H:P, j, :], ACT.Gelu, bias=cb1[AT_H:P, :])\
                            .then_inc(h_kept, 1)
                    if st.has(2):
                        j = st.slot(2)
                        act.wait_ge(compT_ready, st.seq(2, c=1))
                        wait(act, scores_ready, st.seq(3))
                        nc.scalar.copy(compT[:, j, :], c_ps[:, j, 0:P]).then_inc(compT_kept, 1)

                scored(act, step)
                act.wait_ge(comp_ready, 1)
                nc.scalar.activation(comp[:, :, :], comp[:, :, :], ACT.Tanh).then_inc(comp_kept, 1)
                for k in range(2):
                    act.wait_ge(pos_ready, k + 1)
                    nc.scalar.activation(pos[:, :, :], value[:, :, :], ACT.Exp).then_inc(exp_kept, 1)

            @block.vector
            def _(dve):
                done = [0]

                def issue(ins):
                    ins.then_inc(chain, 1)
                    done[0] += 1
                    return done[0]

                def then(ins):
                    dve.wait_ge(chain, issue(ins))

                dve.wait_ge(rawT_ready, 1)
                dve.wait_ge(consts, TPC + 1)
                then(nc.vector.tensor_copy(rawT[:, :], t_ps[:, 0, 0:NT]))
                then(nc.vector.tensor_scalar(above[:, :], rawT[:, :], 0.3, None, ALU.is_gt))
                then(nc.vector.tensor_scalar(below[:, :], rawT[:, :], -0.3, None, ALU.is_lt))
                then(nc.vector.tensor_tensor(above[:, :], above[:, :], below[:, :], ALU.subtract))
                then(nc.vector.tensor_tensor(above[:, :], above[:, :], rawT[:, :], ALU.subtract))
                then(nc.vector.tensor_tensor(sigs[:, NC:NS], rawT[:, :], above[:, :], ALU.add))
                by_tile = sigs[:, NC:NS].rearrange("p (c t) -> p t c", t=TPC)
                then(nc.vector.tensor_tensor(sums[:, :], by_tile[:, 0, :], by_tile[:, 1, :], ALU.add))
                for t in range(2, TPC):
                    then(nc.vector.tensor_tensor(sums[:, :], sums[:, :], by_tile[:, t, :], ALU.add))
                then(nc.vector.tensor_scalar(above[:, 0:NC], sums[:, :], 0.0, None, ALU.is_gt))
                then(nc.vector.tensor_scalar(below[:, 0:NC], sums[:, :], 0.0, None, ALU.is_lt))
                nc.vector.tensor_tensor(sigs[:, 0:NC], above[:, 0:NC], below[:, 0:NC], ALU.subtract)\
                    .then_inc(tables_kept, 1)
                then(nc.vector.tensor_tensor(rises[:, :], knots[:, 1:KNOTS], knots[:, 0:KNOTS - 1], ALU.subtract))
                then(nc.vector.tensor_scalar(temp[:, :], temp[:, :], 1e-6, None, ALU.add))
                then(nc.vector.reciprocal(temp[:, :], temp[:, :]))
                then(nc.vector.tensor_scalar(temp[:, :], temp[:, :], -1.0, None, ALU.mult))
                then(nc.vector.tensor_scalar(table[:, DIR:TABLE], table[:, DIR:TABLE], out_scale[:, :], None, ALU.mult))
                then(nc.vector.tensor_copy(table_hm[:, :], table[:, :]))
                then(nc.vector.tensor_tensor(table_rest[:, :], table[:, :], table_hm[:, :], ALU.subtract))
                then(nc.vector.tensor_copy(table_hm[NT:P, :], table_rest[NT:P, :]))
                then(nc.vector.tensor_copy(table_l[0:NT, :], table_rest[0:NT, :]))
                then(nc.vector.tensor_tensor(table_rest[0:NT, :], table_rest[0:NT, :], table_l[0:NT, :], ALU.subtract))
                then(nc.vector.tensor_copy(table_l[0:NT, :], table_rest[0:NT, :]))

                def step(st):
                    if st.has(3):
                        j, tiles = st.slot(3), bass.ds(st.seq(3, SG), SG)
                        dve.wait_ge(scores_ready, st.seq(3, c=1))
                        nc.vector.tensor_copy(scores[:, tiles, :].rearrange("p t n -> p (t n)"),
                                              s_ps[:, j, 0:COMP_AT]).then_inc(scores_kept, 1)
                        nc.vector.tensor_copy(comp[:, tiles, :], s_ps[:, j, COMP_AT:COMP_AT + P].rearrange(
                            "p (t m) -> p t m", m=32)[:, :, 0:2]).then_inc(scores_kept, 1)
                    if st.has(1):
                        j = st.slot(1)
                        dve.wait_ge(products_ready, st.seq(1, c=1))
                        wait(dve, scores_ready, st.seq(2))
                        nc.vector.tensor_copy(sT[:, j, :], p_ps[0:NS, j, :]).then_inc(sT_kept, 1)

                scored(dve, step)
                dve.wait_ge(scores_kept, 2 * SPLINE_GROUPS)
                nc.vector.tensor_tensor(comp[:, :, :], comp[:, :, :], cb2[:, :].unsqueeze(1).broadcast_to([P, TILES, 2]),
                                        ALU.add).then_inc(comp_ready, 1)

                def over(ap):
                    return ap.unsqueeze(2).broadcast_to([P, TILES, TPC])

                def calibrate(of, k):
                    nc.vector.tensor_scalar(value[:, :, :], of, temp[:, :], 88.0, ALU.mult, ALU.min)\
                        .then_inc(pos_ready, 1)
                    dve.wait_ge(exp_kept, k + 1)
                    then(nc.vector.tensor_scalar(pos[:, :, :], pos[:, :, :], 1.0, None, ALU.add))
                    then(nc.vector.reciprocal(pos[:, :, :], pos[:, :, :]))
                    then(nc.vector.tensor_scalar(pos[:, :, :], pos[:, :, :], float(KNOTS - 1), None, ALU.mult))
                    then(nc.vector.tensor_scalar(low[:, :, :], pos[:, :, :], 1.0, None, ALU.is_ge))
                    for n in range(2, KNOTS - 1):
                        then(nc.vector.scalar_tensor_tensor(out=low[:, :, :], in0=pos[:, :, :], scalar=float(n),
                                                            in1=low[:, :, :], op0=ALU.is_ge, op1=ALU.add))
                    then(nc.vector.tensor_tensor(pos[:, :, :], pos[:, :, :], low[:, :, :], ALU.subtract))
                    def compare(n):
                        return issue(nc.vector.tensor_scalar(equals[n % 3][:, :, :], low[:, :, :], float(n), None,
                                                             ALU.is_equal))

                    def pick(n, to, by):
                        if n == 0:
                            return issue(nc.vector.tensor_scalar(to[:, :, :], equals[0][:, :, :], by[:, 0:1], None,
                                                                 ALU.mult))
                        return issue(nc.vector.scalar_tensor_tensor(
                            out=to[:, :, :], in0=equals[n % 3][:, :, :], scalar=by[:, n:n + 1], in1=to[:, :, :],
                            op0=ALU.mult, op1=ALU.add))

                    valued = compare(0)
                    for n in range(KNOTS - 1):
                        if n + 1 < KNOTS - 1:
                            compare(n + 1)
                        dve.wait_ge(chain, valued)
                        value_at = pick(n, val, knots)
                        if n:
                            dve.wait_ge(chain, rose)
                        rose, valued = pick(n, rise, rises), value_at
                    dve.wait_ge(chain, rose)
                    then(nc.vector.tensor_tensor(rise[:, :, :], rise[:, :, :], pos[:, :, :], ALU.mult))
                    then(nc.vector.tensor_tensor(val[:, :, :], val[:, :, :], rise[:, :, :], ALU.add))

                def first_best(to):
                    then(nc.vector.tensor_reduce(top[:, :], val[:, :, :], AX_X, ALU.max))
                    then(nc.vector.tensor_tensor(equal[:, :, :], val[:, :, :], over(top[:, :]), ALU.is_equal))
                    then(nc.vector.tensor_tensor(score[:, :, :], equal[:, :, :],
                                                 rank[:, :].unsqueeze(1).broadcast_to([P, TILES, TPC]), ALU.mult))
                    then(nc.vector.tensor_reduce(top[:, :], score[:, :, :], AX_X, ALU.max))
                    then(nc.vector.tensor_tensor(to[:, :, :], score[:, :, :], over(top[:, :]), ALU.is_equal))

                calibrate(scores[:, :, 0:NC], 0)
                first_best(cluster)
                of_cluster = cluster[:, :, :].unsqueeze(3).broadcast_to([P, TILES, NC, TPC])
                then(nc.vector.tensor_tensor(big[:, :, :].rearrange("p n (c t) -> p n c t", c=NC),
                                             scores[:, :, NC:NS].rearrange("p n (c t) -> p n c t", c=NC),
                                             of_cluster, ALU.mult))
                then(nc.vector.tensor_reduce(score[:, :, :], big[:, :, :].rearrange("p n (c t) -> p n t c", c=NC),
                                             AX_X, ALU.add))
                calibrate(score[:, :, :], 1)
                first_best(local)
                then(nc.vector.tensor_tensor(onehot[:, :, 0, :].rearrange("p n (c t) -> p n c t", c=NC), of_cluster,
                                             local[:, :, :].unsqueeze(2).broadcast_to([P, TILES, NC, TPC]), ALU.mult))
                then(nc.vector.tensor_copy(onehot[:, :, 1, :], onehot[:, :, 0, :]))

        ohT_ready, ohT_kept, rows_ready, rows_kept = (
            sem(x) for x in ("ohT_ready", "ohT_kept", "rows_ready", "rows_kept"))
        terms, bent_sum, hidden, mag_kept, y_kept = (
            sem(x) for x in ("terms", "bent_sum", "hidden", "mag_kept", "y_kept"))
        stats_kept, mv_kept = ([sem(f"{x}{k}") for k in range(2)] for x in ("stats_kept", "mv_kept"))
        var_kept, rstd_kept, shift_kept = (sem(x) for x in ("var_kept", "rstd_kept", "shift_kept"))
        norm_kept, scaled, z_kept, o_kept = (sem(x) for x in ("norm_kept", "scaled", "z_kept", "o_kept"))
        stored = sem("stored")
        BENT_GROUPS = TILES // RG

        def steps(eng, step):
            pipeline(eng, step, SPLINE_SLOTS, SPLINE_DEPTH, BENT_GROUPS, 0)

        with nc.psum_tensor("ffn_o_ps", [P, SPLINE_SLOTS, 512], F32) as o_ps, \
                nc.psum_tensor("ffn_r_ps", [P, RG // 2, 512], F32) as r_ps, nc.Block() as block:

            @block.sync
            def _(sp):
                def step(st):
                    if st.has(5):
                        sp.wait_ge(o_kept, st.seq(5, RG, RG))
                        tiles = bass.ds(st.seq(5, RG), RG)
                        sp.dma_start(out_tiles[:, tiles, :], x_all[:, tiles, :]).then_inc(stored, 16)

                steps(sp, step)
                sp.wait_ge(stored, 16 * BENT_GROUPS)

            @block.tensor
            def _(pe):
                def step(st):
                    if st.has(0):
                        b = st.slot(0)
                        wait(pe, ohT_kept, st.seq(SPLINE_SLOTS, c=1))
                        for t in range(RG):
                            last = nc.tensor.transpose(
                                o_ps[:, b, t * P // 2:(t + 1) * P // 2].bitcast(BF16),
                                onehot[:, bass.ds(st.seq(0, RG, t), 1), :, :].rearrange("p n k t -> p (n k t)"),
                                ident_h[:, :])
                        last.then_inc(ohT_ready, 1)
                        pe.wait_ge(ohT_kept, st.seq(0, c=1))
                        wait(pe, rows_kept, st.seq(0, RG // 2))
                        for t in range(RG):
                            to = r_ps[:, t // 2, t % 2 * TABLE:(t % 2 + 1) * TABLE]
                            one = ohT[:, st.slot(0), t * P:(t + 1) * P]
                            nc.tensor.matmul(to, one, table_hm[:, :], start=True, stop=False)
                            last = nc.tensor.matmul(to, one, table_l[:, :], start=False, stop=True)
                        last.then_inc(rows_ready, 1)

                steps(pe, step)

            @block.scalar
            def _(act):
                def step(st):
                    if st.has(0):
                        sl = st.slot(0)
                        act.wait_ge(ohT_ready, st.seq(0, c=1))
                        nc.scalar.copy(ohT[:, sl, :], o_ps[:, sl, 0:RG * P // 2].bitcast(BF16)).then_inc(ohT_kept, 1)
                    if st.has(2):
                        sl = st.slot(2)
                        act.wait_ge(shift_kept, st.seq(1))
                        wait(act, o_kept, st.seq(2 + SPLINE_SLOTS, RG, RG))
                        for t in range(RG):
                            nc.scalar.activation(z[:, sl, t, :], y[:, sl, t, :], ACT.Identity,
                                                 bias=shift[:, st.slot(1), 0, t:t + 1],
                                                 scale=rstd[:, st.slot(1), 0, t:t + 1]).then_inc(norm_kept, 1)
                    if st.has(0):
                        sl = st.slot(0)
                        act.wait_ge(rows_ready, st.seq(0, c=1))
                        wait(act, y_kept, st.seq(SPLINE_SLOTS, RG, RG))
                        for b in range(RG // 2):
                            nc.scalar.copy(rows[:, sl, 2 * b:2 * b + 2, :].rearrange("p t n -> p (t n)"),
                                           r_ps[:, b, 0:2 * TABLE]).then_inc(rows_kept, 1)
                    if st.has(5):
                        act.wait_ge(shift_kept, st.seq(1))
                        for t in range(RG):
                            x = x_all[:, bass.ds(st.seq(5, RG, t), 1), :].rearrange("p t c -> p (t c)")
                            nc.scalar.activation(x, z[:, st.slot(5), t, :], ACT.Identity,
                                                 bias=shift[:, st.slot(1), 1, t:t + 1],
                                                 scale=rstd[:, st.slot(1), 1, t:t + 1]).then_inc(o_kept, 1)

                steps(act, step)

            @block.gpsimd
            def _(pool):
                def step(st):
                    if st.has(3):
                        sl = st.slot(3)
                        pool.wait_ge(norm_kept, st.seq(3, RG, RG))
                        nc.gpsimd.tensor_tensor(z[:, sl, :, :], z[:, sl, :, :],
                                                gamma[:, :].unsqueeze(1).broadcast_to([P, RG, C]), ALU.mult)\
                            .then_inc(scaled, 1)
                        pool.wait_ge(scaled, st.seq(3, c=1))
                        nc.gpsimd.tensor_tensor(z[:, sl, :, :], z[:, sl, :, :],
                                                x_beta[:, bass.ds(st.seq(3, RG), RG), :], ALU.add)\
                            .then_inc(z_kept, 1)
                    if st.has(1) or st.has(4):
                        pool.wait_ge(var_kept, st.seq(0))
                        nc.gpsimd.tensor_tensor(rstd[:, st.slot(0), :, :].rearrange("p k t -> p (k t)"),
                                                var[:, :, :].rearrange("p k t -> p (k t)"),
                                                mem["minus_half"][:, 0:2 * RG], ALU.pow).then_inc(rstd_kept, 1)

                steps(pool, step)

            @block.vector
            def _(dve):
                def statistics(st, lag, k, of):
                    for t in range(RG):
                        nc.vector.bn_stats(stats[:, k, t, :], of[:, st.slot(lag), t, :]).then_inc(stats_kept[k], 1)

                def moments(st, lag, k):
                    dve.wait_ge(stats_kept[k], st.seq(lag, RG, RG))
                    apart(dve, mem)
                    for t in range(RG):
                        nc.vector.bn_aggr(mv[:, k, t, :], stats[:, k, t, :]).then_inc(mv_kept[k], 1)

                def variances(st):
                    for k, lag in ((0, 1), (1, 4)):
                        if st.has(lag):
                            dve.wait_ge(mv_kept[k], st.seq(lag, RG, RG))
                    nc.vector.tensor_scalar(var[:, :, :], mv[:, :, :, 1], EPS, None, ALU.add).then_inc(var_kept, 1)

                def shifts(st):
                    dve.wait_ge(rstd_kept, st.seq(1))
                    nc.vector.scalar_tensor_tensor(out=shift[:, st.slot(1), :, :], in0=mv[:, :, :, 0], scalar=-1.0,
                                                   in1=rstd[:, st.slot(1), :, :], op0=ALU.mult, op1=ALU.mult)\
                        .then_inc(shift_kept, 1)

                def step(st):
                    sl = st.slot(1)
                    if st.has(1):
                        dve.wait_ge(rows_kept, st.seq(1, RG // 2, RG // 2))
                        for k in range(2):
                            nc.vector.tensor_tensor(bent[:, k, :, :], rows[:, sl, :, W1 + k * GRID:W1 + (k + 1) * GRID],
                                                    comp[:, bass.ds(st.seq(1, RG), RG), k:k + 1].broadcast_to(
                                                        [P, RG, GRID]), ALU.mult).then_inc(terms, 1)
                        dve.wait_ge(terms, st.seq(1, 2, 2))
                        nc.vector.tensor_tensor(bent[:, 0, :, :], bent[:, 0, :, :], bent[:, 1, :, :], ALU.add)\
                            .then_inc(bent_sum, 1)
                        dve.wait_ge(bent_sum, st.seq(1, 2, 1))
                        nc.vector.tensor_tensor(bent[:, 0, :, :], bent[:, 0, :, :], rows[:, sl, :, B1:B1 + GRID],
                                                ALU.add).then_inc(bent_sum, 1)
                        dve.wait_ge(bent_sum, st.seq(1, 2, 2))
                        nc.vector.scalar_tensor_tensor(out=bent[:, 1, :, :], in0=bent[:, 0, :, :], scalar=0.0,
                                                       in1=rows[:, sl, :, W2:W2 + GRID], op0=ALU.max, op1=ALU.mult)\
                            .then_inc(hidden, 1)
                        dve.wait_ge(hidden, st.seq(1, c=1))
                        nc.vector.tensor_reduce(mag[:, :], bent[:, 1, :, :], AX_X, ALU.add).then_inc(mag_kept, 1)
                        dve.wait_ge(mag_kept, st.seq(1, 2, 1))
                        nc.vector.tensor_tensor(mag[:, :], mag[:, :], rows[:, sl, :, B2], ALU.add).then_inc(mag_kept, 1)
                        dve.wait_ge(mag_kept, st.seq(1, 2, 2))
                    if st.has(2) or st.has(5):
                        shifts(st)
                    if st.has(1):
                        wait(dve, norm_kept, st.seq(1 + SPLINE_SLOTS, RG, RG))
                        for t in range(RG):
                            nc.vector.scalar_tensor_tensor(
                                out=y[:, sl, t, :], in0=rows[:, sl, t, DIR:TABLE], scalar=mag[:, t:t + 1],
                                in1=x_all[:, bass.ds(st.seq(1, RG, t), 1), :].rearrange("p t c -> p (t c)"),
                                op0=ALU.mult, op1=ALU.add).then_inc(y_kept, 1)
                        dve.wait_ge(y_kept, st.seq(1, RG, RG))
                        statistics(st, 1, 0, y)
                    if st.has(4):
                        dve.wait_ge(z_kept, st.seq(4, c=1))
                        statistics(st, 4, 1, z)
                    if st.has(1):
                        moments(st, 1, 0)
                    if st.has(4):
                        moments(st, 4, 1)
                    if st.has(1) or st.has(4):
                        variances(st)

                steps(dve, step)



def prepare(nc, mem, w):
    with ExitStack() as ctx:
        def sb(label, shape, dt=F32):
            return ctx.enter_context(nc.sbuf_tensor(f"prep_{label}", shape, dt))

        def sem(label):
            return nc.alloc_semaphore(name=f"prep_{label}")

        w_raw = [sb(f"w_raw{n}", [P, 3, C]) for n in range(2)]
        a_T = sb("a_T", [R, 2, D])
        b_r = sb("b_r", [R, 2, D])
        a_rep = sb("a_rep", [R, 2, H, D])
        b_rep = sb("b_rep", [R, 2, H, D])
        b_col = sb("b_col", [P, 3])
        by_feature = sb("by_feature", [P, P])
        bv_wide = sb("bv_wide", [P, P])
        diagonal = sb("diagonal", [P, P])
        lora = sb("lora", [P, 2, P])
        lora_diag = sb("lora_diag", [P, 2, P])
        g_q = sb("g_q", [P, P])
        g_v = sb("g_v", [P, P])
        wT = sb("wT", [P, 2, P])
        ps = ctx.enter_context(nc.psum_tensor("prep_ps", [P, 4, 512], F32))

        loaded, consts, zeroed, masked = sem("loaded"), sem("consts"), sem("zeroed"), sem("masked")
        repeated, lora_ready, lora_kept, diag_kept, folded = (
            sem(x) for x in ("repeated", "lora_ready", "lora_kept", "diag_kept", "folded"))
        wT_ready, wT_kept, new_ready, new_kept = (sem(x) for x in ("wT_ready", "wT_kept", "new_ready", "new_kept"))
        ALL = 1 + 4 + 3 + 6
        block = ctx.enter_context(nc.Block())

        @block.sync
        def _(sp):
            sp.dma_start(w_raw[0][:, :, :], w["L0_attn_w_qkv"].rearrange("c (s f) -> c s f", s=3)).then_inc(loaded, 16)
            for s, k in enumerate(("q", "v")):
                sp.dma_start(a_T[:, s, :], w[f"L0_attn_a_{k}"].rearrange("d r -> r d"),
                             allow_slow_non_contiguous=True).then_inc(loaded, 16)
                sp.dma_start(b_r[:, s, :], w[f"L0_attn_b_{k}"]).then_inc(loaded, 16)
            bias = w["L0_attn_b_qkv"].rearrange("(s f one) -> s f one", s=3, one=1)
            sp.dma_start(b_col[:, 0:1], bias[0]).then_inc(loaded, 16)
            sp.dma_start(b_col[:, 1:2], bias[2]).then_inc(loaded, 16)
            sp.dma_start(b_col[:, 2:3], bias[1]).then_inc(loaded, 16)
            sp.dma_start(mem["wo0"][:, :], w["L0_attn_w_proj"]).then_inc(loaded, 16)
            bo = w["L0_attn_b_proj"]
            sp.dma_start(mem["bo0"][:, :], bass.AP(bo.tensor, bo.offset, [[0, P], [1, C]])).then_inc(loaded, 16)
            sp.dma_start(w_raw[1][:, :, :], w["L1_attn_w_qkv"].rearrange("c (s f) -> c s f", s=3)).then_inc(loaded, 16)
            for k in ("cos", "sin"):
                sp.dma_start(mem[k][:, :], w[k]).then_inc(loaded, 16)
            sp.dma_start(mem["wo1"][:, :], w["L1_attn_w_proj"]).then_inc(loaded, 16)
            sp.wait_ge(loaded, 16 * ALL)



        @block.gpsimd
        def _(pool):
            for t in (mem["ident"], mem["ident_h"], mem["mask_qk"], mem["mask_kq"]):
                nc.gpsimd.memset(t[:], 0.0).then_inc(zeroed, 1)
            nc.gpsimd.memset(diagonal[:, :], 1.0).then_inc(zeroed, 1)
            nc.gpsimd.memset(mem["sigs"][:, :], 0.0).then_inc(zeroed, 1)
            nc.gpsimd.memset(mem["cw2"][:, :], 0.0).then_inc(zeroed, 1)
            nc.gpsimd.memset(mem["minus_half"][:, :], -0.5).then_inc(consts, 1)
            pool.wait_ge(zeroed, 7)
            for t in (mem["ident"], mem["ident_h"]):
                nc.gpsimd.affine_select(out=t[:, :], in_=t[:, :], compare_op=ALU.not_equal, fill=1.0, base=0,
                                        pattern=[[-1, P]], channel_multiplier=1).then_inc(consts, 1)
            nc.gpsimd.affine_select(out=mem["mask_qk"][:], in_=mem["mask_qk"][:], compare_op=ALU.is_ge, fill=MASKED,
                                    base=0, pattern=[[0, 2], [-1, P]], channel_multiplier=1).then_inc(consts, 1)
            nc.gpsimd.affine_select(out=mem["mask_kq"][:], in_=mem["mask_kq"][:], compare_op=ALU.is_ge, fill=MASKED,
                                    base=0, pattern=[[0, 2], [1, P]], channel_multiplier=-1).then_inc(consts, 1)
            nc.gpsimd.affine_select(out=diagonal[:, :], in_=diagonal[:, :], compare_op=ALU.is_ge, fill=0.0,
                                    base=0, pattern=[[-D, H], [0, D]], channel_multiplier=1).then_inc(masked, 1)
            pool.wait_ge(masked, 1)
            nc.gpsimd.affine_select(out=diagonal[:, :], in_=diagonal[:, :], compare_op=ALU.is_ge, fill=0.0,
                                    base=D - 1, pattern=[[D, H], [0, D]], channel_multiplier=-1).then_inc(consts, 1)

        @block.vector
        def _(dve):
            dve.wait_ge(loaded, 16 * ALL)
            for s in range(2):
                nc.vector.tensor_copy(a_rep[:, s, :, :], a_T[:, s, :].unsqueeze(1).broadcast_to([R, H, D]))\
                    .then_inc(repeated, 1)
                nc.vector.tensor_copy(b_rep[:, s, :, :], b_r[:, s, :].unsqueeze(1).broadcast_to([R, H, D]))\
                    .then_inc(repeated, 1)
            nc.vector.tensor_copy(bv_wide[:, :], b_col[:, 1:2].broadcast_to([P, P])).then_inc(repeated, 1)
            heads_last = "p (h d) -> p d h"
            for to, of in ((mem["wqk0"][:, 1, :], w_raw[0][:, 1, :]), (mem["wqk1"][:, 0, :], w_raw[1][:, 0, :]),
                           (mem["wqk1"][:, 1, :], w_raw[1][:, 1, :])):
                nc.vector.tensor_copy(to.rearrange("p (d h) -> p d h", d=D), of.rearrange(heads_last, d=D))\
                    .then_inc(repeated, 1)
            nc.vector.tensor_copy(mem["wv1"][:, :], w_raw[1][:, 2, :]).then_inc(repeated, 1)
            dve.wait_ge(consts, 6)
            dve.wait_ge(lora_ready, 1)
            for s in range(2):
                nc.vector.scalar_tensor_tensor(out=lora[:, s, :], in0=ps[:, s, 0:P], scalar=LORA_SCALE,
                                               in1=diagonal[:, :], op0=ALU.mult, op1=ALU.mult).then_inc(lora_kept, 1)
            dve.wait_ge(lora_kept, 2)
            nc.vector.tensor_tensor(g_q[:, :].rearrange("p (d h) -> p d h", d=D),
                                    lora[:, 0, :].rearrange(heads_last, d=D),
                                    mem["ident"][:, :].rearrange(heads_last, d=D), ALU.add).then_inc(folded, 1)
            nc.vector.tensor_tensor(g_v[:, :], lora[:, 1, :], mem["ident"][:, :], ALU.add).then_inc(folded, 1)
            nc.vector.tensor_copy(by_feature[:, :].rearrange("p (d h) -> p d h", d=D),
                                  mem["ident"][:, :].rearrange(heads_last, d=D)).then_inc(folded, 1)
            dve.wait_ge(wT_ready, 1)
            for s in range(2):
                nc.vector.tensor_copy(wT[:, s, :], ps[:, 2, s * P:(s + 1) * P]).then_inc(wT_kept, 1)
            dve.wait_ge(new_ready, 1)
            for to, of in ((mem["wqk0"][:, 0, :], ps[:, 3, 0:P]), (mem["wv0"][:, :], ps[:, 3, P:2 * P]),
                           (mem["bv0"][:, :], ps[:, 3, 2 * P:3 * P]), (mem["bqk0"][:, :], ps[:, 3, 3 * P:3 * P + 2])):
                nc.vector.tensor_copy(to, of).then_inc(new_kept, 1)

        @block.tensor
        def _(pe):
            pe.wait_ge(repeated, 9)
            for s in range(2):
                last = nc.tensor.matmul(ps[:, s, 0:P], a_rep[:, s, :, :].rearrange("r h d -> r (h d)"),
                                        b_rep[:, s, :, :].rearrange("r h d -> r (h d)"), start=True, stop=True)
            last.then_inc(lora_ready, 1)
            pe.wait_ge(consts, 6)
            for s, of in enumerate((0, 2)):
                last = nc.tensor.transpose(ps[:, 2, s * P:(s + 1) * P], w_raw[0][:, of, :], mem["ident"][:, :])
            last.then_inc(wT_ready, 1)
            pe.wait_ge(folded, 3)
            pe.wait_ge(wT_kept, 2)
            nc.tensor.matmul(ps[:, 3, 0:P], wT[:, 0, :], g_q[:, :], start=True, stop=True)
            nc.tensor.matmul(ps[:, 3, P:2 * P], wT[:, 1, :], g_v[:, :], start=True, stop=True)
            nc.tensor.matmul(ps[:, 3, 2 * P:3 * P], bv_wide[:, :], g_v[:, :], start=True, stop=True)
            nc.tensor.matmul(ps[:, 3, 3 * P:3 * P + 1], g_q[:, :], b_col[:, 0:1], start=True, stop=True)
            nc.tensor.matmul(ps[:, 3, 3 * P + 1:3 * P + 2], by_feature[:, :], b_col[:, 2:3], start=True, stop=True)\
                .then_inc(new_ready, 1)

        @block.scalar
        def _(act):
            act.wait_ge(loaded, 16 * ALL)
            for g in range(4):
                n = TILES // 4
                act.dma_start(mem["x_all"][:, g * n:(g + 1) * n, :], w["x_tiles"][:, g * n:(g + 1) * n, :])\
                    .then_inc(mem["x_all_loaded"], 16)


def build(nc, w, out):
    with ExitStack() as ctx:
        def sb(label, shape, dt=F32):
            return ctx.enter_context(nc.sbuf_tensor(label, shape, dt))

        mem = {"x_all": sb("x_all", [P, TILES, C]), "x_mid": sb("x_mid", [P, TILES, C]),
               "ident": sb("ident", [P, P]), "ident_h": sb("ident_h", [P, P], BF16),
               "mask_qk": sb("mask_qk", [P, 2, P], BF16), "mask_kq": sb("mask_kq", [P, 2, P], BF16),
               "cos": sb("cos", [P, N]), "sin": sb("sin", [P, N]),
               "minus_half": sb("minus_half", [P, TILES])}
        for n in range(2):
            mem |= {f"wqk{n}": sb(f"wqk{n}", [P, 2, P]), f"wv{n}": sb(f"wv{n}", [P, C]), f"wo{n}": sb(f"wo{n}", [P, C])}
        mem |= {"bqk0": sb("bqk0", [P, 2]), "bv0": sb("bv0", [P, C]), "bo0": sb("bo0", [P, C])}
        mem |= {"raw": sb("raw", [NT, C]), "knots": sb("knots", [P, KNOTS]), "temp": sb("temp", [P, 1]),
                "sigs": sb("sigs", [P, P]),
                "cb1": sb("cb1", [P, 1]),
                "cw2": sb("cw2", [P, 32]),
                "cb2": sb("cb2", [P, 2]),
                "table": sb("table", [P, TABLE]),
                "gamma": sb("gamma", [P, C]), "beta": sb("beta", [P, C]), "out_scale": sb("out_scale", [P, 1])}
        mem["ffn_loaded"] = ctx.enter_context(nc.semaphore("ffn_loaded"))
        mem["apart"] = ctx.enter_context(nc.semaphore("apart"))
        mem["x_all_loaded"] = ctx.enter_context(nc.semaphore("x_all_loaded"))
        w = dict(w, x_tiles=w["L0_attn_x"].rearrange("b (t p) c -> p (b t) c", p=P))
        prepare(nc, mem, w)

        def layer(n):
            return mem | {"x_all": mem["x_mid"] if n else mem["x_all"]} | {k: mem.get(f"{k}{n}") for k in ("wqk", "wv", "wo", "bqk", "bv", "bo")}

        out_tiles = out.rearrange("b (t p) c -> p (b t) c", p=P)
        snap = nc.snapshot_sems()
        attention(nc, "attn0", layer(0), False, w["x_tiles"], True, False)
        nc.clear_and_free_semaphores(nc.allocated_since(snap))
        nc.all_engine_barrier()
        moe(nc, mem, w)
        attention(nc, "attn1", layer(1), True, None, False, True)
        spline_ffn(nc, mem, w, out_tiles)


def rotary_tables():
    half = D // 2
    theta = (1.0 / 10000.0 ** (np.arange(half, dtype=np.float32) / np.float32(half))).astype(np.float32)
    freqs = np.arange(N, dtype=np.float32)[:, None] * theta[None, :]
    cos, sin = (np.repeat(np.repeat(f(freqs).astype(np.float32), 2, axis=1).T, H, axis=0) for f in (np.cos, np.sin))
    sin[:P // 2] *= -1
    return np.ascontiguousarray(cos), np.ascontiguousarray(sin)



def kernel(**inputs):
    import concourse.bacc as _bacc
    from concourse import mybir as _mybir
    from concourse.bass_utils import run_bass_kernel_spmd as _run

    nc = _bacc.Bacc("TRN2", target_bir_lowering=False, num_devices=1)
    inputs = {k: np.ascontiguousarray(v) for k, v in inputs.items()}
    inputs["cos"], inputs["sin"] = rotary_tables()
    arrays = {f"in_{k}_dram": v for k, v in inputs.items()}
    w = {k: nc.dram_tensor(f"in_{k}_dram", v.shape, _mybir.dt.from_np(v.dtype), kind="ExternalInput").ap()
         for k, v in inputs.items()}
    out = nc.dram_tensor("out_0_dram", (B, N, C), _mybir.dt.float32, kind="ExternalOutput").ap()
    build(nc, w, out)
    r = _run(nc, [arrays], core_ids=[0])
    return r.results[0]["out_0_dram"]
```
